# Optimizing a Trainium2 kernel written in Bass

```python
import numpy as np
import jax
import jax.numpy as jnp

def _softmax(x, axis=-1):
    return jax.nn.softmax(x, axis=axis)

def _gelu(x):
    return jax.nn.gelu(x, approximate=True)

def _silu(x):
    return jax.nn.silu(x)

def _sigmoid(x):
    return jax.nn.sigmoid(x)

def _layernorm(x, axis=-1, eps=1e-05):
    m = jnp.mean(x, axis=axis, keepdims=True)
    v = jnp.var(x, axis=axis, keepdims=True)
    return (x - m) / jnp.sqrt(v + eps)

def _scatter_add(tgt, idx, src, axis=0):
    return tgt.at[idx].add(src)

def _segment_sum(src, seg, n):
    return jax.ops.segment_sum(src, seg, n)
kernel_name = 'mk_decoder_postln_d1_seqx_r4_30d7da'

def setup_inputs(seed: int=0):
    np.random.seed(seed)
    _w = jnp.asarray

    def _rec_inputs():
        import jax
        import jax.numpy as jnp
        _rk = jax.random.key(seed)
        x = -0.0002928 + 1 * jax.random.normal(jax.random.fold_in(_rk, 1), (2, 1024, 256), jnp.float32)
        _lenS = 1024 - jax.random.randint(jax.random.fold_in(_rk, 7), (2,), 0, max(1, 1024 // 4) + 1, jnp.int32)
        _lenS2 = 77 - jax.random.randint(jax.random.fold_in(_rk, 8), (2,), 0, max(1, 77 // 4) + 1, jnp.int32)
        _ctx_1024P = jax.random.normal(jax.random.fold_in(_rk, 11), (2, 16, 256), jnp.float32)
        _ctx_1024c = jax.random.dirichlet(jax.random.fold_in(_rk, 511), 0.3 * jnp.ones((16,), jnp.float32), (2, 77))
        _ctx_1024t = jnp.einsum('bsk,bkd->bsd', _ctx_1024c, _ctx_1024P)
        _ctx_1024t = _ctx_1024t * jax.lax.rsqrt(jnp.mean(jnp.square(_ctx_1024t)) + 1e-12) * 0.953939
        ctx_1024 = 2.81802e-05 + 1.00001 * (_ctx_1024t + 0.3 * jax.random.normal(jax.random.fold_in(_rk, 611), (2, 77, 256), jnp.float32))
        _validS = jnp.arange(1024)[None, :] < _lenS[:, None]
        _validS2 = jnp.arange(77)[None, :] < _lenS2[:, None]
        _causal = jnp.tril(jnp.ones((1024, 1024), dtype=bool))
        mask_BxS2_bk1 = jnp.broadcast_to(_validS2[:, :], (2, 77))
        return (x, ctx_1024, mask_BxS2_bk1)
    x, ctx_1024, mask_BxS2_bk1 = _rec_inputs()

    def _L0_attn_setup():
        import jax, jax.numpy as jnp
        import numpy as np
        B, L, D_MODEL = (4, 512, 256)
        D_INNER = 2 * D_MODEL
        D_STATE = 64
        D_CONV = 4
        DT_RANK = D_MODEL // 16

        def _mamba_block(x, ln_w, ln_b, W_in, conv_w, conv_b, W_xproj, W_dt, b_dt, A_log, D, W_out):
            residual = x
            mu = jnp.mean(x, axis=-1, keepdims=True)
            var = jnp.mean(jnp.square(x - mu), axis=-1, keepdims=True)
            xn = (x - mu) * jax.lax.rsqrt(var + 1e-05) * ln_w + ln_b
            xz = xn @ W_in
            xi, z = jnp.split(xz, 2, axis=-1)
            xc = jnp.transpose(xi, (0, 2, 1))
            xc = jax.lax.conv_general_dilated(xc, conv_w, window_strides=(1,), padding=[(D_CONV - 1, 0)], feature_group_count=D_INNER, dimension_numbers=('NCH', 'OIH', 'NCH'))
            xc = jnp.transpose(xc, (0, 2, 1)) + conv_b
            u = jax.nn.silu(xc)
            x_dbl = u @ W_xproj
            dt_r = x_dbl[..., :DT_RANK]
            Bm = x_dbl[..., DT_RANK:DT_RANK + D_STATE]
            Cm = x_dbl[..., DT_RANK + D_STATE:]
            delta = jax.nn.softplus(dt_r @ W_dt + b_dt)
            A = -jnp.exp(A_log)

            def step(h, inputs):
                d_t, B_t, C_t, u_t = inputs
                dA = jnp.exp(d_t[:, :, None] * A)
                h = h * dA + (d_t * u_t)[:, :, None] * B_t[:, None, :]
                y_t = jnp.einsum('bdn,bn->bd', h, C_t)
                return (h, y_t)
            h0 = jnp.zeros((x.shape[0], D_INNER, D_STATE), x.dtype)
            seq = (jnp.transpose(delta, (1, 0, 2)), jnp.transpose(Bm, (1, 0, 2)), jnp.transpose(Cm, (1, 0, 2)), jnp.transpose(u, (1, 0, 2)))
            _, ys = jax.lax.scan(step, h0, seq)
            y = jnp.transpose(ys, (1, 0, 2)) + u * D
            y = y * jax.nn.silu(z)
            out = y @ W_out
            return residual + out
        key = jax.random.key(seed)
        ks = jax.random.split(key, 10)
        inp = {}
        inp['x'] = jax.random.normal(ks[0], (B, L, D_MODEL), dtype=jnp.float32)
        inp['ln_w'] = jnp.ones((D_MODEL,), jnp.float32)
        inp['ln_b'] = jnp.zeros((D_MODEL,), jnp.float32)
        inp['W_in'] = jax.random.normal(ks[1], (D_MODEL, 2 * D_INNER), jnp.float32) / np.sqrt(D_MODEL)
        inp['conv_w'] = jax.random.normal(ks[2], (D_INNER, 1, D_CONV), jnp.float32) / np.sqrt(D_CONV)
        inp['conv_b'] = jax.random.normal(ks[3], (D_INNER,), jnp.float32) * 0.01
        inp['W_xproj'] = jax.random.normal(ks[4], (D_INNER, DT_RANK + 2 * D_STATE), jnp.float32) / np.sqrt(D_INNER)
        inp['W_dt'] = jax.random.normal(ks[5], (DT_RANK, D_INNER), jnp.float32) / np.sqrt(DT_RANK)
        inp['b_dt'] = jax.random.normal(ks[6], (D_INNER,), jnp.float32) * 0.1 - 4.0
        inp['A_log'] = jnp.log(jnp.broadcast_to(jnp.arange(1, D_STATE + 1, dtype=jnp.float32), (D_INNER, D_STATE)))
        inp['D'] = jnp.ones((D_INNER,), jnp.float32)
        inp['W_out'] = jax.random.normal(ks[7], (D_INNER, D_MODEL), jnp.float32) / np.sqrt(D_INNER)
        return inp
    _L0_attn_all = _L0_attn_setup()
    _L0_attn_in = {k: v for k, v in _L0_attn_all.items() if k in ('ln_w', 'ln_b', 'W_in', 'conv_w', 'conv_b', 'W_xproj', 'W_dt', 'b_dt', 'A_log', 'D', 'W_out')}
    del _L0_attn_all

    def _L0_xattn_setup():
        import jax, jax.numpy as jnp
        import numpy as np
        B, N, M = (4, 256, 1024)
        DQ, DC = (256, 256)
        H, DH = (16, 64)
        INNER = H * DH
        SCALE = DH ** (-0.5)
        key = jax.random.key(seed)
        ks = jax.random.split(key, 6)
        x = jax.random.normal(ks[0], (B, N, DQ), dtype=jnp.float32)
        context = jax.random.normal(ks[1], (B, M, DC), dtype=jnp.float32)
        mask = jax.random.bernoulli(ks[2], 0.9, (B, M))
        Wq = jax.random.normal(ks[3], (DQ, INNER), dtype=jnp.float32) / np.sqrt(DQ)
        Wkv = jax.random.normal(ks[4], (DC, 2 * INNER), dtype=jnp.float32) / np.sqrt(DC)
        Wo = jax.random.normal(ks[5], (INNER, DQ), dtype=jnp.float32) / np.sqrt(INNER)
        bo = jnp.zeros((DQ,), dtype=jnp.float32)
        return {'x': x, 'context': context, 'mask': mask, 'Wq': Wq, 'Wkv': Wkv, 'Wo': Wo, 'bo': bo}
    _L0_xattn_all = _L0_xattn_setup()
    _L0_xattn_in = {k: v for k, v in _L0_xattn_all.items() if k in ('Wq', 'Wkv', 'Wo', 'bo')}
    del _L0_xattn_all

    def _L0_ffn_setup():
        import jax, jax.numpy as jnp
        import numpy as np
        B, S, D = (2, 256, 256)
        E, K, F, FS = (8, 2, 128, 256)
        key = jax.random.key(seed)
        ks = jax.random.split(key, 9)
        s = lambda k, shape, fan: jax.random.normal(k, shape, jnp.float32) * fan ** (-0.5)
        return {'x': jax.random.normal(ks[0], (B, S, D), jnp.float32), 'Wr': s(ks[1], (D, E), D), 'Wg': s(ks[2], (E, D, F), D), 'Wu': s(ks[3], (E, D, F), D), 'Wd': s(ks[4], (E, F, D), F), 'Sg': s(ks[5], (D, FS), D), 'Su': s(ks[6], (D, FS), D), 'Sd': s(ks[7], (FS, D), FS), 'expert_bias': jnp.zeros((E,), jnp.float32)}
    _L0_ffn_all = _L0_ffn_setup()
    _L0_ffn_in = {k: v for k, v in _L0_ffn_all.items() if k in ('Wr', 'Wg', 'Wu', 'Wd', 'Sg', 'Su', 'Sd', 'expert_bias')}
    del _L0_ffn_all
    return {'x': x, 'ctx_1024': ctx_1024, 'mask_BxS2_bk1': mask_BxS2_bk1, 'L0_attn_ln_w': _L0_attn_in['ln_w'], 'L0_attn_ln_b': _L0_attn_in['ln_b'], 'L0_attn_W_in': _L0_attn_in['W_in'], 'L0_attn_conv_w': _L0_attn_in['conv_w'], 'L0_attn_conv_b': _L0_attn_in['conv_b'], 'L0_attn_W_xproj': _L0_attn_in['W_xproj'], 'L0_attn_W_dt': _L0_attn_in['W_dt'], 'L0_attn_b_dt': _L0_attn_in['b_dt'], 'L0_attn_A_log': _L0_attn_in['A_log'], 'L0_attn_D': _L0_attn_in['D'], 'L0_attn_W_out': _L0_attn_in['W_out'], 'L0_xattn_Wq': _L0_xattn_in['Wq'], 'L0_xattn_Wkv': _L0_xattn_in['Wkv'], 'L0_xattn_Wo': _L0_xattn_in['Wo'], 'L0_xattn_bo': _L0_xattn_in['bo'], 'L0_ffn_Wr': _L0_ffn_in['Wr'], 'L0_ffn_Wg': _L0_ffn_in['Wg'], 'L0_ffn_Wu': _L0_ffn_in['Wu'], 'L0_ffn_Wd': _L0_ffn_in['Wd'], 'L0_ffn_Sg': _L0_ffn_in['Sg'], 'L0_ffn_Su': _L0_ffn_in['Su'], 'L0_ffn_Sd': _L0_ffn_in['Sd'], 'L0_ffn_expert_bias': _L0_ffn_in['expert_bias']}

def reference(x, ctx_1024, mask_BxS2_bk1, L0_attn_ln_w, L0_attn_ln_b, L0_attn_W_in, L0_attn_conv_w, L0_attn_conv_b, L0_attn_W_xproj, L0_attn_W_dt, L0_attn_b_dt, L0_attn_A_log, L0_attn_D, L0_attn_W_out, L0_xattn_Wq, L0_xattn_Wkv, L0_xattn_Wo, L0_xattn_bo, L0_ffn_Wr, L0_ffn_Wg, L0_ffn_Wu, L0_ffn_Wd, L0_ffn_Sg, L0_ffn_Su, L0_ffn_Sd, L0_ffn_expert_bias):
    import jax
    import jax.numpy as jnp

    def _L0_attn_ref(x, ln_w, ln_b, W_in, conv_w, conv_b, W_xproj, W_dt, b_dt, A_log, D, W_out):
        import jax, jax.numpy as jnp
        import numpy as np
        B, L, D_MODEL = (4, 512, 256)
        D_INNER = 2 * D_MODEL
        D_STATE = 64
        D_CONV = 4
        DT_RANK = D_MODEL // 16

        def _mamba_block(x, ln_w, ln_b, W_in, conv_w, conv_b, W_xproj, W_dt, b_dt, A_log, D, W_out):
            residual = x
            mu = jnp.mean(x, axis=-1, keepdims=True)
            var = jnp.mean(jnp.square(x - mu), axis=-1, keepdims=True)
            xn = (x - mu) * jax.lax.rsqrt(var + 1e-05) * ln_w + ln_b
            xz = xn @ W_in
            xi, z = jnp.split(xz, 2, axis=-1)
            xc = jnp.transpose(xi, (0, 2, 1))
            xc = jax.lax.conv_general_dilated(xc, conv_w, window_strides=(1,), padding=[(D_CONV - 1, 0)], feature_group_count=D_INNER, dimension_numbers=('NCH', 'OIH', 'NCH'))
            xc = jnp.transpose(xc, (0, 2, 1)) + conv_b
            u = jax.nn.silu(xc)
            x_dbl = u @ W_xproj
            dt_r = x_dbl[..., :DT_RANK]
            Bm = x_dbl[..., DT_RANK:DT_RANK + D_STATE]
            Cm = x_dbl[..., DT_RANK + D_STATE:]
            delta = jax.nn.softplus(dt_r @ W_dt + b_dt)
            A = -jnp.exp(A_log)

            def step(h, inputs):
                d_t, B_t, C_t, u_t = inputs
                dA = jnp.exp(d_t[:, :, None] * A)
                h = h * dA + (d_t * u_t)[:, :, None] * B_t[:, None, :]
                y_t = jnp.einsum('bdn,bn->bd', h, C_t)
                return (h, y_t)
            h0 = jnp.zeros((x.shape[0], D_INNER, D_STATE), x.dtype)
            seq = (jnp.transpose(delta, (1, 0, 2)), jnp.transpose(Bm, (1, 0, 2)), jnp.transpose(Cm, (1, 0, 2)), jnp.transpose(u, (1, 0, 2)))
            _, ys = jax.lax.scan(step, h0, seq)
            y = jnp.transpose(ys, (1, 0, 2)) + u * D
            y = y * jax.nn.silu(z)
            out = y @ W_out
            return residual + out
        return _mamba_block(x, ln_w, ln_b, W_in, conv_w, conv_b, W_xproj, W_dt, b_dt, A_log, D, W_out)

    def _L0_xattn_ref(x, context, mask, Wq, Wkv, Wo, bo):
        import jax, jax.numpy as jnp
        import numpy as np
        B, N, M = (4, 256, 1024)
        DQ, DC = (256, 256)
        H, DH = (16, 64)
        INNER = H * DH
        SCALE = DH ** (-0.5)
        q = x @ Wq
        kv = context @ Wkv
        k, v = jnp.split(kv, 2, axis=-1)

        def heads(t):
            b, s, _ = t.shape
            return t.reshape(b, s, H, DH).transpose(0, 2, 1, 3)
        q, k, v = (heads(q), heads(k), heads(v))
        sim = jnp.einsum('bhid,bhjd->bhij', q, k) * SCALE
        max_neg = -jnp.finfo(sim.dtype).max
        sim = jnp.where(mask[:, None, None, :], sim, max_neg)
        sim = jnp.clip(sim, -5.0, 5.0)
        attn = jax.nn.softmax(sim, axis=-1)
        out = jnp.einsum('bhij,bhjd->bhid', attn, v)
        out = out.transpose(0, 2, 1, 3).reshape(x.shape[0], x.shape[1], INNER)
        return out @ Wo + bo

    def _L0_ffn_ref(x, Wr, Wg, Wu, Wd, Sg, Su, Sd, expert_bias):
        import jax, jax.numpy as jnp
        import numpy as np
        B, S, D = (2, 256, 256)
        E, K, F, FS = (8, 2, 128, 256)
        b, s, d = x.shape
        xf = x.reshape(-1, d)
        T = xf.shape[0]
        logits = xf @ Wr + expert_bias
        top_v, top_i = jax.lax.top_k(logits, K)
        probs = jax.nn.softmax(top_v, axis=-1)
        rw = jnp.zeros_like(logits).at[jnp.arange(T)[:, None], top_i].set(probs)
        gate = jnp.einsum('td,edf->tef', xf, Wg)
        up = jnp.einsum('td,edf->tef', xf, Wu)
        h = jax.nn.silu(gate) * up
        eo = jnp.einsum('tef,efd->ted', h, Wd)
        out = jnp.einsum('te,ted->td', rw, eo)
        out = out + jax.nn.silu(xf @ Sg) * (xf @ Su) @ Sd
        return out.reshape(b, s, d)
    x = _layernorm(x + _L0_attn_ref(x, L0_attn_ln_w, L0_attn_ln_b, L0_attn_W_in, L0_attn_conv_w, L0_attn_conv_b, L0_attn_W_xproj, L0_attn_W_dt, L0_attn_b_dt, L0_attn_A_log, L0_attn_D, L0_attn_W_out), axis=-1)
    x = _layernorm(x + _L0_xattn_ref(x, ctx_1024, mask_BxS2_bk1, L0_xattn_Wq, L0_xattn_Wkv, L0_xattn_Wo, L0_xattn_bo), axis=-1)
    x = _layernorm(x + _L0_ffn_ref(x, L0_ffn_Wr, L0_ffn_Wg, L0_ffn_Wu, L0_ffn_Wd, L0_ffn_Sg, L0_ffn_Su, L0_ffn_Sd, L0_ffn_expert_bias), axis=-1)
    return x

_drawn_inputs = setup_inputs


def setup_inputs(seed=0):
    import zlib

    import numpy as np

    out = dict(_drawn_inputs(seed))
    spreads = {'L0_attn_ln_w': (1.0, 0.2),
     'L0_attn_ln_b': (0.0, 0.1),
     'L0_attn_D': (1.0, 0.2),
     'L0_xattn_bo': (0.0, 0.1),
     'L0_ffn_expert_bias': (0.0, 0.1)}
    factors = {'L0_attn_conv_b': 10.369,
     'L0_attn_b_dt': 32.488,
     'L0_attn_W_xproj': 8.0,
     'L0_attn_W_dt': 8.0,
     'L0_attn_A_log': 8.0}
    for name, (base, spread) in spreads.items():
        noise = np.random.default_rng([zlib.crc32(name.encode()), seed]).standard_normal(out[name].shape)
        drawn = base * np.exp(spread * noise) if base else spread * noise
        out[name] = jnp.asarray(drawn.astype(out[name].dtype))
    for name, factor in factors.items():
        out[name] = (out[name] * factor).astype(out[name].dtype)
    return out
```

```python
import concourse.bass as bass
from concourse import mybir
from contextlib import ExitStack

F32 = mybir.dt.float32
BF16 = mybir.dt.bfloat16
U8 = mybir.dt.uint8
ALU = mybir.AluOpType
ACT = mybir.ActivationFunctionType
AXX = mybir.AxisListType.X

P = 128
NB, L, D = 2, 1024, 256
T = NB * L
KD = D // P
DI, NS, R = 512, 64, 16
MB = DI // P
TAPS = 4
S2, H, DH = 77, 16, 64
HJ = H * S2
E, F = 8, 128
FB = E + 2
TB = T // P
BB = L // P
HALF = 512
PAIRS = DI // 2
GP = 16
GROUPS = PAIRS // GP
PARTS = 3
ROWS = GP * 2 * PARTS
EPS = 1e-5
LOG1P = (0.99999976, -0.49997175, 0.3327193, -0.24474774, 0.17687477, -0.10685003, 0.0434939, -0.008371153)
HEAD_GROUPS = ((0, 6), (6, 11), (11, 16))
HJ_CHUNKS = -(-HJ // P)
HJ_LAST = HJ - (HJ_CHUNKS - 1) * P


def stage_context(nc, io, mem):
    KV = 2 * H // 2
    BANKS = 8
    with ExitStack() as ctx:
        sb = lambda n, s, d=F32: ctx.enter_context(nc.sbuf_tensor(n, s, d))
        sem = lambda n: ctx.enter_context(nc.semaphore(n))
        cx = sb("cx", [S2, NB, D])
        wq = sb("wq", [P, KD, H * DH])
        wkv = sb("wkv", [P, KD, 2 * H * DH])
        wo = sb("wo", [P, H // 2, D])
        cxT = sb("cxT", [P, KD, NB * S2])
        wqT = sb("wqT", [P, H // 2, D])
        kvT = sb("kvT", [P, 2 * H, NB * S2])
        vo = sb("vo", [S2, NB, H, D])
        mask = sb("mask", [P, NB * S2], U8)
        alog = sb("alog", [P, 2, P])
        bank = [ctx.enter_context(nc.psum_tensor(f"cbank{i}", [P, HALF], F32)) for i in range(BANKS)]
        ld_consts, ld_ctx, ld_wkv, ld_wq, ld_wo = (sem(n) for n in ("ld_consts", "ld_ctx", "ld_wkv", "ld_wq", "ld_wo"))
        ld_mask, ld_alog = sem("ld_mask"), sem("ld_alog")
        kv_zeroed = sem("kv_zeroed")
        filled = sem("filled")
        act_emptied = sem("act_emptied")
        dve_emptied = sem("dve_emptied")
        limits_done, stored = sem("limits_done"), sem("stored")
        J_A, J_CTX, J_KV = 0, 1, 2
        J_WQ = J_KV + KV // 2
        J_G = J_WQ + H // 4
        J_VO = J_G + NB * KD * len(HEAD_GROUPS)
        J_END = J_VO + NB * H // 2

        def emptied(eng, job):
            if job % 2:
                eng.wait_ge(dve_emptied, job // 2 + 1)
            else:
                eng.wait_ge(act_emptied, job // 2 + 1)

        block = ctx.enter_context(nc.Block())

        @block.sync
        def _(sp):
            sp.dma_start(mem["ident"][:], io["c_ident"]).then_inc(ld_consts, 16)
            sp.dma_start(alog[:], io["L0_attn_A_log"].rearrange("(c p e) n -> p c (e n)", p=P, e=2)).then_inc(ld_alog, 16)
            sp.dma_start(cx[:], io["ctx_1024"].rearrange("b j d -> j b d")).then_inc(ld_ctx, 16)
            sp.dma_start(wkv[:], io["L0_xattn_Wkv"].rearrange("(k p) n -> p k n", p=P)).then_inc(ld_wkv, 16)
            sp.dma_start(wq[:], io["L0_xattn_Wq"].rearrange("(k p) n -> p k n", p=P)).then_inc(ld_wq, 16)
            sp.dma_start(mask[:], io["mask_BxS2_bk1"].rearrange("b j -> (b j)").unsqueeze(0).broadcast_to([P, NB * S2])).then_inc(ld_mask, 16)
            sp.dma_start(wo[:], io["L0_xattn_Wo"].rearrange("(k p) n -> p k n", p=P)).then_inc(ld_wo, 16)
            for b in range(NB):
                emptied(sp, J_VO + (b + 1) * H // 2 - 1)
                emptied(sp, J_VO + (b + 1) * H // 2 - 2)
                sp.dma_start(mem["vo_dram"][b, :, :].rearrange("(h j) e -> j h e", j=S2), vo[:, b, :, :]).then_inc(stored, 16)
            sp.wait_ge(stored, 16 * NB)

        @block.gpsimd
        def _(pool):
            nc.gpsimd.memset(kvT[:], 0.0).then_inc(kv_zeroed, 1)

        @block.tensor
        def _(pe):
            pe.wait_ge(ld_consts, 16)
            pe.wait_ge(ld_alog, 16)
            for c in range(2):
                last = nc.tensor.transpose(bank[J_A][:, c * P:(c + 1) * P], alog[:, c, :], mem["ident"][:])
            last.then_inc(filled, 1)
            pe.wait_ge(ld_ctx, 16)
            for k in range(KD):
                for b in range(NB):
                    at = (k * NB + b) * S2
                    last = nc.tensor.transpose(bank[J_CTX][:, at:at + S2], cx[:, b, k * P:(k + 1) * P], mem["ident"][0:S2, 0:S2])
            last.then_inc(filled, 1)
            pe.wait_ge(ld_wkv, 16)
            emptied(pe, J_CTX)
            for job in range(J_KV, J_WQ):
                if job >= BANKS:
                    emptied(pe, job - BANKS)
                for s in range(2):
                    rb = 2 * (job - J_KV) + s
                    for k in range(KD):
                        last = nc.tensor.matmul(bank[job % BANKS][:, s * 256:s * 256 + NB * S2], wkv[:, k, rb * P:(rb + 1) * P],
                                                cxT[:, k, :], start=(k == 0), stop=(k == KD - 1))
                last.then_inc(filled, 1)
            pe.wait_ge(ld_wq, 16)
            for job in range(J_WQ, J_G):
                emptied(pe, job - BANKS)
                for s in range(2):
                    rb = 2 * (job - J_WQ) + s
                    for k in range(KD):
                        last = nc.tensor.transpose(bank[job % BANKS][:, s * D + k * P:s * D + (k + 1) * P],
                                                   wq[:, k, rb * P:(rb + 1) * P], mem["ident"][:])
                last.then_inc(filled, 1)
            job = J_G
            emptied(pe, J_G - 1)
            emptied(pe, J_G - 2)
            for b in range(NB):
                for k in range(KD):
                    for h0, h1 in HEAD_GROUPS:
                        emptied(pe, job - BANKS)
                        for h in range(h0, h1):
                            last = nc.tensor.matmul(bank[job % BANKS][:, (h - h0) * S2:(h - h0 + 1) * S2], wqT[:, h // 2, k * P:(k + 1) * P],
                                                    kvT[:, h, b * S2:(b + 1) * S2], start=True, stop=True)
                        last.then_inc(filled, 1)
                        job += 1
            pe.wait_ge(ld_wo, 16)
            for b in range(NB):
                for hp in range(H // 2):
                    emptied(pe, job - BANKS)
                    for s in range(2):
                        last = nc.tensor.matmul(bank[job % BANKS][0:S2, s * D:(s + 1) * D], kvT[:, H + 2 * hp + s, b * S2:(b + 1) * S2],
                                                wo[:, hp, :], start=True, stop=True)
                    last.then_inc(filled, 1)
                    job += 1

        def copies(job):
            src = bank[job % BANKS]
            if job < J_KV:
                return [(cxT[:].rearrange("p k n -> p (k n)"), src[:, 0:KD * NB * S2], 1.0)]
            if job < J_WQ:
                both = src[:].rearrange("p (s n) -> p s n", s=2)[:, :, 0:NB * S2]
                rb = 2 * (job - J_KV)
                to = kvT[:].rearrange("p (r e) n -> p r e n", e=2)
                return [(to[e * DH:(e + 1) * DH, rb:rb + 2, e, :], both[e * DH:(e + 1) * DH], 1.0) for e in range(2)]
            if job < J_G:
                rb = 2 * (job - J_WQ)
                return [(wqT[:, rb:rb + 2, :].rearrange("p r n -> p (r n)"), src[:], 1.0)]
            if job < J_VO:
                q, g = divmod(job - J_G, len(HEAD_GROUPS))
                h0, h1 = HEAD_GROUPS[g]
                b, k = divmod(q, KD)
                return [(mem["G"][:, b, k, h0 * S2:h1 * S2], src[:, 0:(h1 - h0) * S2], DH ** -0.5)]
            b, hp = divmod(job - J_VO, H // 2)
            return [(vo[:, b, 2 * hp:2 * hp + 2, :].rearrange("p s n -> p (s n)"), src[0:S2, :], 1.0)]

        @block.scalar
        def _(act):
            act.wait_ge(kv_zeroed, 1)
            for job in range(0, J_END, 2):
                act.wait_ge(filled, job + 1)
                if job == J_A:
                    for b in range(NB):
                        last = nc.scalar.activation(mem["AT"][:, b * PAIRS:(b + 1) * PAIRS], bank[J_A][:, 0:PAIRS], ACT.Exp)
                else:
                    for out, src, factor in copies(job):
                        last = nc.scalar.activation(out, src, ACT.Copy, scale=factor)
                last.then_inc(act_emptied, 1)

        @block.vector
        def _(dve):
            dve.wait_ge(kv_zeroed, 1)
            for job in range(1, J_END, 2):
                dve.wait_ge(filled, job + 1)
                for out, src, factor in copies(job):
                    last = nc.vector.tensor_scalar(out, src, factor, None, ALU.mult)
                last.then_inc(dve_emptied, 1)
                if job == 1:
                    dve.wait_ge(ld_mask, 16)
                    nc.vector.tensor_scalar(mem["upper"][:], mask[:], 10.0, -5.0, ALU.mult, ALU.add).then_inc(limits_done, 1)
            dve.wait_ge(act_emptied, J_A // 2 + 1)
            nc.vector.tensor_scalar(mem["AT"][:], mem["AT"][:], -1.0, None, ALU.mult).then_inc(limits_done, 1)


def stage_mixer_in(nc, io, mem):
    OUTS = MB * 2 + 3 + MB
    Z0, LOW, BJ, CJ, DT0 = MB, 2 * MB, 2 * MB + 1, 2 * MB + 2, 2 * MB + 3
    ACT_OUTS = OUTS - 2
    SLOTS = 3
    HALO = TAPS - 1
    with ExitStack() as ctx:
        sb = lambda n, s, d=F32: ctx.enter_context(nc.sbuf_tensor(n, s, d))
        sem = lambda n: ctx.enter_context(nc.semaphore(n))
        w_in = sb("w_in", [P, KD, 2 * DI])
        w_low = sb("w_low", [P, MB, R])
        w_B = sb("w_B", [P, MB, 2, NS])
        w_C = sb("w_C", [P, MB, 2, NS])
        w_dt = sb("w_dt", [R, DI])
        vectors = sb("vectors", [P, 2 * KD + MB * TAPS + 3 * MB])
        lnw, lnb = vectors[:, 0:KD], vectors[:, KD:2 * KD]
        at = 2 * KD + MB * TAPS
        cw = vectors[:, 2 * KD:at].rearrange("p (m t) -> p m t", t=TAPS)
        cb, bdt, skip = (vectors[:, at + i * MB:at + (i + 1) * MB] for i in range(3))
        st, mv, sd, rs = sb("st", [P, BB, 6]), sb("mv", [P, BB, 2]), sb("sd", [P, BB]), sb("rs", [P, BB])
        xn = sb("xn", [P, BB, D])
        xnT = sb("xnT", [P, KD, L])
        xi = sb("xi", [P, MB, HALO + L])
        u = sb("u", [P, MB, L])
        sz = [sb(f"sz{i}", [P, L]) for i in range(2)]
        uD = [sb(f"uD{i}", [P, L]) for i in range(2)]
        low = sb("low", [R, L])
        e_ = [sb(f"e{i}", [P, L]) for i in range(2)]
        pos = [sb(f"pos{i}", [P, L]) for i in range(2)]
        q = sb("q", [P, L])
        delta = [sb(f"delta{i}", [P, L]) for i in range(2)]
        du = [sb(f"du{i}", [P, L]) for i in range(2)]
        rem = [sb(f"rem{i}", [P, L]) for i in range(2)]
        parts = [sb(f"parts{i}", [P, PARTS, L], BF16) for i in range(2)]
        tp = [ctx.enter_context(nc.psum_tensor(f"tp{i}", [P, HALF], F32)) for i in range(2)]
        mm = [ctx.enter_context(nc.psum_tensor(f"mm{i}", [P, L], F32)) for i in range(SLOTS)]

        ld_x = [sem(f"ld_x{b}") for b in range(NB)]
        ld_w, ld_w2 = sem("ld_w"), sem("ld_w2")
        halo_zeroed, passed = sem("halo_zeroed"), sem("passed0")
        stats_done, mean_done, sd_done, rs_done, xn_done = (sem(n) for n in ("stats_done", "mean_done", "sd_done", "rs_done", "xn_done"))
        tp_full, tp_emptied = sem("tp_full"), sem("tp_emptied")
        mm_full, mm_act, mm_dve = sem("mm_full"), sem("mm_act"), sem("mm_dve")
        conv_step, u_done, uD_done = sem("conv_step"), sem("u_done"), sem("uD_done")
        sz_out = [sem(f"sz_out{i}") for i in range(2)]
        uD_out = [sem(f"uD_out{i}") for i in range(2)]
        pos_done, abs_done, e_done = sem("pos_done"), sem("abs_done"), sem("e_done")
        horner, delta_done = sem("horner"), sem("delta_done")
        pool_step, cast_step = sem("pool_step"), sem("cast_step")
        parts_out = [sem(f"parts_out{i}") for i in range(2)]
        N_W, N_W2 = 2, 6
        NH = len(LOG1P)
        P_DU, P_REM, P_LOW, P_ALL = 1, 2, 4, 5
        C_HI, C_MID, C_ALL = 0, 2, 4

        block = ctx.enter_context(nc.Block())

        @block.sync
        def _(sp):
            for b in range(NB):
                sp.dma_start(mem["x"][:, b * BB:(b + 1) * BB, :], io["x"][b].rearrange("(n p) d -> p n d", p=P)).then_inc(ld_x[b], 16)
                if b == 0:
                    sp.dma_start(w_in[:], io["L0_attn_W_in"].rearrange("(k p) n -> p k n", p=P)).then_inc(ld_w, 16)
                    sp.dma_start(vectors[:], io["vectors"]).then_inc(ld_w, 16)
            wx = io["L0_attn_W_xproj"].rearrange("(m p) n -> p m n", p=P)
            sp.dma_start(w_low[:], wx[:, :, 0:R]).then_inc(ld_w2, 16)
            sp.dma_start(w_dt[:], io["L0_attn_W_dt"]).then_inc(ld_w2, 16)
            sp.dma_start(w_B[:, :, 0, :], wx[:, :, R:R + NS]).then_inc(ld_w2, 16)
            sp.dma_start(w_C[:, :, 0, :], wx[:, :, R + NS:R + 2 * NS]).then_inc(ld_w2, 16)
            sp.dma_start(w_B[:, :, 1, :], wx[:, :, R:R + NS]).then_inc(ld_w2, 16)
            sp.dma_start(w_C[:, :, 1, :], wx[:, :, R + NS:R + 2 * NS]).then_inc(ld_w2, 16)
            with nc.sync.Fori(0, NB) as b:
                for m in range(MB):
                    rows = slice(m * P, (m + 1) * P)
                    sp.wait_ge(mm_act, b * ACT_OUTS + Z0 + m + 1)
                    sp.dma_start(mem["sz_dram"][rows, bass.ds(b * L, L)], sz[m % 2][:]).then_inc(sz_out[m % 2], 16)
                    sp.wait_ge(uD_done, b * MB + m + 1)
                    sp.dma_start(mem["uD_dram"][rows, bass.ds(b * L, L)], uD[m % 2][:]).then_inc(uD_out[m % 2], 16)
                for m in range(MB):
                    for i, name in enumerate(("delta_dram", "du_dram")):
                        sp.wait_ge(pool_step, b * (MB * P_ALL) + m * P_ALL + P_LOW + i)
                        sp.dma_start(mem[name][bass.ds(b * (DI * PARTS * L) + m * (P * PARTS * L), P * PARTS * L)].rearrange("(p n) -> p n", p=P),
                                     parts[i][:].rearrange("p a n -> p (a n)")).then_inc(parts_out[i], 16)
            for i in range(2):
                sp.wait_ge(sz_out[i], 16 * NB * MB // 2)
                sp.wait_ge(uD_out[i], 16 * NB * MB // 2)
                sp.wait_ge(parts_out[i], 16 * NB * MB)

        @block.tensor
        def _(pe):
            with nc.tensor.Fori(0, NB) as b:
                for t in range(2 * KD):
                    half, k = divmod(t, KD)
                    pe.wait_ge(xn_done, b * BB + (half + 1) * (BB // 2))
                    if t >= 2:
                        pe.wait_ge(tp_emptied, b * (2 * KD) + t - 1)
                    for n in range(BB // 2):
                        last = nc.tensor.transpose(tp[t % 2][:, n * P:(n + 1) * P], xn[:, half * (BB // 2) + n, k * P:(k + 1) * P], mem["ident"][:])
                    last.then_inc(tp_full, 1)
                pe.wait_ge(ld_w, 16 * N_W)
                pe.wait_ge(tp_emptied, (b + 1) * (2 * KD))
                for j in range(OUTS):
                    o = mm[j % SLOTS]
                    if j >= SLOTS:
                        if j - SLOTS in (BJ, CJ):
                            pe.wait_ge(mm_dve, b * 2 + (j - SLOTS - BJ) + 1)
                        else:
                            pe.wait_ge(mm_act, b * ACT_OUTS + (j - SLOTS + 1 if j - SLOTS < BJ else j - SLOTS - 1))
                    if j == LOW:
                        pe.wait_ge(ld_w2, 16 * N_W2)
                        pe.wait_ge(u_done, (b + 1) * MB)
                    if j == DT0:
                        pe.wait_ge(mm_act, b * ACT_OUTS + LOW + 1)
                    for half in range(2):
                        cols = slice(half * HALF, (half + 1) * HALF)
                        if j < LOW:
                            for k in range(KD):
                                last = nc.tensor.matmul(o[:, cols], w_in[:, k, j * P:(j + 1) * P], xnT[:, k, cols], start=(k == 0), stop=(k == KD - 1))
                        elif j < DT0:
                            w = (w_low, w_B, w_C)[j - LOW]
                            for m in range(MB):
                                lhsT = w[:, m, :] if j == LOW else w[:, m, :, :].rearrange("p c n -> p (c n)")
                                last = nc.tensor.matmul(o[0:(R if j == LOW else P), cols], lhsT, u[:, m, cols], start=(m == 0), stop=(m == MB - 1))
                        else:
                            m = j - DT0
                            last = nc.tensor.matmul(o[:, cols], w_dt[:, m * P:(m + 1) * P], low[:, cols], start=True, stop=True)
                    last.then_inc(mm_full, 1)

        @block.scalar
        def _(act):
            with nc.scalar.Fori(0, NB) as b:
                act.wait_ge(mean_done, (b + 1) * BB)
                nc.scalar.activation(sd[:], mv[:, :, 1], ACT.Sqrt, bias=mem["eps"][:, 0:1]).then_inc(sd_done, 1)
                act.wait_ge(ld_w, 16 * N_W)
                for t in range(2 * KD):
                    half, k = divmod(t, KD)
                    act.wait_ge(tp_full, b * (2 * KD) + t + 1)
                    nc.scalar.activation(xnT[:, k, half * HALF:(half + 1) * HALF], tp[t % 2][:], ACT.Identity,
                                         scale=lnw[:, k:k + 1], bias=lnb[:, k:k + 1]).then_inc(tp_emptied, 1)
                for m in range(MB):
                    act.wait_ge(mm_full, b * OUTS + m + 1)
                    if m == 0:
                        act.wait_ge(halo_zeroed, 1)
                    nc.scalar.activation(xi[:, m, HALO:HALO + L], mm[m % SLOTS][:], ACT.Copy).then_inc(mm_act, 1)
                act.wait_ge(ld_w2, 16 * N_W2)
                for m in range(MB):
                    act.wait_ge(mm_full, b * OUTS + Z0 + m + 1)
                    if m >= 2:
                        act.wait_ge(sz_out[m % 2], b * (16 * MB // 2) + 16 * (m // 2))
                        act.wait_ge(uD_out[m % 2], b * (16 * MB // 2) + 16 * (m // 2))
                    nc.scalar.activation(sz[m % 2][:], mm[(Z0 + m) % SLOTS][:], ACT.Silu).then_inc(mm_act, 1)
                    act.wait_ge(conv_step, b * (MB * TAPS) + (m + 1) * TAPS)
                    nc.scalar.activation(u[:, m, :], u[:, m, :], ACT.Silu).then_inc(u_done, 1)
                    act.wait_ge(u_done, b * MB + m + 1)
                    nc.scalar.activation(uD[m % 2][:], u[:, m, :], ACT.Identity, scale=skip[:, m:m + 1]).then_inc(uD_done, 1)
                act.wait_ge(mm_full, b * OUTS + LOW + 1)
                nc.scalar.activation(low[:], mm[LOW % SLOTS][0:R, :], ACT.Copy).then_inc(mm_act, 1)

                def softplus_inputs(m):
                    act.wait_ge(mm_full, b * OUTS + DT0 + m + 1)
                    if m >= 2:
                        act.wait_ge(delta_done, b * MB + m - 1)
                    nc.scalar.activation(pos[m % 2][:], mm[(DT0 + m) % SLOTS][:], ACT.Relu, bias=bdt[:, m:m + 1]).then_inc(pos_done, 1)
                    nc.scalar.activation(e_[m % 2][:], mm[(DT0 + m) % SLOTS][:], ACT.Abs, bias=bdt[:, m:m + 1]).then_inc(mm_act, 1)
                    act.wait_ge(mm_act, b * ACT_OUTS + DT0 - 2 + m + 1)
                    nc.scalar.activation(e_[m % 2][:], e_[m % 2][:], ACT.Exp, scale=-1.0).then_inc(e_done, 1)

                softplus_inputs(0)
                for m in range(MB):
                    if m + 1 < MB:
                        softplus_inputs(m + 1)
                    act.wait_ge(delta_done, b * MB + m + 1)
                    for i, src in enumerate((delta, du)):
                        if m >= 1:
                            act.wait_ge(parts_out[i], b * (16 * MB) + 16 * m)
                        if i == 1:
                            act.wait_ge(pool_step, b * (MB * P_ALL) + m * P_ALL + P_DU)
                        nc.scalar.activation(parts[i][:, 0, :], src[m % 2][:], ACT.Copy).then_inc(cast_step, 1)
                    for i in range(2):
                        act.wait_ge(pool_step, b * (MB * P_ALL) + m * P_ALL + P_REM + i)
                        nc.scalar.activation(parts[i][:, 1, :], rem[i][:], ACT.Copy).then_inc(cast_step, 1)
                for i in range(2):
                    act.wait_ge(sz_out[i], (b + 1) * (16 * MB // 2))
                    act.wait_ge(uD_out[i], (b + 1) * (16 * MB // 2))
                    act.wait_ge(parts_out[i], (b + 1) * (16 * MB))

        @block.gpsimd
        def _(pool):
            with nc.gpsimd.Fori(0, NB) as b:
                for m in range(MB):
                    pool.wait_ge(delta_done, b * MB + m + 1)
                    if m >= 2:
                        pool.wait_ge(cast_step, b * (MB * C_ALL) + (m - 2) * C_ALL + 2)
                    nc.gpsimd.tensor_tensor(du[m % 2][:], delta[m % 2][:], u[:, m, :], ALU.mult).then_inc(pool_step, 1)
                    if m >= 1:
                        pool.wait_ge(pool_step, b * (MB * P_ALL) + m * P_ALL)
                    for i, src in enumerate((delta, du)):
                        if i == 1:
                            pool.wait_ge(pool_step, b * (MB * P_ALL) + m * P_ALL + P_DU)
                        pool.wait_ge(cast_step, b * (MB * C_ALL) + m * C_ALL + 1 + i)
                        nc.gpsimd.tensor_tensor(rem[i][:], src[m % 2][:], parts[i][:, 0, :], ALU.subtract).then_inc(pool_step, 1)
                    for i in range(2):
                        pool.wait_ge(cast_step, b * (MB * C_ALL) + m * C_ALL + C_MID + 1 + i)
                        nc.gpsimd.tensor_tensor(parts[i][:, 2, :], rem[i][:], parts[i][:, 1, :], ALU.subtract).then_inc(pool_step, 1)

        @block.vector
        def _(dve):
            nc.vector.memset(xi[:, :, 0:HALO], 0.0).then_inc(halo_zeroed, 1)
            nc.vector.memset(mem["eps"][:], EPS).then_inc(halo_zeroed, 1)
            for b in range(NB):
                dve.wait_ge(ld_x[b], 16)
            with nc.vector.Fori(0, NB) as b:
                for n in range(BB):
                    nc.vector.bn_stats(st[:, n, :], mem["x"][:, bass.ds(b * BB + n, 1), :].rearrange("p a d -> p (a d)")).then_inc(stats_done, 1)
                wait_apart(dve, stats_done, (b + 1) * BB, passed)
                for n in range(BB):
                    nc.vector.bn_aggr(mv[:, n, :], st[:, n, :]).then_inc(mean_done, 1)
                dve.wait_ge(sd_done, b + 1)
                nc.vector.reciprocal(rs[:], sd[:]).then_inc(rs_done, 1)
                dve.wait_ge(rs_done, b + 1)
                for n in range(BB):
                    nc.vector.tensor_scalar(xn[:, n, :], mem["x"][:, bass.ds(b * BB + n, 1), :].rearrange("p a d -> p (a d)"), mv[:, n, 0:1], rs[:, n:n + 1],
                                            ALU.subtract, ALU.mult).then_inc(xn_done, 1)
                dve.wait_ge(ld_w, 16 * N_W)
                for m in range(MB):
                    dve.wait_ge(mm_act, b * ACT_OUTS + m + 1)
                    nc.vector.tensor_scalar(u[:, m, :], xi[:, m, 0:L], cw[:, m, 0:1], cb[:, m:m + 1], ALU.mult, ALU.add).then_inc(conv_step, 1)
                    for tap in range(1, TAPS):
                        dve.wait_ge(conv_step, b * (MB * TAPS) + m * TAPS + tap)
                        nc.vector.scalar_tensor_tensor(out=u[:, m, :], in0=xi[:, m, tap:tap + L], scalar=cw[:, m, tap:tap + 1], in1=u[:, m, :],
                                                       op0=ALU.mult, op1=ALU.add).then_inc(conv_step, 1)
                for j, dst in ((BJ, "B"), (CJ, "C")):
                    dve.wait_ge(mm_full, b * OUTS + j + 1)
                    nc.vector.tensor_copy(mem[dst][:, bass.ds(b * L, L)], mm[j % SLOTS][:]).then_inc(mm_dve, 1)
                for m in range(MB):
                    e = e_[m % 2]
                    dve.wait_ge(e_done, b * MB + m + 1)
                    if m >= 1:
                        dve.wait_ge(delta_done, b * MB + m)
                    nc.vector.tensor_scalar(q[:], e[:], LOG1P[-1], None, ALU.mult).then_inc(horner, 1)
                    for step, c in enumerate(LOG1P[-2::-1]):
                        dve.wait_ge(horner, b * (MB * NH) + m * NH + step + 1)
                        nc.vector.scalar_tensor_tensor(out=q[:], in0=q[:], scalar=c, in1=e[:], op0=ALU.add, op1=ALU.mult).then_inc(horner, 1)
                    dve.wait_ge(horner, b * (MB * NH) + (m + 1) * NH)
                    if m >= 2:
                        dve.wait_ge(pool_step, b * (MB * P_ALL) + (m - 2) * P_ALL + P_REM)
                    nc.vector.tensor_tensor(delta[m % 2][:], q[:], pos[m % 2][:], ALU.add).then_inc(delta_done, 1)
                dve.wait_ge(pool_step, (b + 1) * (MB * P_ALL))


def stage_scan(nc, io, mem):
    BODY = 2 * GP
    TURNS = NB * PAIRS // BODY
    AHEAD = 3
    NA, NBUF, NHB, NP = 2, 2, 4, 4
    with ExitStack() as ctx:
        sb = lambda n, s, d=F32: ctx.enter_context(nc.sbuf_tensor(n, s, d))
        sem = lambda n: ctx.enter_context(nc.semaphore(n))
        pick_wide = sb("pick_wide", [ROWS, GP, P])
        pick = sb("pick", [ROWS, GP, P], BF16)
        summer = sb("summer", [P, 2 * GP + 2 * GP - 2])
        delta_rows = [sb(f"delta_rows{i}", [ROWS, L], BF16) for i in range(2)]
        du_rows = [sb(f"du_rows{i}", [ROWS, L], BF16) for i in range(2)]
        A_cols = [sb(f"A_cols{i}", [P, GP]) for i in range(2)]
        inp = [sb(f"inp{i}", [P, L]) for i in range(NBUF)]
        state = [sb(f"state{i}", [P, L]) for i in range(NHB)]
        prod = [sb(f"prod{i}", [P, L]) for i in range(NP)]
        y_sb = [sb(f"y_sb{i}", [2 * GP, L]) for i in range(2)]
        decay = [ctx.enter_context(nc.psum_tensor(f"decay{i}", [P, L], F32)) for i in range(NA)]
        du_all = ctx.enter_context(nc.psum_tensor("du_all", [P, L], F32))
        y_ps = ctx.enter_context(nc.psum_tensor("y_ps", [2 * GP, L], F32))
        ld_const, pick_done = sem("ld_const"), sem("pick_done")
        rows_in = [sem(f"rows_in{i}") for i in range(2)]
        delta_spread = sem("delta_spread")
        du_spread = sem("du_spread")
        decay_done = sem("decay_done")
        inp_done = sem("inp_done")
        scan_done = sem("scan_done")
        prod_done = sem("prod_done")
        summed = sem("summed")
        y_copied = sem("y_copied")
        y_out = [sem(f"y_out{i}") for i in range(2)]

        block = ctx.enter_context(nc.Block())

        @block.sync
        def _(sp):
            for s in range(2):
                sp.sem_inc(y_out[s], 16)
            sp.dma_start(pick_wide[:], io["c_pick"]).then_inc(ld_const, 16)
            sp.dma_start(summer[:], io["c_summer"]).then_inc(ld_const, 16)

            def load(turn, s):
                at = (turn * 2 + s) * (ROWS * L)
                for rows, name in ((delta_rows, "delta_dram"), (du_rows, "du_dram")):
                    sp.dma_start(rows[s][:], mem[name][bass.ds(at, ROWS * L)].rearrange("(r n) -> r n", n=L)).then_inc(rows_in[s], 16)
                sp.dma_start(A_cols[s][:], mem["AT"][:, bass.ds(turn * BODY + s * GP, GP)]).then_inc(rows_in[s], 16)

            def store(turn, s):
                sp.wait_ge(y_copied, turn * 2 + s + 2)
                at = (turn * 2 + s) * (2 * GP * L)
                sp.dma_start(mem["y_dram"][bass.ds(at, 2 * GP * L)].rearrange("(r n) -> r n", n=L), y_sb[s][:]).then_inc(y_out[s], 16)

            for s in range(2):
                load(0, s)
            with nc.sync.Fori(1, TURNS) as turn:
                for s in range(2):
                    sp.wait_ge(du_spread, (turn - 1) * BODY + (s + 1) * GP)
                    sp.wait_ge(delta_spread, (turn - 1) * BODY + (s + 1) * GP)
                    sp.wait_ge(decay_done, (turn - 1) * BODY + (s + 1) * GP)
                    load(turn, s)
                    store(turn - 1, s)
            for s in range(2):
                store(TURNS - 1, s)
            for s in range(2):
                sp.wait_ge(y_out[s], 16 + 16 * TURNS)

        @block.tensor
        def _(pe):
            pe.sem_inc(summed, NP)
            pe.wait_ge(ld_const, 32)
            pe.wait_ge(pick_done, 1)

            def spread(turn, i):
                s, j = (i // GP) % 2, i % GP
                at = turn * BODY + i
                if j == 0:
                    pe.wait_ge(rows_in[s], turn * 48 + (i // BODY + 1) * 48)
                pe.wait_ge(inp_done, at + 1)
                for c in range(2):
                    cols = slice(c * HALF, (c + 1) * HALF)
                    last = nc.tensor.matmul(du_all[:, cols], pick[:, j, :], du_rows[s][:, cols], start=True, stop=True)
                last.then_inc(du_spread, 1)
                pe.wait_ge(scan_done, at + 1)
                for c in range(2):
                    cols = slice(c * HALF, (c + 1) * HALF)
                    last = nc.tensor.matmul(decay[i % NA][:, cols], pick[:, j, :], delta_rows[s][:, cols], start=True, stop=True)
                last.then_inc(delta_spread, 1)

            def add_up(turn, i):
                j = i % GP
                if j == 0:
                    pe.wait_ge(y_copied, turn * 2 + i // GP + 1)
                pe.wait_ge(prod_done, turn * BODY + i + 1 + NHB)
                for c in range(2):
                    last = nc.tensor.matmul(y_ps[:, c * HALF:(c + 1) * HALF], summer[:, 2 * GP - 2 - 2 * j:4 * GP - 2 - 2 * j],
                                            prod[i % NP][:, c * HALF:(c + 1) * HALF], start=(j == 0), stop=(j == GP - 1))
                last.then_inc(summed, 1)

            for i in range(AHEAD):
                spread(0, i)
            with nc.tensor.Fori(0, TURNS - 1) as turn:
                for i in range(BODY):
                    spread(turn, i + AHEAD)
                    add_up(turn, i)
            for i in range(BODY):
                if i + AHEAD < BODY:
                    spread(TURNS - 1, i + AHEAD)
                add_up(TURNS - 1, i)

        @block.scalar
        def _(act):
            act.sem_inc(y_copied, 1)
            act.wait_ge(ld_const, 32)
            nc.scalar.activation(pick[:], pick_wide[:], ACT.Copy).then_inc(pick_done, 1)

            def decays(turn, i):
                s, j = i // GP, i % GP
                if j == 0:
                    act.wait_ge(rows_in[s], turn * 48 + 48)
                act.wait_ge(delta_spread, turn * BODY + i + 1)
                nc.scalar.activation(decay[i % NA][:], decay[i % NA][:], ACT.Exp, scale=A_cols[s][:, j:j + 1]).then_inc(decay_done, 1)

            def copy_sums(turn, s):
                act.wait_ge(summed, turn * BODY + (s + 1) * GP + NP)
                act.wait_ge(y_out[s], turn * 16 + 16)
                nc.scalar.activation(y_sb[s][:], y_ps[:], ACT.Copy).then_inc(y_copied, 1)

            for i in range(BODY):
                decays(0, i)
                if i == GP + AHEAD:
                    copy_sums(0, 0)
            with nc.scalar.Fori(1, TURNS) as turn:
                for i in range(BODY):
                    decays(turn, i)
                    if i == AHEAD:
                        copy_sums(turn - 1, 1)
                    if i == GP + AHEAD:
                        copy_sums(turn, 0)
            copy_sums(TURNS - 1, 1)

        @block.vector
        def _(dve):
            dve.sem_inc(inp_done, 1)
            dve.sem_inc(scan_done, NA)
            for b in range(NB):
                B_b = mem["B"][:, b * L:(b + 1) * L]
                with nc.vector.Fori(0, GROUPS // 2) as gg:
                    first = b * PAIRS + gg * BODY

                    def inputs(i):
                        dve.wait_ge(du_spread, first + i + 1)
                        dve.wait_ge(scan_done, first + i + 1)
                        nc.vector.tensor_tensor(inp[i % NBUF][:], du_all[:], B_b, ALU.mult).then_inc(inp_done, 1)

                    inputs(0)
                    for i in range(BODY):
                        if i + 1 < BODY:
                            inputs(i + 1)
                        dve.wait_ge(inp_done, first + i + 2)
                        dve.wait_ge(decay_done, first + i + 1)
                        dve.wait_ge(prod_done, first + i + 1)
                        nc.vector.tensor_tensor_scan(state[i % NHB][:], decay[i % NA][:], inp[i % NBUF][:], 0.0, ALU.mult, ALU.add).then_inc(scan_done, 1)

        @block.gpsimd
        def _(pool):
            pool.sem_inc(prod_done, NHB)
            for b in range(NB):
                C_b = mem["C"][:, b * L:(b + 1) * L]
                with nc.gpsimd.Fori(0, GROUPS // 2) as gg:
                    first = b * PAIRS + gg * BODY
                    for i in range(BODY):
                        pool.wait_ge(scan_done, first + i + 1 + NA)
                        pool.wait_ge(summed, first + i + 1)
                        nc.gpsimd.tensor_tensor(prod[i % NP][:], state[i % NHB][:], C_b, ALU.mult).then_inc(prod_done, 1)


def wait_apart(eng, semaphore, value, passed):
    eng.wait_ge(semaphore, value)
    eng.sem_inc(passed, 1)


def stage_mixer_out(nc, io, mem):
    CB = HALF // P
    TURNS = T // HALF
    PER_B = L // HALF
    with ExitStack() as ctx:
        sb = lambda n, s, d=F32: ctx.enter_context(nc.sbuf_tensor(n, s, d))
        sem = lambda n: ctx.enter_context(nc.semaphore(n))
        w_out = sb("w_out", [P, MB, D])
        y = [sb(f"y{i}", [P, MB, HALF]) for i in range(PER_B)]
        uD = [sb(f"uDs{i}", [P, MB, HALF]) for i in range(PER_B)]
        sz = [sb(f"szs{i}", [P, MB, HALF]) for i in range(PER_B)]
        st, mv = sb("st1", [P, 2, 6]), sb("mv1_pair", [P, 2, 2])
        o = [ctx.enter_context(nc.psum_tensor(f"o{i}", [P, 2, D], F32)) for i in range(4)]
        ld_w = sem("ld_wout")
        ld = [sem(f"ld_y{i}") for i in range(PER_B)]
        sum_done, gated, projected, added = sem("sum_done"), sem("gated"), sem("projected"), sem("added")
        stats_done, mean_done, mean_kept, passed = sem("stats1_done"), sem("mean1_done"), sem("mean1_kept"), sem("passed1")
        block = ctx.enter_context(nc.Block())

        @block.sync
        def _(sp):
            sp.dma_start(w_out[:], io["L0_attn_W_out"].rearrange("(m p) n -> p m n", p=P)).then_inc(ld_w, 16)

            def load(b, h):
                cols = bass.ds(b * L + h * HALF, HALF)
                y_b = mem["y_dram"][bass.ds(b * (DI * L), DI * L)].rearrange("(m p n) -> p m n", p=P, n=L)
                sp.dma_start(y[h][:], y_b[:, :, h * HALF:(h + 1) * HALF]).then_inc(ld[h], 16)
                sp.dma_start(uD[h][:], mem["uD_dram"][:, cols].rearrange("(m p) n -> p m n", p=P)).then_inc(ld[h], 16)
                sp.dma_start(sz[h][:], mem["sz_dram"][:, cols].rearrange("(m p) n -> p m n", p=P)).then_inc(ld[h], 16)

            for h in range(PER_B):
                load(0, h)
            with nc.sync.Fori(1, NB) as b:
                for h in range(PER_B):
                    sp.wait_ge(projected, (b - 1) * (PER_B * 2) + (h + 1) * 2)
                    load(b, h)

        @block.vector
        def _(dve):
            with nc.vector.Fori(0, NB) as b:
                for h in range(PER_B):
                    turn = b * PER_B + h
                    dve.wait_ge(ld[h], (b + 1) * 48)
                    nc.vector.tensor_tensor(y[h][:], y[h][:], uD[h][:], ALU.add).then_inc(sum_done, 1)
                    dve.wait_ge(sum_done, turn + 1)
                    nc.vector.tensor_tensor(y[h][:], y[h][:], sz[h][:], ALU.mult).then_inc(gated, 1)
                for h in range(PER_B):
                    for pr in range(2):
                        pair = b * (PER_B * 2) + h * 2 + pr
                        dve.wait_ge(projected, pair + 1)
                        rows = mem["x"][:, bass.ds(pair * 2, 2), :]
                        nc.vector.scalar_tensor_tensor(out=rows, in0=rows, scalar=2.0, in1=o[h * 2 + pr][:], op0=ALU.mult, op1=ALU.add).then_inc(added, 1)
                        wait_apart(dve, added, pair + 1, passed)
                        for s in range(2):
                            nc.vector.bn_stats(st[:, s, :], mem["x"][:, bass.ds(pair * 2 + s, 1), :].rearrange("p a d -> p (a d)")).then_inc(stats_done, 1)
                        wait_apart(dve, stats_done, (pair + 1) * 2, passed)
                        for s in range(2):
                            nc.vector.bn_aggr(mv[:, s, :], st[:, s, :]).then_inc(mean_done, 1)
                        dve.wait_ge(mean_done, (pair + 1) * 2)
                        nc.vector.tensor_scalar(mem["mv1"][:, bass.ds(pair * 2, 2), :], mv[:], 1.0, None, ALU.mult).then_inc(mean_kept, 1)

        @block.tensor
        def _(pe):
            pe.wait_ge(ld_w, 16)
            with nc.tensor.Fori(0, NB) as b:
                for h in range(PER_B):
                    pe.wait_ge(gated, b * PER_B + h + 1)
                    for pr in range(2):
                        for s in range(2):
                            n = pr * 2 + s
                            for m in range(MB):
                                last = nc.tensor.matmul(o[h * 2 + pr][:, s, :], y[h][:, m, n * P:(n + 1) * P], w_out[:, m, :], start=(m == 0), stop=(m == MB - 1))
                        last.then_inc(projected, 1)


def stage_attention(nc, io, mem):
    SLOT = 2
    SG = len(HEAD_GROUPS)
    TP = -(-HJ_CHUNKS // 4)
    with ExitStack() as ctx:
        sb = lambda n, s, d=F32: ctx.enter_context(nc.sbuf_tensor(n, s, d))
        sem = lambda n: ctx.enter_context(nc.semaphore(n))
        vo = sb("vo_in", [P, NB, HJ_CHUNKS, D])
        sd, rs = sb("sd1", [P, TB]), sb("rs1", [P, TB])
        x1 = [sb(f"x1_{i}", [P, D]) for i in range(SLOT)]
        xT = [sb(f"xT1_{i}", [P, KD, P]) for i in range(SLOT)]
        p = [sb(f"p{i}", [P, H, S2]) for i in range(SLOT)]
        den = [sb(f"den{i}", [P, H]) for i in range(SLOT)]
        pT = [sb(f"pT{i}", [P, HJ_CHUNKS, P]) for i in range(SLOT)]
        st, mv = sb("st2", [P, SLOT, 6]), sb("mv2_pair", [P, SLOT, 2])
        xT_ps = ctx.enter_context(nc.psum_tensor("xT_ps", [P, KD, P], F32))
        s_ps = [ctx.enter_context(nc.psum_tensor(f"s_ps{i}", [P, HALF], F32)) for i in range(SG)]
        pT_ps = [ctx.enter_context(nc.psum_tensor(f"pT_ps{i}", [P, 4, P], F32)) for i in range(2)]
        o_ps = [ctx.enter_context(nc.psum_tensor(f"o_ps{i}", [P, D], F32)) for i in range(SLOT)]
        ld_vo, ones_set = sem("ld_vo"), sem("ones_set")
        sd_done, rs_done, x1_done = sem("sd1_done"), sem("rs1_done"), sem("x1_done")
        xT_full, xT_copied, scored = sem("xT_full"), sem("xT_copied"), sem("scored")
        clipped, exp_done, den_done, inv_done, p_done = sem("clipped"), sem("exp_done"), sem("den_done"), sem("inv_done"), sem("p_done")
        pT_full, pT_copied, out_done, added = sem("pT_full"), sem("pT_copied"), sem("out_done"), sem("added2")
        stats_done, mean_done, mean_kept, passed = sem("stats2_done"), sem("mean2_done"), sem("mean2_kept"), sem("passed2")
        block = ctx.enter_context(nc.Block())

        @block.sync
        def _(sp):
            for b in range(NB):
                sp.dma_start(vo[:, b, 0:HJ_CHUNKS - 1, :], mem["vo_dram"][b, 0:(HJ_CHUNKS - 1) * P, :].rearrange("(c p) e -> p c e", p=P)).then_inc(ld_vo, 16)
                sp.dma_start(vo[0:HJ_LAST, b, HJ_CHUNKS - 1, :], mem["vo_dram"][b, (HJ_CHUNKS - 1) * P:HJ, :]).then_inc(ld_vo, 16)
                sp.dma_start(vo[HJ_LAST:HJ_LAST + 1, b, HJ_CHUNKS - 1, :], io["L0_xattn_bo"].unsqueeze(0)).then_inc(ld_vo, 16)

        @block.scalar
        def _(act):
            nc.scalar.activation(sd[:], mem["mv1"][:, :, 1], ACT.Sqrt, bias=mem["eps"][:, 0:1]).then_inc(sd_done, 1)
            with nc.scalar.Fori(0, TB // SLOT) as i:
                for s in range(SLOT):
                    n = i * SLOT + s
                    act.wait_ge(xT_full, n + 1)
                    nc.scalar.activation(xT[s][:], xT_ps[:], ACT.Copy).then_inc(xT_copied, 1)
                for s in range(SLOT):
                    n = i * SLOT + s
                    act.wait_ge(clipped, (n + 2) * SG)
                    nc.scalar.activation(p[s][:], p[s][:], ACT.Exp).then_inc(exp_done, 1)
                for s in range(SLOT):
                    n = i * SLOT + s
                    for t in range(TP):
                        act.wait_ge(pT_full, n * TP + t + 1)
                        if t == 0:
                            act.wait_ge(ones_set, 1)
                        chunks = range(4 * t, min(4 * t + 4, HJ_CHUNKS))
                        whole = sum(1 for c in chunks if c < HJ_CHUNKS - 1)
                        if whole:
                            last = nc.scalar.activation(pT[s][:, 4 * t:4 * t + whole, :], pT_ps[t % 2][:, 0:whole, :], ACT.Copy)
                        if HJ_CHUNKS - 1 in chunks:
                            last = nc.scalar.activation(pT[s][0:HJ_LAST, HJ_CHUNKS - 1, :], pT_ps[t % 2][0:HJ_LAST, whole, :], ACT.Copy)
                        last.then_inc(pT_copied, 1)

        @block.vector
        def _(dve):
            dve.sem_inc(clipped, SG)
            for s in range(SLOT):
                last = nc.vector.memset(pT[s][64:P, HJ_CHUNKS - 1, :], 1.0)
            last.then_inc(ones_set, 1)
            dve.wait_ge(sd_done, 1)
            nc.vector.reciprocal(rs[:], sd[:]).then_inc(rs_done, 1)
            dve.wait_ge(rs_done, 1)
            with nc.vector.Fori(0, NB) as b:
                upper = mem["upper"][:, bass.ds(b * S2, S2)]
                with nc.vector.Fori(0, BB // SLOT) as i:
                    for s in range(SLOT):
                        n = b * BB + i * SLOT + s
                        nc.vector.tensor_scalar(x1[s][:], mem["x"][:, bass.ds(n, 1), :].rearrange("p a d -> p (a d)"),
                                                mem["mv1"][:, bass.ds(n, 1), 0:1].rearrange("p a d -> p (a d)"), rs[:, bass.ds(n, 1)],
                                                ALU.subtract, ALU.mult).then_inc(x1_done, 1)
                    for s in range(SLOT):
                        n = b * BB + i * SLOT + s
                        for g, (h0, h1) in enumerate(HEAD_GROUPS):
                            dve.wait_ge(scored, n * SG + g + 1)
                            nc.vector.scalar_tensor_tensor(out=p[s][:, h0:h1, :], in0=s_ps[g][:, 0:(h1 - h0) * S2].rearrange("p (h j) -> p h j", j=S2),
                                                           scalar=-5.0, in1=upper.unsqueeze(1).broadcast_to([P, h1 - h0, S2]),
                                                           op0=ALU.max, op1=ALU.min).then_inc(clipped, 1)
                    for s in range(SLOT):
                        n = b * BB + i * SLOT + s
                        dve.wait_ge(exp_done, n + 1)
                        nc.vector.tensor_reduce(den[s][:], p[s][:], AXX, ALU.add).then_inc(den_done, 1)
                        dve.wait_ge(den_done, n + 1)
                        nc.vector.reciprocal(den[s][:], den[s][:]).then_inc(inv_done, 1)
                    for s in range(SLOT):
                        n = b * BB + i * SLOT + s
                        dve.wait_ge(out_done, n + 1)
                        rows = mem["x"][:, bass.ds(n, 1), :].rearrange("p a d -> p (a d)")
                        nc.vector.tensor_tensor(rows, x1[s][:], o_ps[s][:], ALU.add).then_inc(added, 1)
                    after = b * BB + i * SLOT + SLOT
                    wait_apart(dve, added, after, passed)
                    for s in range(SLOT):
                        nc.vector.bn_stats(st[:, s, :], mem["x"][:, bass.ds(b * BB + i * SLOT + s, 1), :].rearrange("p a d -> p (a d)")).then_inc(stats_done, 1)
                    wait_apart(dve, stats_done, after, passed)
                    for s in range(SLOT):
                        nc.vector.bn_aggr(mv[:, s, :], st[:, s, :]).then_inc(mean_done, 1)
                    dve.wait_ge(mean_done, after)
                    nc.vector.tensor_scalar(mem["mv2"][:, bass.ds(b * BB + i * SLOT, SLOT), :], mv[:], 1.0, None, ALU.mult).then_inc(mean_kept, 1)

        @block.gpsimd
        def _(pool):
            with nc.gpsimd.Fori(0, TB // SLOT) as i:
                for s in range(SLOT):
                    pool.wait_ge(inv_done, i * SLOT + s + 1)
                    nc.gpsimd.tensor_tensor(p[s][:], p[s][:], den[s][:].unsqueeze(2).broadcast_to([P, H, S2]), ALU.mult).then_inc(p_done, 1)

        @block.tensor
        def _(pe):
            def scores(b, n, s):
                pe.wait_ge(x1_done, n + 1)
                for k in range(KD):
                    last = nc.tensor.transpose(xT_ps[:, k, :], x1[s][:, k * P:(k + 1) * P], mem["ident"][:])
                last.then_inc(xT_full, 1)
                pe.wait_ge(xT_copied, n + 1)
                for g, (h0, h1) in enumerate(HEAD_GROUPS):
                    pe.wait_ge(clipped, n * SG + g + 1)
                    for k in range(KD):
                        last = nc.tensor.matmul(s_ps[g][:, 0:(h1 - h0) * S2], xT[s][:, k, :], mem["G"][:, b, k, h0 * S2:h1 * S2], start=(k == 0), stop=(k == KD - 1))
                    last.then_inc(scored, 1)

            def outputs(b, n, s):
                pe.wait_ge(p_done, n + 1)
                flat = p[s][:].rearrange("p h j -> p (h j)")
                for t in range(TP):
                    if t >= 2:
                        pe.wait_ge(pT_copied, n * TP + t - 1)
                    for c in range(4 * t, min(4 * t + 4, HJ_CHUNKS)):
                        w = P if c < HJ_CHUNKS - 1 else HJ_LAST
                        last = nc.tensor.transpose(pT_ps[t % 2][0:w, c - 4 * t, :], flat[:, c * P:c * P + w], mem["ident"][:])
                    last.then_inc(pT_full, 1)
                for c in range(HJ_CHUNKS):
                    w = P if c < HJ_CHUNKS - 1 else HJ_LAST + 1
                    if c % 4 == 0:
                        pe.wait_ge(pT_copied, n * TP + c // 4 + 1)
                    last = nc.tensor.matmul(o_ps[s][:], pT[s][0:w, c, :], vo[0:w, b, c, :], start=(c == 0), stop=(c == HJ_CHUNKS - 1))
                last.then_inc(out_done, 1)

            pe.wait_ge(ld_vo, 16 * 3 * NB)
            for b in range(NB):
                with nc.tensor.Fori(0, BB // SLOT) as i:
                    for s in range(SLOT):
                        scores(b, b * BB + i * SLOT + s, s)
                    for s in range(SLOT):
                        outputs(b, b * BB + i * SLOT + s, s)


def stage_experts(nc, io, mem):
    CB = HALF // P
    CH = T // HALF
    SLOT = 2
    G_OPS = 15
    with ExitStack() as ctx:
        sb = lambda n, s, d=F32: ctx.enter_context(nc.sbuf_tensor(n, s, d))
        sem = lambda n: ctx.enter_context(nc.semaphore(n))
        w_gate = sb("w_gate", [P, KD, FB, F])
        w_up = sb("w_up", [P, KD, FB, F])
        w_down = sb("w_down", [P, FB, D])
        w_r = sb("w_r", [P, KD, E])
        bias = sb("bias", [P, E])
        rank = sb("rank", [P, E])
        expand = sb("expand", [E, E, P])
        sd, rs = sb("sd2", [P, TB]), sb("rs2", [P, TB])
        x2 = [sb(f"x2_{i}", [P, CB, D]) for i in range(SLOT)]
        xT = [sb(f"xT2_{i}", [P, KD, HALF]) for i in range(SLOT)]
        lg, eq, hot1, l2, hot2 = (sb(n, [P, CB, E]) for n in ("lg", "eq", "hot1", "l2", "hot2"))
        m1, m2, first1, first2, gap, th, p1, p2 = (sb(n, [P, CB]) for n in ("m1", "m2", "first1", "first2", "gap", "th", "w_first", "w_second"))
        rw = [sb(f"rw{i}", [P, CB, E]) for i in range(SLOT)]
        rwT = [sb(f"rwT{i}", [E, HALF]) for i in range(SLOT)]
        act_g = [sb(f"act_g{i}", [P, HALF]) for i in range(SLOT)]
        hid = [sb(f"hid{i}", [P, FB, HALF]) for i in range(SLOT)]
        st, mv_pair = sb("st3", [P, 2, 6]), sb("mv3_pair", [P, 2, 2])
        mv, sd3, rs3 = sb("mv3", [P, TB, 2]), sb("sd3", [P, TB]), sb("rs3", [P, TB])
        tp = ctx.enter_context(nc.psum_tensor("tp2", [P, HALF], F32))
        lg_ps = ctx.enter_context(nc.psum_tensor("lg_ps", [P, CB, E], F32))
        g_ps = [ctx.enter_context(nc.psum_tensor(f"g_ps{i}", [P, HALF], F32)) for i in range(2)]
        u_ps = [ctx.enter_context(nc.psum_tensor(f"u_ps{i}", [P, HALF], F32)) for i in range(2)]
        rw_ps = ctx.enter_context(nc.psum_tensor("rw_ps", [P, HALF], F32))
        d_ps = ctx.enter_context(nc.psum_tensor("d_ps", [P, 2, D], F32))
        ld_r, ld_gu, ld_dn = sem("ld_r"), sem("ld_gu"), sem("ld_dn")
        sd_done, rs_done, x2_done = sem("sd2_done"), sem("rs2_done"), sem("x2_done")
        tp_full, xT_copied, rwT_copied = sem("tp2_full"), sem("xT2_copied"), sem("rwT_copied")
        logits_done, routing, routed, th_done = sem("logits_done"), sem("routing"), sem("routed"), sem("th_done")
        up_full, rw_full, silu_done, mixed, hid_done = sem("up_full"), sem("rw_full"), sem("silu_done"), sem("mixed"), sem("hid_done")
        down_full, added, stats_done, mean_done = sem("down_full"), sem("added3"), sem("stats3_done"), sem("mean3_done")
        mean_kept, passed = sem("mean3_kept"), sem("passed3")
        sd3_done, rs3_done, normed, stored = sem("sd3_done"), sem("rs3_done"), sem("normed"), sem("stored3")
        block = ctx.enter_context(nc.Block())

        @block.sync
        def _(sp):
            sp.dma_start(w_r[:], io["L0_ffn_Wr"].rearrange("(k p) e -> p k e", p=P)).then_inc(ld_r, 16)
            sp.dma_start(bias[:], io["L0_ffn_expert_bias"].unsqueeze(0).broadcast_to([P, E])).then_inc(ld_r, 16)
            sp.dma_start(rank[:], io["c_rank"]).then_inc(ld_r, 16)
            sp.dma_start(expand[:], io["c_expand"]).then_inc(ld_r, 16)
            for w, routed_w, shared in ((w_gate, "L0_ffn_Wg", "L0_ffn_Sg"), (w_up, "L0_ffn_Wu", "L0_ffn_Su")):
                for k in range(KD):
                    sp.dma_start(w[:, k, 0:E, :], io[routed_w][:, k * P:(k + 1) * P, :].rearrange("e p f -> p e f")).then_inc(ld_gu, 16)
                    sp.dma_start(w[:, k, E:FB, :].rearrange("p a f -> p (a f)"), io[shared][k * P:(k + 1) * P, :]).then_inc(ld_gu, 16)
            sp.dma_start(w_down[:, 0:E, :], io["L0_ffn_Wd"].rearrange("e p d -> p e d")).then_inc(ld_dn, 16)
            sp.dma_start(w_down[:, E:FB, :], io["L0_ffn_Sd"].rearrange("(a p) d -> p a d", p=P)).then_inc(ld_dn, 16)
            with nc.sync.Fori(0, CH) as c:
                sp.wait_ge(normed, (c + 1) * CB)
                sp.dma_start(io["out"][bass.ds(c * HALF, HALF), :].rearrange("(n p) d -> p n d", p=P), mem["x"][:, bass.ds(c * CB, CB), :]).then_inc(stored, 16)
            sp.wait_ge(stored, 16 * CH)

        @block.scalar
        def _(act):
            nc.scalar.activation(sd[:], mem["mv2"][:, :, 1], ACT.Sqrt, bias=mem["eps"][:, 0:1]).then_inc(sd_done, 1)
            with nc.scalar.Fori(0, CH // SLOT) as i:
                for s in range(SLOT):
                    c = i * SLOT + s
                    for k in range(KD):
                        act.wait_ge(tp_full, c * (KD + 1) + k + 1)
                        nc.scalar.activation(xT[s][:, k, :], tp[:], ACT.Copy).then_inc(xT_copied, 1)
                    act.wait_ge(routing, c * G_OPS + 9)
                    nc.scalar.activation(th[:], gap[:], ACT.Tanh, scale=0.5).then_inc(th_done, 1)
                    act.wait_ge(tp_full, (c + 1) * (KD + 1))
                    nc.scalar.activation(rwT[s][:], tp[0:E, :], ACT.Copy).then_inc(rwT_copied, 1)
                    for f in range(FB):
                        j = c * FB + f
                        act.wait_ge(up_full, j + 1)
                        if f >= 2:
                            act.wait_ge(mixed, j - 1)
                        nc.scalar.activation(act_g[f % 2][:], g_ps[f % 2][:], ACT.Silu).then_inc(silu_done, 1)
            act.wait_ge(mean_kept, TB // 2)
            nc.scalar.activation(sd3[:], mv[:, :, 1], ACT.Sqrt, bias=mem["eps"][:, 0:1]).then_inc(sd3_done, 1)

        @block.vector
        def _(dve):
            dve.wait_ge(sd_done, 1)
            nc.vector.reciprocal(rs[:], sd[:]).then_inc(rs_done, 1)
            dve.wait_ge(rs_done, 1)
            dve.wait_ge(ld_r, 64)

            def wide(a):
                return a.unsqueeze(2).broadcast_to([P, CB, E])

            def each(a):
                return a.unsqueeze(1).broadcast_to([P, CB, E])

            with nc.vector.Fori(0, CH // SLOT) as i:
                for s in range(SLOT):
                    c = i * SLOT + s
                    for n in range(CB):
                        nc.vector.tensor_scalar(x2[s][:, n, :], mem["x"][:, bass.ds(c * CB + n, 1), :].rearrange("p a d -> p (a d)"),
                                                mem["mv2"][:, bass.ds(c * CB + n, 1), 0:1].rearrange("p a d -> p (a d)"), rs[:, bass.ds(c * CB + n, 1)],
                                                ALU.subtract, ALU.mult).then_inc(x2_done, 1)

                    def then(n, ins):
                        ins.then_inc(routing, 1)
                        dve.wait_ge(routing, c * G_OPS + n)

                    dve.wait_ge(logits_done, c + 1)
                    then(1, nc.vector.tensor_tensor(lg[:], lg_ps[:], each(bias[:]), ALU.add))
                    then(2, nc.vector.tensor_reduce(m1[:], lg[:], AXX, ALU.max))
                    then(3, nc.vector.tensor_tensor(eq[:], lg[:], wide(m1[:]), ALU.is_equal))
                    then(4, nc.vector.tensor_tensor(eq[:], eq[:], each(rank[:]), ALU.mult))
                    then(5, nc.vector.tensor_reduce(first1[:], eq[:], AXX, ALU.max))
                    then(6, nc.vector.tensor_tensor(hot1[:], each(rank[:]), wide(first1[:]), ALU.is_equal))
                    then(7, nc.vector.scalar_tensor_tensor(out=l2[:], in0=hot1[:], scalar=-3e38, in1=lg[:], op0=ALU.mult, op1=ALU.add))
                    then(8, nc.vector.tensor_reduce(m2[:], l2[:], AXX, ALU.max))
                    then(9, nc.vector.tensor_tensor(gap[:], m2[:], m1[:], ALU.subtract))
                    then(10, nc.vector.tensor_tensor(eq[:], l2[:], wide(m2[:]), ALU.is_equal))
                    then(11, nc.vector.tensor_tensor(eq[:], eq[:], each(rank[:]), ALU.mult))
                    then(12, nc.vector.tensor_reduce(first2[:], eq[:], AXX, ALU.max))
                    then(13, nc.vector.tensor_tensor(hot2[:], each(rank[:]), wide(first2[:]), ALU.is_equal))
                    dve.wait_ge(th_done, c + 1)
                    nc.vector.tensor_scalar(p2[:], th[:], 0.5, 0.5, ALU.mult, ALU.add)
                    then(14, nc.vector.tensor_scalar(p1[:], th[:], -0.5, 0.5, ALU.mult, ALU.add))
                    nc.vector.tensor_tensor(hot1[:], hot1[:], wide(p1[:]), ALU.mult)
                    then(15, nc.vector.tensor_tensor(hot2[:], hot2[:], wide(p2[:]), ALU.mult))
                    nc.vector.tensor_tensor(rw[s][:], hot1[:], hot2[:], ALU.add).then_inc(routed, 1)
                    for f in range(FB):
                        j = c * FB + f
                        dve.wait_ge(silu_done, j + 1)
                        nc.vector.tensor_tensor(hid[s][:, f, :], act_g[f % 2][:], u_ps[f % 2][:], ALU.mult).then_inc(mixed, 1)
                        if f < E:
                            dve.wait_ge(mixed, j + 1)
                            dve.wait_ge(rw_full, c * E + f + 1)
                            nc.vector.tensor_tensor(hid[s][:, f, :], hid[s][:, f, :], rw_ps[:], ALU.mult).then_inc(hid_done, 1)
                    for pr in range(2):
                        pair = c * 2 + pr
                        rows = mem["x"][:, bass.ds(pair * 2, 2), :]
                        dve.wait_ge(down_full, pair + 1)
                        nc.vector.tensor_tensor(rows, x2[s][:, 2 * pr:2 * pr + 2, :], d_ps[:], ALU.add).then_inc(added, 1)
                        wait_apart(dve, added, pair + 1, passed)
                        for t in range(2):
                            nc.vector.bn_stats(st[:, t, :], mem["x"][:, bass.ds(pair * 2 + t, 1), :].rearrange("p a d -> p (a d)")).then_inc(stats_done, 1)
                        wait_apart(dve, stats_done, (pair + 1) * 2, passed)
                        for t in range(2):
                            nc.vector.bn_aggr(mv_pair[:, t, :], st[:, t, :]).then_inc(mean_done, 1)
                        dve.wait_ge(mean_done, (pair + 1) * 2)
                        nc.vector.tensor_scalar(mv[:, bass.ds(pair * 2, 2), :], mv_pair[:], 1.0, None, ALU.mult).then_inc(mean_kept, 1)
            dve.wait_ge(sd3_done, 1)
            nc.vector.reciprocal(rs3[:], sd3[:]).then_inc(rs3_done, 1)
            dve.wait_ge(rs3_done, 1)
            for n in range(TB):
                nc.vector.tensor_scalar(mem["x"][:, n, :], mem["x"][:, n, :], mv[:, n, 0:1], rs3[:, n:n + 1], ALU.subtract, ALU.mult).then_inc(normed, 1)

        @block.tensor
        def _(pe):
            pe.wait_ge(ld_r, 64)
            with nc.tensor.Fori(0, CH // SLOT) as i:
                for s in range(SLOT):
                    c = i * SLOT + s
                    pe.wait_ge(x2_done, (c + 1) * CB)
                    for k in range(KD):
                        if k >= 1:
                            pe.wait_ge(xT_copied, c * KD + k)
                        for n in range(CB):
                            last = nc.tensor.transpose(tp[:, n * P:(n + 1) * P], x2[s][:, n, k * P:(k + 1) * P], mem["ident"][:])
                        last.then_inc(tp_full, 1)
                    pe.wait_ge(xT_copied, (c + 1) * KD)
                    for n in range(CB):
                        for k in range(KD):
                            last = nc.tensor.matmul(lg_ps[:, n, :], xT[s][:, k, n * P:(n + 1) * P], w_r[:, k, :], start=(k == 0), stop=(k == KD - 1))
                    last.then_inc(logits_done, 1)

                    def up(f):
                        j = c * FB + f
                        if f >= 2:
                            pe.wait_ge(mixed, j - 1)
                        for k in range(KD):
                            nc.tensor.matmul(g_ps[f % 2][:], w_gate[:, k, f, :], xT[s][:, k, :], start=(k == 0), stop=(k == KD - 1))
                        for k in range(KD):
                            last = nc.tensor.matmul(u_ps[f % 2][:], w_up[:, k, f, :], xT[s][:, k, :], start=(k == 0), stop=(k == KD - 1))
                        last.then_inc(up_full, 1)

                    pe.wait_ge(ld_gu, 16 * 4 * KD)
                    up(0)
                    up(1)
                    pe.wait_ge(routed, c + 1)
                    for n in range(CB):
                        last = nc.tensor.transpose(tp[0:E, n * P:(n + 1) * P], rw[s][:, n, :], mem["ident"][:])
                    last.then_inc(tp_full, 1)
                    pe.wait_ge(rwT_copied, c + 1)
                    for f in range(FB):
                        if f < E:
                            if f >= 1:
                                pe.wait_ge(hid_done, c * E + f)
                            nc.tensor.matmul(rw_ps[:], expand[:, f, :], rwT[s][:], start=True, stop=True).then_inc(rw_full, 1)
                        if f + 2 < FB:
                            up(f + 2)
                    pe.wait_ge(ld_dn, 32)
                    pe.wait_ge(mixed, (c + 1) * FB)
                    pe.wait_ge(hid_done, (c + 1) * E)
                    for pr in range(2):
                        if pr:
                            pe.wait_ge(added, c * 2 + pr)
                        for t in range(2):
                            n = 2 * pr + t
                            for f in range(FB):
                                last = nc.tensor.matmul(d_ps[:, t, :], hid[s][:, f, n * P:(n + 1) * P], w_down[:, f, :], start=(f == 0), stop=(f == FB - 1))
                        last.then_inc(down_full, 1)


def build(nc, io):
    with ExitStack() as ctx:
        sb = lambda n, s, d=F32: ctx.enter_context(nc.sbuf_tensor(n, s, d))
        mem = {
            "ident": sb("ident", [P, P]),
            "eps": sb("eps", [P, 1]),
            "x": sb("x", [P, TB, D]),
            "B": sb("B", [P, T]), "C": sb("C", [P, T]),
            "AT": sb("AT", [P, NB * PAIRS]),
            "G": sb("G", [P, NB, KD, HJ]),
            "upper": sb("upper", [P, NB * S2]),
            "mv1": sb("mv1", [P, TB, 2]), "mv2": sb("mv2", [P, TB, 2]),
        }
        for name, shape, dt in (("delta_dram", [NB * DI * PARTS * L], BF16), ("du_dram", [NB * DI * PARTS * L], BF16),
                                ("uD_dram", [DI, T], F32), ("sz_dram", [DI, T], F32), ("y_dram", [NB * DI * L], F32),
                                ("vo_dram", [NB, HJ, D], F32)):
            mem[name] = nc.dram_tensor(name, shape, dt, kind="Internal").ap()
        stage_context(nc, io, mem)
        stage_mixer_in(nc, io, mem)
        stage_scan(nc, io, mem)
        stage_mixer_out(nc, io, mem)
        stage_attention(nc, io, mem)
        stage_experts(nc, io, mem)


_INS = ["x", "ctx_1024", "mask_BxS2_bk1", "L0_attn_W_in", "L0_attn_W_xproj", "L0_attn_W_dt", "L0_attn_A_log", "L0_attn_W_out", "L0_xattn_Wq",
        "L0_xattn_Wkv", "L0_xattn_Wo", "L0_xattn_bo", "L0_ffn_Wr", "L0_ffn_Wg", "L0_ffn_Wu", "L0_ffn_Wd", "L0_ffn_Sg",
        "L0_ffn_Su", "L0_ffn_Sd", "L0_ffn_expert_bias"]


def _constants():
    import numpy as np
    pick = np.zeros((ROWS, GP, P), np.float32)
    for j in range(GP):
        for c in range(2):
            at = (j * 2 + c) * PARTS
            pick[at:at + PARTS, j, c * NS:(c + 1) * NS] = 1
    summer = np.zeros((P, 4 * GP - 2), np.float32)
    for c in range(2):
        summer[c * NS:(c + 1) * NS, 2 * GP - 2 + c] = 1
    expand = np.zeros((E, E, P), np.float32)
    for e in range(E):
        expand[e, e, :] = 1
    rank = np.ascontiguousarray(np.broadcast_to(np.arange(E, 0, -1, dtype=np.float32), (P, E)))
    return {"c_ident": np.eye(P, dtype=np.float32), "c_pick": pick, "c_summer": summer, "c_expand": expand, "c_rank": rank}


def kernel(**inputs):
    import numpy as _np
    import concourse.bacc as _bacc
    from concourse import mybir as _mybir
    from concourse.bass_utils import run_bass_kernel_spmd as _run

    nc = _bacc.Bacc("TRN2", target_bir_lowering=False, num_devices=1)
    arrays, io = {}, {}
    consts = _constants()
    vectors = [_np.asarray(inputs[name]).reshape(-1, P).T for name in ("L0_attn_ln_w", "L0_attn_ln_b")]
    vectors.append(_np.asarray(inputs["L0_attn_conv_w"]).reshape(MB, P, TAPS).transpose(1, 0, 2).reshape(P, MB * TAPS))
    vectors += [_np.asarray(inputs[name]).reshape(-1, P).T for name in ("L0_attn_conv_b", "L0_attn_b_dt", "L0_attn_D")]
    consts["vectors"] = _np.concatenate(vectors, axis=1)
    for name in _INS + list(consts):
        a = _np.ascontiguousarray(inputs[name] if name in inputs else consts[name])
        arrays[f"in_{name}"] = a
        io[name] = nc.dram_tensor(f"in_{name}", a.shape, _mybir.dt.from_np(a.dtype), kind="ExternalInput").ap()
    io["out"] = nc.dram_tensor("out_0", (T, D), F32, kind="ExternalOutput").ap()
    build(nc, io)
    r = _run(nc, [arrays], core_ids=[0])
    return r.results[0]["out_0"].reshape(NB, L, D)
```

```python
import concourse.bass as bass
from concourse import mybir
from contextlib import ExitStack

F32 = mybir.dt.float32
BF16 = mybir.dt.bfloat16
U8 = mybir.dt.uint8
ALU = mybir.AluOpType
ACT = mybir.ActivationFunctionType
AXX = mybir.AxisListType.X

P = 128
NB, L, D = 2, 1024, 256
T = NB * L
KD = D // P
DI, NS, R = 512, 64, 16
MB = DI // P
TAPS = 4
S2, H, DH = 77, 16, 64
HJ = H * S2
E, F = 8, 128
FB = E + 2
TB = T // P
BB = L // P
HALF = 512
QM = 2
QD = MB // QM
QUARTERS = NB * QD
EPS = 1e-5
LOG1P = (0.99999976, -0.49997175, 0.3327193, -0.24474774, 0.17687477, -0.10685003, 0.0434939, -0.008371153)
HEAD_GROUPS = ((0, 6), (6, 11), (11, 16))
HJ_CHUNKS = -(-HJ // P)
HJ_LAST = HJ - (HJ_CHUNKS - 1) * P


def stage_context(nc, io, mem):
    KV = 2 * H // 2
    BANKS = 8
    with ExitStack() as ctx:
        sb = lambda n, s, d=F32: ctx.enter_context(nc.sbuf_tensor(n, s, d))
        sem = lambda n: ctx.enter_context(nc.semaphore(n))
        cx = sb("cx", [S2, NB, D])
        wq = sb("wq", [P, KD, H * DH])
        wkv = sb("wkv", [P, KD, 2 * H * DH])
        wo = sb("wo", [P, H // 2, D])
        cxT = sb("cxT", [P, KD, NB * S2])
        wqT = sb("wqT", [P, H // 2, D])
        kvT = sb("kvT", [P, 2 * H, NB * S2])
        vo = sb("vo", [S2, NB, H, D])
        mask = sb("mask", [P, NB * S2], U8)
        bank = [ctx.enter_context(nc.psum_tensor(f"cbank{i}", [P, HALF], F32)) for i in range(BANKS)]
        ld_ctx, ld_wkv, ld_wq, ld_wo = (sem(n) for n in ("ld_ctx", "ld_wkv", "ld_wq", "ld_wo"))
        ld_mask = sem("ld_mask")
        kv_zeroed = sem("kv_zeroed")
        filled = sem("filled")
        act_emptied = sem("act_emptied")
        dve_emptied = sem("dve_emptied")
        limits_done, stored = sem("limits_done"), sem("stored")
        J_CTX, J_KV = 0, 1
        J_WQ = J_KV + KV // 2
        J_G = J_WQ + H // 4
        J_VO = J_G + NB * KD * len(HEAD_GROUPS)
        J_END = J_VO + NB * H // 2

        def emptied(eng, job):
            if job % 2:
                eng.wait_ge(dve_emptied, job // 2 + 1)
            else:
                eng.wait_ge(act_emptied, job // 2 + 1)

        block = ctx.enter_context(nc.Block())

        @block.sync
        def _(sp):
            sp.dma_start(cx[:], io["ctx_1024"].rearrange("b j d -> j b d")).then_inc(ld_ctx, 16)
            sp.dma_start(wkv[:], io["L0_xattn_Wkv"].rearrange("(k p) n -> p k n", p=P)).then_inc(ld_wkv, 16)
            sp.dma_start(wq[:], io["L0_xattn_Wq"].rearrange("(k p) n -> p k n", p=P)).then_inc(ld_wq, 16)
            sp.dma_start(mask[:], io["mask_BxS2_bk1"].rearrange("b j -> (b j)").unsqueeze(0).broadcast_to([P, NB * S2])).then_inc(ld_mask, 16)
            sp.dma_start(wo[:], io["L0_xattn_Wo"].rearrange("(k p) n -> p k n", p=P)).then_inc(ld_wo, 16)
            for b in range(NB):
                emptied(sp, J_VO + (b + 1) * H // 2 - 1)
                emptied(sp, J_VO + (b + 1) * H // 2 - 2)
                sp.dma_start(mem["vo_dram"][b, :, :].rearrange("(h j) e -> j h e", j=S2), vo[:, b, :, :]).then_inc(stored, 16)
            sp.wait_ge(stored, 16 * NB)

        @block.gpsimd
        def _(pool):
            nc.gpsimd.memset(kvT[:], 0.0).then_inc(kv_zeroed, 1)

        @block.tensor
        def _(pe):
            pe.wait_ge(ld_ctx, 16)
            for k in range(KD):
                for b in range(NB):
                    at = (k * NB + b) * S2
                    last = nc.tensor.transpose(bank[J_CTX][:, at:at + S2], cx[:, b, k * P:(k + 1) * P], mem["ident"][0:S2, 0:S2])
            last.then_inc(filled, 1)
            pe.wait_ge(ld_wkv, 16)
            emptied(pe, J_CTX)
            for job in range(J_KV, J_WQ):
                if job >= BANKS:
                    emptied(pe, job - BANKS)
                for s in range(2):
                    rb = 2 * (job - J_KV) + s
                    for k in range(KD):
                        last = nc.tensor.matmul(bank[job % BANKS][:, s * 256:s * 256 + NB * S2], wkv[:, k, rb * P:(rb + 1) * P],
                                                cxT[:, k, :], start=(k == 0), stop=(k == KD - 1))
                last.then_inc(filled, 1)
            pe.wait_ge(ld_wq, 16)
            for job in range(J_WQ, J_G):
                emptied(pe, job - BANKS)
                for s in range(2):
                    rb = 2 * (job - J_WQ) + s
                    for k in range(KD):
                        last = nc.tensor.transpose(bank[job % BANKS][:, s * D + k * P:s * D + (k + 1) * P],
                                                   wq[:, k, rb * P:(rb + 1) * P], mem["ident"][:])
                last.then_inc(filled, 1)
            job = J_G
            emptied(pe, J_G - 1)
            emptied(pe, J_G - 2)
            for b in range(NB):
                for k in range(KD):
                    for h0, h1 in HEAD_GROUPS:
                        emptied(pe, job - BANKS)
                        for h in range(h0, h1):
                            last = nc.tensor.matmul(bank[job % BANKS][:, (h - h0) * S2:(h - h0 + 1) * S2], wqT[:, h // 2, k * P:(k + 1) * P],
                                                    kvT[:, h, b * S2:(b + 1) * S2], start=True, stop=True)
                        last.then_inc(filled, 1)
                        job += 1
            pe.wait_ge(ld_wo, 16)
            for b in range(NB):
                for hp in range(H // 2):
                    emptied(pe, job - BANKS)
                    for s in range(2):
                        last = nc.tensor.matmul(bank[job % BANKS][0:S2, s * D:(s + 1) * D], kvT[:, H + 2 * hp + s, b * S2:(b + 1) * S2],
                                                wo[:, hp, :], start=True, stop=True)
                    last.then_inc(filled, 1)
                    job += 1

        def copies(job):
            src = bank[job % BANKS]
            if job < J_KV:
                return [(cxT[:].rearrange("p k n -> p (k n)"), src[:, 0:KD * NB * S2], 1.0)]
            if job < J_WQ:
                both = src[:].rearrange("p (s n) -> p s n", s=2)[:, :, 0:NB * S2]
                rb = 2 * (job - J_KV)
                to = kvT[:].rearrange("p (r e) n -> p r e n", e=2)
                return [(to[e * DH:(e + 1) * DH, rb:rb + 2, e, :], both[e * DH:(e + 1) * DH], 1.0) for e in range(2)]
            if job < J_G:
                rb = 2 * (job - J_WQ)
                return [(wqT[:, rb:rb + 2, :].rearrange("p r n -> p (r n)"), src[:], 1.0)]
            if job < J_VO:
                q, g = divmod(job - J_G, len(HEAD_GROUPS))
                h0, h1 = HEAD_GROUPS[g]
                b, k = divmod(q, KD)
                return [(mem["G"][:, b, k, h0 * S2:h1 * S2], src[:, 0:(h1 - h0) * S2], DH ** -0.5)]
            b, hp = divmod(job - J_VO, H // 2)
            return [(vo[:, b, 2 * hp:2 * hp + 2, :].rearrange("p s n -> p (s n)"), src[0:S2, :], 1.0)]

        @block.scalar
        def _(act):
            act.wait_ge(kv_zeroed, 1)
            for job in range(0, J_END, 2):
                act.wait_ge(filled, job + 1)
                for out, src, factor in copies(job):
                    last = nc.scalar.activation(out, src, ACT.Copy, scale=factor)
                last.then_inc(act_emptied, 1)

        @block.vector
        def _(dve):
            dve.wait_ge(kv_zeroed, 1)
            for job in range(1, J_END, 2):
                dve.wait_ge(filled, job + 1)
                for out, src, factor in copies(job):
                    last = nc.vector.tensor_scalar(out, src, factor, None, ALU.mult)
                last.then_inc(dve_emptied, 1)
                if job == 1:
                    dve.wait_ge(ld_mask, 16)
                    nc.vector.tensor_scalar(mem["upper"][:], mask[:], 10.0, -5.0, ALU.mult, ALU.add).then_inc(limits_done, 1)


def reach(eng, semaphore, value):
    if value > 0:
        eng.wait_ge(semaphore, value)


def stage_mixer_in(nc, io, mem):
    A_JOBS, B_JOBS = 2 * MB, 3 + MB
    SLOTS = 3
    J_B = NB * A_JOBS
    LOW, CJ, BJ, DT0 = 0, 1, 2, 3
    DVE_OUTS = 2
    HALO = TAPS - 1
    N_CH = BB // 2
    with ExitStack() as ctx:
        sb = lambda n, s, d=F32: ctx.enter_context(nc.sbuf_tensor(n, s, d))
        sem = lambda n: ctx.enter_context(nc.semaphore(n))
        w_in = sb("w_in", [P, KD, 2 * DI])
        w_x = sb("w_x", [P, MB, R + 2 * NS])
        w_dt = sb("w_dt", [R, DI])
        vectors = sb("vectors", [P, 2 * KD + MB * TAPS + 2 * MB])
        lnw, lnb = vectors[:, 0:KD], vectors[:, KD:2 * KD]
        at = 2 * KD + MB * TAPS
        cw = vectors[:, 2 * KD:at].rearrange("p (m t) -> p m t", t=TAPS)
        cb, bdt = (vectors[:, at + i * MB:at + (i + 1) * MB] for i in range(2))
        alog = sb("alog", [P, MB, NS])
        st, mv, sd, rs = sb("st", [P, BB, 6]), sb("mv", [P, BB, 2]), sb("sd", [P, BB]), sb("rs", [P, BB])
        xn = sb("xn", [P, BB, D])
        xnT = sb("xnT", [P, KD, L])
        xi = sb("xi", [P, MB, HALO + L])
        sz = [sb(f"sz{i}", [P, L]) for i in range(2)]
        low = sb("low", [R, L])
        C_sb = sb("C_sb", [NS, L])
        e_ = [sb(f"e{i}", [P, L]) for i in range(2)]
        pos = [sb(f"pos{i}", [P, L]) for i in range(2)]
        q = sb("q", [P, L])
        du = [xn[:, i * BB // 2:(i + 1) * BB // 2, :].rearrange("p n d -> p (n d)") for i in range(2)]
        u, delta, duT = mem["u"], mem["delta"], mem["duT"]
        tp = [ctx.enter_context(nc.psum_tensor(f"tp{i}", [P, N_CH, P], F32)) for i in range(2)]
        mm = [ctx.enter_context(nc.psum_tensor(f"mm{i}", [P, L], F32)) for i in range(SLOTS)]

        ld_x = [sem(f"ld_x{b}") for b in range(NB)]
        ld_ident, ld_w, ld_w2 = sem("ld_ident"), sem("ld_w"), sem("ld_w2")
        zeroed, eps_set = sem("zeroed"), sem("eps_set")
        stats_done, mean_done, sd_done, rs_done, xn_done = (sem(n) for n in ("stats_done", "mean_done", "sd_done", "rs_done", "xn_done"))
        tp_full, tp_emptied = sem("tp_full"), sem("tp_emptied")
        mm_full, mm_act, mm_dve = sem("mm_full"), sem("mm_act"), sem("mm_dve")
        conv_step, u_done = sem("conv_step"), sem("u_done")
        sz_out = [sem(f"sz_out{i}") for i in range(2)]
        C_out = sem("C_out")
        pos_done, e_done, rates_exp, rates_done = sem("pos_done"), sem("e_done"), sem("rates_exp"), sem("rates_done")
        horner, log_done, delta_done, du_done = sem("horner"), sem("log_done"), sem("delta_done"), sem("du_done")
        N_W, N_W2 = 2, 3
        NH = len(LOG1P)
        TA, TB_ = 2 * KD, 2 * MB

        def emptied(eng, job):
            if job < 0:
                return
            if job < J_B:
                eng.wait_ge(mm_act, job + 1)
                return
            b, j = divmod(job - J_B, B_JOBS)
            if j in (CJ, BJ):
                eng.wait_ge(mm_dve, b * DVE_OUTS + j)
            else:
                eng.wait_ge(mm_act, J_B + b * (B_JOBS - DVE_OUTS) + (1 if j == LOW else j - 1))

        block = ctx.enter_context(nc.Block())

        @block.sync
        def _(sp):
            sp.dma_start(mem["x"][:, 0:BB, :], io["x"][0].rearrange("(n p) d -> p n d", p=P)).then_inc(ld_x[0], 16)
            sp.dma_start(mem["ident"][:], io["c_ident"]).then_inc(ld_ident, 16)
            sp.dma_start(vectors[:], io["vectors"]).then_inc(ld_w, 16)
            sp.dma_start(w_in[:], io["L0_attn_W_in"].rearrange("(k p) n -> p k n", p=P)).then_inc(ld_w, 16)
            sp.dma_start(mem["x"][:, BB:TB, :], io["x"][1].rearrange("(n p) d -> p n d", p=P)).then_inc(ld_x[1], 16)
            sp.dma_start(w_x[:], io["L0_attn_W_xproj"].rearrange("(m p) n -> p m n", p=P)).then_inc(ld_w2, 16)
            sp.dma_start(w_dt[:], io["L0_attn_W_dt"]).then_inc(ld_w2, 16)
            sp.dma_start(alog[:], io["L0_attn_A_log"].rearrange("(m p) n -> p m n", p=P)).then_inc(ld_w2, 16)
            for b in range(NB):
                for m in range(MB):
                    emptied(sp, b * A_JOBS + MB + m)
                    sp.dma_start(mem["sz_dram"][m * P:(m + 1) * P, b * L:(b + 1) * L], sz[m % 2][:]).then_inc(sz_out[m % 2], 16)
            for b in range(NB):
                emptied(sp, J_B + b * B_JOBS + CJ)
                sp.dma_start(mem["C_dram"][b], C_sb[:]).then_inc(C_out, 16)
            for i in range(2):
                sp.wait_ge(sz_out[i], 16 * NB * MB // 2)
            sp.wait_ge(C_out, 16 * NB)

        @block.tensor
        def _(pe):
            pe.wait_ge(ld_ident, 16)
            for b in range(NB):
                for t in range(TA):
                    half, k = divmod(t, KD)
                    pe.wait_ge(xn_done, b * BB + (half + 1) * N_CH)
                    reach(pe, tp_emptied, b * TA + t - 1)
                    for n in range(N_CH):
                        last = nc.tensor.transpose(tp[t % 2][:, n, :], xn[:, half * N_CH + n, k * P:(k + 1) * P], mem["ident"][:])
                    last.then_inc(tp_full, 1)
                pe.wait_ge(ld_w, 16 * N_W)
                pe.wait_ge(tp_emptied, (b + 1) * TA)
                for j in range(A_JOBS):
                    job = b * A_JOBS + j
                    emptied(pe, job - SLOTS)
                    for half in range(2):
                        cols = slice(half * HALF, (half + 1) * HALF)
                        for k in range(KD):
                            last = nc.tensor.matmul(mm[job % SLOTS][:, cols], w_in[:, k, j * P:(j + 1) * P], xnT[:, k, cols], start=(k == 0), stop=(k == KD - 1))
                    last.then_inc(mm_full, 1)
            pe.wait_ge(ld_w2, 16 * N_W2)

            def transpose_du(b, m):
                pe.wait_ge(du_done, b * MB + m + 1)
                for half in range(2):
                    t = NB * TA + b * TB_ + 2 * m + half
                    pe.wait_ge(tp_emptied, t - 1)
                    for n in range(N_CH):
                        last = nc.tensor.transpose(tp[t % 2][:, n, :], du[m % 2][:, (half * N_CH + n) * P:(half * N_CH + n + 1) * P], mem["ident"][:])
                    last.then_inc(tp_full, 1)

            for b in range(NB):
                pe.wait_ge(u_done, (b + 1) * MB)
                for j in range(B_JOBS):
                    job = J_B + b * B_JOBS + j
                    o = mm[job % SLOTS]
                    emptied(pe, job - SLOTS)
                    if j == BJ:
                        for c in range(BB):
                            for m in range(MB):
                                last = nc.tensor.matmul(o[:, c * NS:(c + 1) * NS], u[:, b, m, c * P:(c + 1) * P], w_x[:, m, R:R + NS], start=(m == 0), stop=(m == MB - 1))
                        last.then_inc(mm_full, 1)
                        continue
                    if j == DT0:
                        emptied(pe, J_B + b * B_JOBS + LOW)
                    for half in range(2):
                        cols = slice(half * HALF, (half + 1) * HALF)
                        if j < DT0:
                            w0, w1 = (0, R) if j == LOW else (R + NS, R + 2 * NS)
                            for m in range(MB):
                                last = nc.tensor.matmul(o[0:w1 - w0, cols], w_x[:, m, w0:w1], u[:, b, m, cols], start=(m == 0), stop=(m == MB - 1))
                        else:
                            m = j - DT0
                            last = nc.tensor.matmul(o[:, cols], w_dt[:, m * P:(m + 1) * P], low[:, cols], start=True, stop=True)
                    last.then_inc(mm_full, 1)
                    if j - DT0 >= 2:
                        transpose_du(b, j - DT0 - 2)
                for m in (MB - 2, MB - 1):
                    transpose_du(b, m)

        @block.scalar
        def _(act):
            act.wait_ge(eps_set, 1)
            for b in range(NB):
                act.wait_ge(mean_done, (b + 1) * BB)
                nc.scalar.activation(sd[:], mv[:, :, 1], ACT.Sqrt, bias=mem["eps"][:, 0:1]).then_inc(sd_done, 1)
                act.wait_ge(ld_w, 16 * N_W)
                for t in range(TA):
                    half, k = divmod(t, KD)
                    act.wait_ge(tp_full, b * TA + t + 1)
                    nc.scalar.activation(xnT[:, k, half * HALF:(half + 1) * HALF], tp[t % 2][:].rearrange("p n c -> p (n c)"), ACT.Identity,
                                         scale=lnw[:, k:k + 1], bias=lnb[:, k:k + 1]).then_inc(tp_emptied, 1)
                for m in range(MB):
                    job = b * A_JOBS + m
                    act.wait_ge(mm_full, job + 1)
                    if b:
                        act.wait_ge(conv_step, ((b - 1) * MB + m + 1) * TAPS)
                    else:
                        act.wait_ge(zeroed, 1)
                    nc.scalar.activation(xi[:, m, HALO:HALO + L], mm[job % SLOTS][:], ACT.Copy).then_inc(mm_act, 1)
                for m in range(MB):
                    job = b * A_JOBS + MB + m
                    act.wait_ge(mm_full, job + 1)
                    reach(act, sz_out[m % 2], 16 * (b * MB // 2 + m // 2))
                    nc.scalar.activation(sz[m % 2][:], mm[job % SLOTS][:], ACT.Silu).then_inc(mm_act, 1)
                for m in range(MB):
                    act.wait_ge(conv_step, (b * MB + m + 1) * TAPS)
                    nc.scalar.activation(u[:, b, m, :], u[:, b, m, :], ACT.Silu).then_inc(u_done, 1)
            act.wait_ge(ld_w2, 16 * N_W2)
            nc.scalar.activation(alog[:], alog[:], ACT.Exp).then_inc(rates_exp, 1)

            def copy_du(b, m):
                for half in range(2):
                    t = NB * TA + b * TB_ + 2 * m + half
                    act.wait_ge(tp_full, t + 1)
                    nc.scalar.activation(duT[:, b, half * N_CH:(half + 1) * N_CH, m * P:(m + 1) * P], tp[t % 2][:], ACT.Copy).then_inc(tp_emptied, 1)

            for b in range(NB):
                job = J_B + b * B_JOBS + LOW
                act.wait_ge(mm_full, job + 1)
                nc.scalar.activation(low[:], mm[job % SLOTS][0:R, :], ACT.Copy).then_inc(mm_act, 1)
                for m in range(MB):
                    job = J_B + b * B_JOBS + DT0 + m
                    act.wait_ge(mm_full, job + 1)
                    reach(act, delta_done, b * MB + m - 1)
                    nc.scalar.activation(pos[m % 2][:], mm[job % SLOTS][:], ACT.Relu, bias=bdt[:, m:m + 1]).then_inc(pos_done, 1)
                    nc.scalar.activation(e_[m % 2][:], mm[job % SLOTS][:], ACT.Abs, bias=bdt[:, m:m + 1]).then_inc(mm_act, 1)
                    emptied(act, job)
                    nc.scalar.activation(e_[m % 2][:], e_[m % 2][:], ACT.Exp, scale=-1.0).then_inc(e_done, 1)
                    if m >= 2:
                        copy_du(b, m - 2)
                for m in (MB - 2, MB - 1):
                    copy_du(b, m)

        @block.gpsimd
        def _(pool):
            for b in range(NB):
                for m in range(MB):
                    pool.wait_ge(log_done, b * MB + m + 1)
                    nc.gpsimd.tensor_tensor(delta[:, b, m, :], delta[:, b, m, :], pos[m % 2][:], ALU.add).then_inc(delta_done, 1)
                    pool.wait_ge(delta_done, b * MB + m + 1)
                    pool.wait_ge(tp_full, NB * TA + max(b * TB_ + 2 * (m - 1), 0))
                    nc.gpsimd.tensor_tensor(du[m % 2], delta[:, b, m, :], u[:, b, m, :], ALU.mult).then_inc(du_done, 1)

        @block.vector
        def _(dve):
            nc.vector.memset(xi[:, :, 0:HALO], 0.0).then_inc(zeroed, 1)
            nc.vector.memset(mem["eps"][:], EPS).then_inc(eps_set, 1)
            for b in range(NB):
                dve.wait_ge(ld_x[b], 16)
                for n in range(BB):
                    nc.vector.bn_stats(st[:, n, :], mem["x"][:, b * BB + n, :]).then_inc(stats_done, 1)
                for n in range(BB):
                    dve.wait_ge(stats_done, b * BB + n + 1)
                    nc.vector.bn_aggr(mv[:, n, :], st[:, n, :]).then_inc(mean_done, 1)
                dve.wait_ge(sd_done, b + 1)
                nc.vector.reciprocal(rs[:], sd[:]).then_inc(rs_done, 1)
                dve.wait_ge(rs_done, b + 1)
                reach(dve, tp_full, b * TA)
                for n in range(BB):
                    nc.vector.tensor_scalar(xn[:, n, :], mem["x"][:, b * BB + n, :], mv[:, n, 0:1], rs[:, n:n + 1],
                                            ALU.subtract, ALU.mult).then_inc(xn_done, 1)
                dve.wait_ge(ld_w, 16 * N_W)
                for m in range(MB):
                    emptied(dve, b * A_JOBS + m)
                    first = (b * MB + m) * TAPS
                    nc.vector.tensor_scalar(u[:, b, m, :], xi[:, m, 0:L], cw[:, m, 0:1], cb[:, m:m + 1], ALU.mult, ALU.add).then_inc(conv_step, 1)
                    for tap in range(1, TAPS):
                        dve.wait_ge(conv_step, first + tap)
                        nc.vector.scalar_tensor_tensor(out=u[:, b, m, :], in0=xi[:, m, tap:tap + L], scalar=cw[:, m, tap:tap + 1], in1=u[:, b, m, :],
                                                       op0=ALU.mult, op1=ALU.add).then_inc(conv_step, 1)
            dve.wait_ge(rates_exp, 1)
            for s in range(QUARTERS):
                for k in range(QM):
                    last = nc.vector.tensor_scalar(mem["rates"][:, k, s * NS:(s + 1) * NS], alog[:, (s % QD) * QM + k, :], -1.0, None, ALU.mult)
            last.then_inc(rates_done, 1)
            for b in range(NB):
                job = J_B + b * B_JOBS + CJ
                dve.wait_ge(mm_full, job + 1)
                reach(dve, C_out, 16 * b)
                nc.vector.tensor_copy(C_sb[:], mm[job % SLOTS][0:NS, :]).then_inc(mm_dve, 1)
                job = J_B + b * B_JOBS + BJ
                dve.wait_ge(mm_full, job + 1)
                for s in range(QD):
                    last = nc.vector.tensor_copy(mem["B"][:, :, (b * QD + s) * NS:(b * QD + s + 1) * NS],
                                                 mm[job % SLOTS][:, 0:BB * NS].rearrange("p (c n) -> p c n", n=NS))
                last.then_inc(mm_dve, 1)
                for m in range(MB):
                    e = e_[m % 2]
                    at = b * MB + m
                    dve.wait_ge(e_done, at + 1)
                    reach(dve, log_done, at)
                    nc.vector.tensor_scalar(q[:], e[:], LOG1P[-1], None, ALU.mult).then_inc(horner, 1)
                    for step, c in enumerate(LOG1P[-2::-1]):
                        dve.wait_ge(horner, at * (NH - 1) + step + 1)
                        out = q[:] if step < NH - 2 else delta[:, b, m, :]
                        nc.vector.scalar_tensor_tensor(out=out, in0=q[:], scalar=c, in1=e[:], op0=ALU.add,
                                                       op1=ALU.mult).then_inc(horner if step < NH - 2 else log_done, 1)


def stage_scan(nc, io, mem):
    BODY = 16
    SUB = 8
    TURNS = NS // BODY
    TILES = BODY * QM
    STEP_AHEAD = 2
    AHEAD = 2
    N_T, N_IN, N_DECAY, N_STATE, N_PROD, N_C = 2, 2, 4, 4, 2, 4
    ACT_CH = 6
    IN_FREE, SCAN_FREE, PROD_FREE, SUM_FREE = 3, 4, 8, 2
    with ExitStack() as ctx:
        sb = lambda n, s, d=F32: ctx.enter_context(nc.sbuf_tensor(n, s, d))
        sem = lambda n: ctx.enter_context(nc.semaphore(n))
        skip = sb("skip", [P, MB])
        zeros = sb("zeros", [1, HALF], BF16)
        B_now = [sb(f"B_now{i}", [P, BB, SUB]) for i in range(2)]
        rates_now = [sb(f"rates_now{i}", [P, QM, SUB]) for i in range(2)]
        inT = [sb(f"inT{i}", [P, BB, QM * P]) for i in range(N_T)]
        decay = [sb(f"decay{i}", [P, L]) for i in range(N_DECAY)]
        state = [sb(f"state{i}", [P, L]) for i in range(N_STATE)]
        prod = [sb(f"prod{i}", [P, L]) for i in range(N_PROD)]
        C_all = [sb(f"C_all{i}", [P, L]) for i in range(N_C)]
        sz = sb("sz_q", [P, QM, L])
        inp = [ctx.enter_context(nc.psum_tensor(f"inp{i}", [P, L], F32)) for i in range(N_IN)]
        y_ps = ctx.enter_context(nc.psum_tensor("y_ps", [P, QM, L], F32))
        ld_skip, sz_in = sem("ld_skip"), sem("sz_in")
        C_in = [sem(f"C_in{i}") for i in range(N_C)]
        zeros_set = sem("zeros_set")
        cols_done = sem("cols_done")
        inT_act, inT_dve = sem("inT_act"), sem("inT_dve")
        in_full = sem("in_full")
        decay_done = sem("decay_done")
        scan_done = sem("scan_done")
        prod_done = sem("prod_done")
        summed = sem("summed")
        y_full = sem("y_full")
        y_skip, y_gated = sem("y_skip"), sem("y_gated")

        class Turn:
            def __init__(self, quarter, turn):
                self.quarter, self.turn = quarter, turn
                self.b, self.half = divmod(quarter, QD)
                self.tiles = quarter * (NS * QM) + turn * TILES
                self.steps = quarter * NS + turn * BODY
                self.subs = quarter * (NS // SUB) + turn * (BODY // SUB)
                self.C_loads = quarter * (NS // N_C * 16) + turn * (BODY // N_C * 16)

        def chunks(b, half):
            return mem["duT"][:, b, :, half * QM * P:(half + 1) * QM * P]

        block = ctx.enter_context(nc.Block())

        @block.sync
        def _(sp):
            sp.dma_start(skip[:], io["skip"]).then_inc(ld_skip, 16)
            for quarter in range(QUARTERS):
                b, half = divmod(quarter, QD)
                with nc.sync.Fori(0, TURNS) as turn:
                    at = Turn(quarter, turn)
                    for n in range(BODY):
                        sp.wait_ge(prod_done, at.tiles + QM * (n - N_C) + QM + PROD_FREE)
                        row = mem["C_dram"][b, bass.ds(turn * BODY + n, 1), :]
                        sp.dma_start(C_all[n % N_C][:], row.broadcast_to([P, L])).then_inc(C_in[n % N_C], 16)
                reach(sp, y_gated, quarter * QM)
                sp.dma_start(sz[:], mem["sz_dram"][half * QM * P:(half + 1) * QM * P, b * L:(b + 1) * L].rearrange("(m p) t -> p m t", p=P)).then_inc(sz_in, 16)

        @block.scalar
        def _(act):
            for quarter in range(QUARTERS):
                with nc.scalar.Fori(0, TURNS) as turn:
                    at = Turn(quarter, turn)
                    for n in range(BODY):
                        s, col = divmod(n, SUB)
                        if col == 0:
                            act.wait_ge(cols_done, at.subs + s + 1)
                        act.wait_ge(in_full, at.tiles + QM * (n - N_T) + QM + IN_FREE)
                        for c in range(ACT_CH):
                            last = nc.scalar.activation(inT[n % N_T][:, c, :], chunks(at.b, at.half)[:, c, :], ACT.Identity,
                                                        scale=B_now[s][:, c, col:col + 1])
                        last.then_inc(inT_act, 1)
                        for k in range(QM):
                            i = QM * n + k
                            act.wait_ge(scan_done, at.tiles + i - N_DECAY + 1 + SCAN_FREE)
                            nc.scalar.activation(decay[i % N_DECAY][:], mem["delta"][:, at.b, at.half * QM + k, :], ACT.Exp,
                                                 scale=rates_now[s][:, k, col:col + 1]).then_inc(decay_done, 1)

        @block.tensor
        def _(pe):
            pe.sem_inc(in_full, IN_FREE)
            pe.sem_inc(summed, SUM_FREE)
            pe.wait_ge(zeros_set, 1)

            def transposes(at, i):
                n, k = divmod(i, QM)
                if k == 0:
                    pe.wait_ge(inT_act, at.steps + n + 1)
                    pe.wait_ge(inT_dve, at.steps + n + 1)
                pe.wait_ge(scan_done, at.tiles + i - N_IN + 1 + SCAN_FREE)
                for c in range(BB):
                    last = nc.tensor.transpose(inp[i % N_IN][:, c * P:(c + 1) * P], inT[n % N_T][:, c, k * P:(k + 1) * P], mem["ident"][:])
                last.then_inc(in_full, 1)

            def add_up(at, i):
                pe.wait_ge(prod_done, at.tiles + i + 1 + PROD_FREE)
                for h in range(2):
                    cols = slice(h * HALF, (h + 1) * HALF)
                    last = nc.tensor.matmul(y_ps[:, i % QM, cols], mem["ident"][:], prod[i % N_PROD][:, cols], start=False, stop=False)
                last.then_inc(summed, 1)

            def bound(k, start):
                for h in range(2):
                    last = nc.tensor.matmul(y_ps[:, k, h * HALF:(h + 1) * HALF], zeros[:, 0:P], zeros[:], start=start, stop=not start)
                return last

            def turn_of(at, first=False, last=False):
                for i in range(TILES):
                    if at.quarter < QUARTERS - 1 or not last or i + AHEAD < TILES:
                        transposes(at, i + AHEAD)
                    if first and i < QM:
                        reach(pe, y_skip, (at.quarter - 1) * QM + i + 1)
                        bound(i, True)
                    add_up(at, i)
                    if last and i >= TILES - QM:
                        bound(i % QM, False).then_inc(y_full, 1)

            for i in range(AHEAD):
                transposes(Turn(0, 0), i)
            for quarter in range(QUARTERS):
                turn_of(Turn(quarter, 0), first=True)
                with nc.tensor.Fori(1, TURNS - 1) as turn:
                    turn_of(Turn(quarter, turn))
                turn_of(Turn(quarter, TURNS - 1), last=True)

        @block.vector
        def _(dve):
            dve.sem_inc(scan_done, SCAN_FREE)
            nc.vector.memset(zeros[:], 0.0).then_inc(zeros_set, 1)

            def columns(at, s):
                reach_first = at.tiles + (s - 1) * SUB * QM
                if not isinstance(reach_first, int) or reach_first > 0:
                    dve.wait_ge(decay_done, reach_first)
                first = at.steps + s * SUB
                nc.vector.tensor_scalar(B_now[s % 2][:], mem["B"][:, :, bass.ds(first, SUB)], 1.0, None, ALU.mult)
                nc.vector.tensor_scalar(rates_now[s % 2][:], mem["rates"][:, :, bass.ds(first, SUB)], 1.0, None, ALU.mult).then_inc(cols_done, 1)

            def form(at, n, last=False):
                b, half = divmod(at.quarter + 1, QD) if last and n >= BODY else (at.b, at.half)
                s, col = divmod(n, SUB)
                if col == 0:
                    dve.wait_ge(cols_done, at.subs + s + 1)
                for c in range(ACT_CH, BB):
                    last = nc.vector.tensor_scalar(inT[n % N_T][:, c, :], chunks(b, half)[:, c, :], B_now[s % 2][:, c, col:col + 1], None, ALU.mult)
                last.then_inc(inT_dve, 1)

            def scan(at, i):
                dve.wait_ge(in_full, at.tiles + i + 1 + IN_FREE)
                dve.wait_ge(decay_done, at.tiles + i + 1)
                dve.wait_ge(prod_done, at.tiles + i - N_STATE + 1 + PROD_FREE)
                nc.vector.tensor_tensor_scan(state[i % N_STATE][:], decay[i % N_DECAY][:], inp[i % N_IN][:], 0.0, ALU.mult, ALU.add).then_inc(scan_done, 1)

            def finish(quarter, part, k):
                b, half = divmod(quarter, QD)
                m = half * QM + k
                rows = mem["u"][:, b, m, :]
                if part == 0:
                    dve.wait_ge(y_full, quarter * QM + k + 1)
                    nc.vector.scalar_tensor_tensor(out=rows, in0=rows, scalar=skip[:, m:m + 1], in1=y_ps[:, k, :], op0=ALU.mult, op1=ALU.add).then_inc(y_skip, 1)
                else:
                    dve.wait_ge(sz_in, 16 * (quarter + 1))
                    dve.wait_ge(y_skip, quarter * QM + k + 1)
                    nc.vector.tensor_tensor(rows, rows, sz[:, k, :], ALU.mult).then_inc(y_gated, 1)

            def steps(at, first=False, last=False):
                end = last and at.quarter == QUARTERS - 1
                for n in range(BODY):
                    if n % SUB == SUB // 2 and not (end and n > SUB):
                        columns(at, n // SUB + 1)
                    scan(at, QM * n)
                    if first and at.quarter and n == 0:
                        finish(at.quarter - 1, 0, 0)
                    if not end or n + STEP_AHEAD < BODY:
                        dve.wait_ge(in_full, at.tiles + QM * n + QM + IN_FREE)
                        form(at, n + STEP_AHEAD, last)
                    scan(at, QM * n + 1)
                    if first and at.quarter and n < 1 + QM:
                        finish(at.quarter - 1, *((0, 1) if n == 0 else (1, n - 1)))

            columns(Turn(0, 0), 0)
            for n in range(STEP_AHEAD):
                form(Turn(0, 0), n)
            dve.wait_ge(ld_skip, 16)
            for quarter in range(QUARTERS):
                steps(Turn(quarter, 0), first=True)
                with nc.vector.Fori(1, TURNS - 1) as turn:
                    steps(Turn(quarter, turn))
                steps(Turn(quarter, TURNS - 1), last=True)
            for part in range(2):
                for k in range(QM):
                    finish(QUARTERS - 1, part, k)

        @block.gpsimd
        def _(pool):
            pool.sem_inc(prod_done, PROD_FREE)
            for quarter in range(QUARTERS):
                with nc.gpsimd.Fori(0, TURNS) as turn:
                    at = Turn(quarter, turn)
                    for i in range(TILES):
                        n, k = divmod(i, QM)
                        if k == 0:
                            pool.wait_ge(C_in[n % N_C], at.C_loads + n // N_C * 16 + 16)
                        pool.wait_ge(scan_done, at.tiles + i + 1 + SCAN_FREE)
                        pool.wait_ge(summed, at.tiles + i - N_PROD + 1 + SUM_FREE)
                        nc.gpsimd.tensor_tensor(prod[i % N_PROD][:], state[i % N_STATE][:], C_all[n % N_C][:], ALU.mult).then_inc(prod_done, 1)


def wait_apart(eng, semaphore, value, passed):
    eng.wait_ge(semaphore, value)
    eng.sem_inc(passed, 1)


def stage_mixer_out(nc, io, mem):
    SLOTS = 8
    with ExitStack() as ctx:
        sb = lambda n, s, d=F32: ctx.enter_context(nc.sbuf_tensor(n, s, d))
        sem = lambda n: ctx.enter_context(nc.semaphore(n))
        w_out = sb("w_out", [P, MB, D])
        st = sb("st1", [P, TB, 6])
        o = [ctx.enter_context(nc.psum_tensor(f"o{i}", [P, 2, D], F32)) for i in range(SLOTS)]
        ld_w, projected, added = sem("ld_wout"), sem("projected"), sem("added")
        stats_done, mean_done = sem("stats1_done"), sem("mean1_done")
        block = ctx.enter_context(nc.Block())

        @block.sync
        def _(sp):
            sp.dma_start(w_out[:], io["L0_attn_W_out"].rearrange("(m p) n -> p m n", p=P)).then_inc(ld_w, 16)

        @block.vector
        def _(dve):
            for pair in range(TB // 2):
                dve.wait_ge(projected, pair + 1)
                rows = mem["x"][:, 2 * pair:2 * pair + 2, :]
                nc.vector.scalar_tensor_tensor(out=rows, in0=rows, scalar=2.0, in1=o[pair % SLOTS][:], op0=ALU.mult, op1=ALU.add).then_inc(added, 1)
                for n in (2 * pair, 2 * pair + 1):
                    dve.wait_ge(added, pair + 1)
                    nc.vector.bn_stats(st[:, n, :], mem["x"][:, n, :]).then_inc(stats_done, 1)
            for n in range(TB):
                dve.wait_ge(stats_done, n + 1)
                nc.vector.bn_aggr(mem["mv1"][:, n, :], st[:, n, :]).then_inc(mean_done, 1)
            dve.wait_ge(mean_done, TB)

        @block.tensor
        def _(pe):
            pe.wait_ge(ld_w, 16)
            for pair in range(TB // 2):
                for s in range(2):
                    b, n = divmod(pair * 2 + s, BB)
                    for m in range(MB):
                        last = nc.tensor.matmul(o[pair % SLOTS][:, s, :], mem["u"][:, b, m, n * P:(n + 1) * P], w_out[:, m, :], start=(m == 0), stop=(m == MB - 1))
                last.then_inc(projected, 1)


def stage_attention(nc, io, mem):
    TURN = 2 * NB
    TURNS = TB // TURN
    AHEAD = 2
    SG = len(HEAD_GROUPS)
    TP = -(-HJ_CHUNKS // 4)
    with ExitStack() as ctx:
        sb = lambda n, s, d=F32: ctx.enter_context(nc.sbuf_tensor(n, s, d))
        sem = lambda n: ctx.enter_context(nc.semaphore(n))
        vo = sb("vo_in", [P, NB, HJ_CHUNKS, D])
        sd, rs = sb("sd1", [P, TB]), sb("rs1", [P, TB])
        x1 = [sb(f"x1_{i}", [P, D]) for i in range(TURN)]
        xT = [sb(f"xT1_{i}", [P, KD, P]) for i in range(2)]
        p = [sb(f"p{i}", [P, H, S2]) for i in range(TURN)]
        den = [sb(f"den{i}", [P, H]) for i in range(TURN)]
        pT = sb("pT", [P, HJ_CHUNKS, P])
        st, mv = sb("st2", [P, TURN, 6]), sb("mv2_turn", [P, TURN, 2])
        xT_ps = ctx.enter_context(nc.psum_tensor("xT_ps", [P, KD, P], F32))
        s_ps = [ctx.enter_context(nc.psum_tensor(f"s_ps{i}", [P, HALF], F32)) for i in range(SG)]
        pT_ps = [ctx.enter_context(nc.psum_tensor(f"pT_ps{i}", [P, 4, P], F32)) for i in range(2)]
        o_ps = [ctx.enter_context(nc.psum_tensor(f"o_ps{i}", [P, D], F32)) for i in range(2)]
        ld_vo, ones_set = sem("ld_vo"), sem("ones_set")
        sd_done, rs_done, x1_done = sem("sd1_done"), sem("rs1_done"), sem("x1_done")
        xT_full, xT_copied, scored = sem("xT_full"), sem("xT_copied"), sem("scored")
        clipped = sem("clipped")
        exp_done, den_done, inv_done, p_done = sem("exp_done"), sem("den_done"), sem("inv_done"), sem("p_done")
        pT_full, pT_copied, out_done = sem("pT_full"), sem("pT_copied"), sem("out_done")
        added = sem("added2")
        O_FREE = len(o_ps)
        stats_done, mean_done, mean_kept, passed = sem("stats2_done"), sem("mean2_done"), sem("mean2_kept"), sem("passed2")
        block = ctx.enter_context(nc.Block())

        def row(turn, s):
            return turn * (TURN // NB) + (s // (TURN // NB) * BB + s % (TURN // NB))

        def batch(s):
            return s % TURN // (TURN // NB)

        def later(turn, s, ahead):
            return turn + (s + ahead) // TURN, (s + ahead) % TURN

        @block.sync
        def _(sp):
            for b in range(NB):
                sp.dma_start(vo[:, b, 0:HJ_CHUNKS - 1, :], mem["vo_dram"][b, 0:(HJ_CHUNKS - 1) * P, :].rearrange("(c p) e -> p c e", p=P)).then_inc(ld_vo, 16)
                sp.dma_start(vo[0:HJ_LAST, b, HJ_CHUNKS - 1, :], mem["vo_dram"][b, (HJ_CHUNKS - 1) * P:HJ, :]).then_inc(ld_vo, 16)
                sp.dma_start(vo[HJ_LAST:HJ_LAST + 1, b, HJ_CHUNKS - 1, :], io["L0_xattn_bo"].unsqueeze(0)).then_inc(ld_vo, 16)

        @block.scalar
        def _(act):
            nc.scalar.activation(sd[:], mem["mv1"][:, :, 1], ACT.Sqrt, bias=mem["eps"][:, 0:1]).then_inc(sd_done, 1)

            def copy_x(turn, s):
                act.wait_ge(xT_full, turn * TURN + s + 1)
                nc.scalar.activation(xT[s % 2][:], xT_ps[:], ACT.Copy).then_inc(xT_copied, 1)

            def exps(turn, s):
                act.wait_ge(clipped, (turn * TURN + s + 2) * SG)
                nc.scalar.activation(p[s][:], p[s][:], ACT.Exp).then_inc(exp_done, 1)

            def copy_p(turn, s):
                for t in range(TP):
                    act.wait_ge(pT_full, (turn * TURN + s) * TP + t + 1)
                    chunks = range(4 * t, min(4 * t + 4, HJ_CHUNKS))
                    whole = sum(1 for c in chunks if c < HJ_CHUNKS - 1)
                    if whole:
                        last = nc.scalar.activation(pT[:, 4 * t:4 * t + whole, :], pT_ps[t % 2][:, 0:whole, :], ACT.Copy)
                    if HJ_CHUNKS - 1 in chunks:
                        last = nc.scalar.activation(pT[0:HJ_LAST, HJ_CHUNKS - 1, :], pT_ps[t % 2][0:HJ_LAST, whole, :], ACT.Copy)
                    last.then_inc(pT_copied, 1)

            for s in range(AHEAD):
                copy_x(0, s)
            for s in range(AHEAD):
                exps(0, s)
            act.wait_ge(ones_set, 1)
            with nc.scalar.Fori(0, TURNS - 1) as turn:
                for s in range(TURN):
                    copy_x(*later(turn, s, AHEAD))
                    copy_p(turn, s)
                    exps(*later(turn, s, AHEAD))
            for s in range(TURN):
                if s + AHEAD < TURN:
                    copy_x(TURNS - 1, s + AHEAD)
                copy_p(TURNS - 1, s)
                if s + AHEAD < TURN:
                    exps(TURNS - 1, s + AHEAD)

        @block.vector
        def _(dve):
            dve.sem_inc(clipped, SG)
            dve.sem_inc(added, O_FREE)
            nc.vector.memset(pT[64:P, HJ_CHUNKS - 1, :], 1.0).then_inc(ones_set, 1)
            dve.wait_ge(sd_done, 1)
            nc.vector.reciprocal(rs[:], sd[:]).then_inc(rs_done, 1)
            dve.wait_ge(rs_done, 1)

            def normed(turn, s):
                n = row(turn, s)
                nc.vector.tensor_scalar(x1[s][:], mem["x"][:, bass.ds(n, 1), :].rearrange("p a d -> p (a d)"),
                                        mem["mv1"][:, bass.ds(n, 1), 0:1].rearrange("p a d -> p (a d)"), rs[:, bass.ds(n, 1)],
                                        ALU.subtract, ALU.mult).then_inc(x1_done, 1)

            def weights(turn, s):
                n = turn * TURN + s
                upper = mem["upper"][:, batch(s) * S2:(batch(s) + 1) * S2]
                for g, (h0, h1) in enumerate(HEAD_GROUPS):
                    dve.wait_ge(scored, n * SG + g + 1)
                    nc.vector.scalar_tensor_tensor(out=p[s][:, h0:h1, :], in0=s_ps[g][:, 0:(h1 - h0) * S2].rearrange("p (h j) -> p h j", j=S2),
                                                   scalar=-5.0, in1=upper.unsqueeze(1).broadcast_to([P, h1 - h0, S2]),
                                                   op0=ALU.max, op1=ALU.min).then_inc(clipped, 1)
                dve.wait_ge(exp_done, n + 1)
                nc.vector.tensor_reduce(den[s][:], p[s][:], AXX, ALU.add).then_inc(den_done, 1)
                dve.wait_ge(den_done, n + 1)
                nc.vector.reciprocal(den[s][:], den[s][:]).then_inc(inv_done, 1)

            def residual(turn, s):
                n, block_n = turn * TURN + s, row(turn, s)
                rows = mem["x"][:, bass.ds(block_n, 1), :].rearrange("p a d -> p (a d)")
                dve.wait_ge(out_done, n + 1)
                nc.vector.tensor_tensor(rows, x1[s][:], o_ps[s % 2][:], ALU.add).then_inc(added, 1)
                wait_apart(dve, added, n + 1 + O_FREE, passed)
                nc.vector.bn_stats(st[:, s, :], rows).then_inc(stats_done, 1)
                wait_apart(dve, stats_done, n + 1, passed)
                nc.vector.bn_aggr(mv[:, s, :], st[:, s, :]).then_inc(mean_done, 1)
                dve.wait_ge(mean_done, n + 1)
                nc.vector.tensor_scalar(mem["mv2"][:, bass.ds(block_n, 1), :].rearrange("p a d -> p (a d)"), mv[:, s, :], 1.0, None, ALU.mult).then_inc(mean_kept, 1)

            for s in range(AHEAD + 1):
                normed(0, s)
            for s in range(AHEAD):
                weights(0, s)
            with nc.vector.Fori(0, TURNS - 1) as turn:
                for s in range(TURN):
                    normed(*later(turn, s, AHEAD + 1))
                    weights(*later(turn, s, AHEAD))
                    residual(turn, s)
            for s in range(TURN):
                if s + AHEAD + 1 < TURN:
                    normed(TURNS - 1, s + AHEAD + 1)
                if s + AHEAD < TURN:
                    weights(TURNS - 1, s + AHEAD)
                residual(TURNS - 1, s)

        @block.gpsimd
        def _(pool):
            with nc.gpsimd.Fori(0, TURNS) as turn:
                for s in range(TURN):
                    pool.wait_ge(inv_done, turn * TURN + s + 1)
                    nc.gpsimd.tensor_tensor(p[s][:], p[s][:], den[s][:].unsqueeze(2).broadcast_to([P, H, S2]), ALU.mult).then_inc(p_done, 1)

        @block.tensor
        def _(pe):
            def transpose_x(turn, s):
                pe.wait_ge(x1_done, turn * TURN + s + 1)
                for k in range(KD):
                    last = nc.tensor.transpose(xT_ps[:, k, :], x1[s][:, k * P:(k + 1) * P], mem["ident"][:])
                last.then_inc(xT_full, 1)

            def scores(turn, s):
                n = turn * TURN + s
                pe.wait_ge(xT_copied, n + 1)
                for g, (h0, h1) in enumerate(HEAD_GROUPS):
                    pe.wait_ge(clipped, n * SG + g + 1)
                    for k in range(KD):
                        last = nc.tensor.matmul(s_ps[g][:, 0:(h1 - h0) * S2], xT[s % 2][:, k, :], mem["G"][:, batch(s), k, h0 * S2:h1 * S2], start=(k == 0), stop=(k == KD - 1))
                    last.then_inc(scored, 1)

            def transpose_p(turn, s, t):
                n = turn * TURN + s
                if t == 0:
                    pe.wait_ge(p_done, n + 1)
                if t >= 2:
                    pe.wait_ge(pT_copied, n * TP + t - 1)
                flat = p[s][:].rearrange("p h j -> p (h j)")
                for c in range(4 * t, min(4 * t + 4, HJ_CHUNKS)):
                    w = P if c < HJ_CHUNKS - 1 else HJ_LAST
                    last = nc.tensor.transpose(pT_ps[t % 2][0:w, c - 4 * t, :], flat[:, c * P:c * P + w], mem["ident"][:])
                last.then_inc(pT_full, 1)

            def outputs(turn, s):
                n = turn * TURN + s
                pe.wait_ge(added, n + 1)
                for c in range(HJ_CHUNKS):
                    w = P if c < HJ_CHUNKS - 1 else HJ_LAST + 1
                    if c % 4 == 0:
                        pe.wait_ge(pT_copied, n * TP + c // 4 + 1)
                    last = nc.tensor.matmul(o_ps[s % 2][:], pT[0:w, c, :], vo[0:w, batch(s), c, :], start=(c == 0), stop=(c == HJ_CHUNKS - 1))
                last.then_inc(out_done, 1)

            def step(turn, s, more):
                if more:
                    transpose_x(*later(turn, s, AHEAD))
                transpose_p(turn, s, 0)
                transpose_p(turn, s, 1)
                if more:
                    scores(*later(turn, s, AHEAD))
                for t in range(2, TP):
                    transpose_p(turn, s, t)
                outputs(turn, s)

            for s in range(AHEAD):
                transpose_x(0, s)
                scores(0, s)
            pe.wait_ge(ld_vo, 16 * 3 * NB)
            with nc.tensor.Fori(0, TURNS - 1) as turn:
                for s in range(TURN):
                    step(turn, s, True)
            for s in range(TURN):
                step(TURNS - 1, s, s + AHEAD < TURN)


def stage_experts(nc, io, mem):
    CB = HALF // P
    CH = T // HALF
    G_OPS = 19
    PARTS = 3
    with ExitStack() as ctx:
        sb = lambda n, s, d=F32: ctx.enter_context(nc.sbuf_tensor(n, s, d))
        sem = lambda n: ctx.enter_context(nc.semaphore(n))
        w_gate = sb("w_gate", [P, KD, FB, F])
        w_up = sb("w_up", [P, KD, FB, F])
        w_down = sb("w_down", [P, FB, D])
        w_r = sb("w_r", [P, KD, E])
        bias = sb("bias", [P, E])
        rank = sb("rank", [P, E])
        expand_wide = sb("expand_wide", [PARTS * E, E, P])
        expand = sb("expand", [PARTS * E, E, P], BF16)
        sd, rs = sb("sd2", [P, TB]), sb("rs2", [P, TB])
        x2 = sb("x2", [P, CB, D])
        xT = sb("xT2", [P, KD, HALF])
        lg, eq, hot1, l2, hot2, rw, rest = (sb(n, [P, CB, E]) for n in ("lg", "eq", "hot1", "l2", "hot2", "rw", "rest"))
        hi, mid = (sb(n, [P, CB, E], BF16) for n in ("rw_hi", "rw_mid"))
        rw3 = sb("rw3", [P, CB, PARTS, E])
        m1, m2, first1, first2, gap, th, p1, p2 = (sb(n, [P, CB]) for n in ("m1", "m2", "first1", "first2", "gap", "th", "w_first", "w_second"))
        rwT = sb("rwT", [PARTS * E, HALF], BF16)
        act_g = [sb(f"act_g{i}", [P, HALF]) for i in range(2)]
        hid = sb("hid", [P, FB, HALF])
        st, mv_pair = sb("st3", [P, 2, 6]), sb("mv3_pair", [P, 2, 2])
        mv, sd3, rs3 = sb("mv3", [P, TB, 2]), sb("sd3", [P, TB]), sb("rs3", [P, TB])
        tp = ctx.enter_context(nc.psum_tensor("tp2", [P, HALF], F32))
        lg_ps = ctx.enter_context(nc.psum_tensor("lg_ps", [P, CB, E], F32))
        g_ps = [ctx.enter_context(nc.psum_tensor(f"g_ps{i}", [P, HALF], F32)) for i in range(2)]
        u_ps = [ctx.enter_context(nc.psum_tensor(f"u_ps{i}", [P, HALF], F32)) for i in range(2)]
        rw_ps = ctx.enter_context(nc.psum_tensor("rw_ps", [P, HALF], F32))
        d_ps = ctx.enter_context(nc.psum_tensor("d_ps", [P, 2, D], F32))
        outs = [d_ps[:], rw_ps[:].rearrange("p (t d) -> p t d", t=2)]
        ld_r, ld_gu, ld_dn, expand_done = sem("ld_r"), sem("ld_gu"), sem("ld_dn"), sem("expand_done")
        sd_done, rs_done, x2_done, x_done = sem("sd2_done"), sem("rs2_done"), sem("x2_done"), sem("x_normed")
        tp_full, xT_copied, rwT_copied = sem("tp2_full"), sem("xT2_copied"), sem("rwT_copied")
        logits_done, routing, routed, th_done = sem("logits_done"), sem("routing"), sem("routed"), sem("th_done")
        up_full, rw_full, silu_done, mixed, hid_done = sem("up_full"), sem("rw_full"), sem("silu_done"), sem("mixed"), sem("hid_done")
        down_full, stats_done, mean_done = sem("down_full"), sem("stats3_done"), sem("mean3_done")
        added = sem("added3")
        mean_kept, passed = sem("mean3_kept"), sem("passed3")
        sd3_done, rs3_done, normed, stored = sem("sd3_done"), sem("rs3_done"), sem("normed"), sem("stored3")
        ENDS = ((0, TB - CB), (TB - CB, TB))
        block = ctx.enter_context(nc.Block())

        @block.sync
        def _(sp):
            sp.dma_start(w_r[:], io["L0_ffn_Wr"].rearrange("(k p) e -> p k e", p=P)).then_inc(ld_r, 16)
            sp.dma_start(bias[:], io["L0_ffn_expert_bias"].unsqueeze(0).broadcast_to([P, E])).then_inc(ld_r, 16)
            sp.dma_start(rank[:], io["c_rank"]).then_inc(ld_r, 16)
            sp.dma_start(expand_wide[:], io["c_expand"]).then_inc(ld_r, 16)
            for w, routed_w, shared in ((w_gate, "L0_ffn_Wg", "L0_ffn_Sg"), (w_up, "L0_ffn_Wu", "L0_ffn_Su")):
                for k in range(KD):
                    sp.dma_start(w[:, k, 0:E, :], io[routed_w][:, k * P:(k + 1) * P, :].rearrange("e p f -> p e f")).then_inc(ld_gu, 16)
                    sp.dma_start(w[:, k, E:FB, :].rearrange("p a f -> p (a f)"), io[shared][k * P:(k + 1) * P, :]).then_inc(ld_gu, 16)
            sp.dma_start(w_down[:, 0:E, :], io["L0_ffn_Wd"].rearrange("e p d -> p e d")).then_inc(ld_dn, 16)
            sp.dma_start(w_down[:, E:FB, :], io["L0_ffn_Sd"].rearrange("(a p) d -> p a d", p=P)).then_inc(ld_dn, 16)
            for c in range(CH):
                sp.wait_ge(normed, (c + 1) * CB)
                sp.dma_start(io["out"][c * HALF:(c + 1) * HALF, :].rearrange("(n p) d -> p n d", p=P), mem["x"][:, c * CB:(c + 1) * CB, :]).then_inc(stored, 16)
            sp.wait_ge(stored, 16 * CH)

        @block.scalar
        def _(act):
            nc.scalar.activation(sd[:], mem["mv2"][:, :, 1], ACT.Sqrt, bias=mem["eps"][:, 0:1]).then_inc(sd_done, 1)
            act.wait_ge(ld_r, 64)
            nc.scalar.activation(expand[:], expand_wide[:], ACT.Copy).then_inc(expand_done, 1)

            def head(c):
                for k in range(KD):
                    act.wait_ge(tp_full, c * (KD + 1) + k + 1)
                    nc.scalar.activation(xT[:, k, :], tp[:], ACT.Copy).then_inc(xT_copied, 1)
                act.wait_ge(routing, c * G_OPS + 9)
                nc.scalar.activation(th[:], gap[:], ACT.Tanh, scale=0.5).then_inc(th_done, 1)

            def hidden(c):
                for f in range(FB):
                    j = c * FB + f
                    act.wait_ge(up_full, j + 1)
                    if f >= 2:
                        act.wait_ge(mixed, j - 1)
                    nc.scalar.activation(act_g[f % 2][:], g_ps[f % 2][:], ACT.Silu).then_inc(silu_done, 1)
                    if f == 0:
                        act.wait_ge(tp_full, (c + 1) * (KD + 1))
                        nc.scalar.activation(rwT[:], tp[0:PARTS * E, :], ACT.Copy).then_inc(rwT_copied, 1)

            head(0)
            with nc.scalar.Fori(0, CH - 1) as c:
                hidden(c)
                head(c + 1)
            hidden(CH - 1)
            for n0, n1 in ENDS:
                act.wait_ge(mean_kept, n1 // 2)
                nc.scalar.activation(sd3[:, n0:n1], mv[:, n0:n1, 1], ACT.Sqrt, bias=mem["eps"][:, 0:1]).then_inc(sd3_done, 1)

        @block.vector
        def _(dve):
            dve.sem_inc(added, 2)
            dve.wait_ge(sd_done, 1)
            nc.vector.reciprocal(rs[:], sd[:]).then_inc(rs_done, 1)
            dve.wait_ge(rs_done, 1)
            dve.wait_ge(ld_r, 64)

            def wide(a):
                return a.unsqueeze(2).broadcast_to([P, CB, E])

            def each(a):
                return a.unsqueeze(1).broadcast_to([P, CB, E])

            def norm(c):
                for out, done in ((x2, x2_done), (None, x_done)):
                    for n in range(CB):
                        rows = mem["x"][:, bass.ds(c * CB + n, 1), :].rearrange("p a d -> p (a d)")
                        nc.vector.tensor_scalar(rows if out is None else out[:, n, :], rows,
                                                mem["mv2"][:, bass.ds(c * CB + n, 1), 0:1].rearrange("p a d -> p (a d)"), rs[:, bass.ds(c * CB + n, 1)],
                                                ALU.subtract, ALU.mult).then_inc(done, 1)

            def route(c):
                def then(n, ins):
                    ins.then_inc(routing, 1)
                    dve.wait_ge(routing, c * G_OPS + n)

                dve.wait_ge(logits_done, c + 1)
                then(1, nc.vector.tensor_tensor(lg[:], lg_ps[:], each(bias[:]), ALU.add))
                then(2, nc.vector.tensor_reduce(m1[:], lg[:], AXX, ALU.max))
                then(3, nc.vector.tensor_tensor(eq[:], lg[:], wide(m1[:]), ALU.is_equal))
                then(4, nc.vector.tensor_tensor(eq[:], eq[:], each(rank[:]), ALU.mult))
                then(5, nc.vector.tensor_reduce(first1[:], eq[:], AXX, ALU.max))
                then(6, nc.vector.tensor_tensor(hot1[:], each(rank[:]), wide(first1[:]), ALU.is_equal))
                then(7, nc.vector.scalar_tensor_tensor(out=l2[:], in0=hot1[:], scalar=-3e38, in1=lg[:], op0=ALU.mult, op1=ALU.add))
                then(8, nc.vector.tensor_reduce(m2[:], l2[:], AXX, ALU.max))
                then(9, nc.vector.tensor_tensor(gap[:], m2[:], m1[:], ALU.subtract))
                then(10, nc.vector.tensor_tensor(eq[:], l2[:], wide(m2[:]), ALU.is_equal))
                then(11, nc.vector.tensor_tensor(eq[:], eq[:], each(rank[:]), ALU.mult))
                then(12, nc.vector.tensor_reduce(first2[:], eq[:], AXX, ALU.max))
                then(13, nc.vector.tensor_tensor(hot2[:], each(rank[:]), wide(first2[:]), ALU.is_equal))
                dve.wait_ge(th_done, c + 1)
                nc.vector.tensor_scalar(p2[:], th[:], 0.5, 0.5, ALU.mult, ALU.add)
                then(14, nc.vector.tensor_scalar(p1[:], th[:], -0.5, 0.5, ALU.mult, ALU.add))
                nc.vector.tensor_tensor(hot1[:], hot1[:], wide(p1[:]), ALU.mult)
                then(15, nc.vector.tensor_tensor(hot2[:], hot2[:], wide(p2[:]), ALU.mult))
                then(16, nc.vector.tensor_tensor(rw[:], hot1[:], hot2[:], ALU.add))
                then(17, nc.vector.tensor_copy(hi[:], rw[:]))
                nc.vector.tensor_copy(rw3[:, :, 0, :], hi[:])
                then(18, nc.vector.tensor_tensor(rest[:], rw[:], hi[:], ALU.subtract))
                then(19, nc.vector.tensor_copy(mid[:], rest[:]))
                nc.vector.tensor_copy(rw3[:, :, 1, :], mid[:])
                nc.vector.tensor_tensor(rw3[:, :, 2, :], rest[:], mid[:], ALU.subtract).then_inc(routed, 1)

            def hidden(c, more):
                for f in range(FB):
                    j = c * FB + f
                    dve.wait_ge(silu_done, j + 1)
                    nc.vector.tensor_tensor(hid[:, f, :], act_g[f % 2][:], u_ps[f % 2][:], ALU.mult).then_inc(mixed, 1)
                    if f < E:
                        dve.wait_ge(mixed, j + 1)
                        dve.wait_ge(rw_full, c * E + f + 1)
                        nc.vector.tensor_tensor(hid[:, f, :], hid[:, f, :], rw_ps[:], ALU.mult).then_inc(hid_done, 1)
                    if f == E and more:
                        norm(c + 1)

            def add(c):
                for pr in range(2):
                    pair = c * 2 + pr
                    rows = mem["x"][:, bass.ds(pair * 2, 2), :]
                    dve.wait_ge(x_done, (c + 1) * CB)
                    dve.wait_ge(down_full, pair + 1)
                    nc.vector.tensor_tensor(rows, rows, outs[pr], ALU.add).then_inc(added, 1)
                    wait_apart(dve, added, pair + 3, passed)
                    for t in range(2):
                        nc.vector.bn_stats(st[:, t, :], mem["x"][:, bass.ds(pair * 2 + t, 1), :].rearrange("p a d -> p (a d)")).then_inc(stats_done, 1)
                    wait_apart(dve, stats_done, (pair + 1) * 2, passed)
                    for t in range(2):
                        nc.vector.bn_aggr(mv_pair[:, t, :], st[:, t, :]).then_inc(mean_done, 1)
                    dve.wait_ge(mean_done, (pair + 1) * 2)
                    nc.vector.tensor_scalar(mv[:, bass.ds(pair * 2, 2), :], mv_pair[:], 1.0, None, ALU.mult).then_inc(mean_kept, 1)

            def end(i):
                n0, n1 = ENDS[i]
                dve.wait_ge(sd3_done, i + 1)
                nc.vector.reciprocal(rs3[:, n0:n1], sd3[:, n0:n1]).then_inc(rs3_done, 1)
                dve.wait_ge(rs3_done, i + 1)
                for n in range(n0, n1):
                    nc.vector.tensor_scalar(mem["x"][:, n, :], mem["x"][:, n, :], mv[:, n, 0:1], rs3[:, n:n + 1], ALU.subtract, ALU.mult).then_inc(normed, 1)

            norm(0)
            route(0)
            with nc.vector.Fori(0, CH - 1) as c:
                hidden(c, True)
                route(c + 1)
                add(c)
            hidden(CH - 1, False)
            end(0)
            add(CH - 1)
            end(1)

        @block.tensor
        def _(pe):
            def transposes(c, k):
                pe.wait_ge(x2_done, (c + 1) * CB)
                if k:
                    pe.wait_ge(xT_copied, c * KD + k)
                for n in range(CB):
                    last = nc.tensor.transpose(tp[:, n * P:(n + 1) * P], x2[:, n, k * P:(k + 1) * P], mem["ident"][:])
                last.then_inc(tp_full, 1)

            def logits(c):
                pe.wait_ge(xT_copied, (c + 1) * KD)
                for n in range(CB):
                    for k in range(KD):
                        last = nc.tensor.matmul(lg_ps[:, n, :], xT[:, k, n * P:(n + 1) * P], w_r[:, k, :], start=(k == 0), stop=(k == KD - 1))
                last.then_inc(logits_done, 1)

            def up(c, f):
                if f >= 2:
                    pe.wait_ge(mixed, c * FB + f - 1)
                for w, o in ((w_gate, g_ps), (w_up, u_ps)):
                    for k in range(KD):
                        last = nc.tensor.matmul(o[f % 2][:], w[:, k, f, :], xT[:, k, :], start=(k == 0), stop=(k == KD - 1))
                last.then_inc(up_full, 1)

            def hidden(c):
                up(c, 0)
                pe.wait_ge(routed, c + 1)
                for n in range(CB):
                    last = nc.tensor.transpose(tp[0:PARTS * E, n * P:(n + 1) * P], rw3[:, n, :, :].rearrange("p a e -> p (a e)"), mem["ident"][:])
                last.then_inc(tp_full, 1)
                up(c, 1)
                pe.wait_ge(rwT_copied, c + 1)
                pe.wait_ge(added, c * 2 + 2)
                for f in range(FB):
                    if f < E:
                        if f >= 1:
                            pe.wait_ge(hid_done, c * E + f)
                        nc.tensor.matmul(rw_ps[:], expand[:, f, :], rwT[:], start=True, stop=True).then_inc(rw_full, 1)
                    if f + 2 < FB:
                        up(c, f + 2)

            def down(c, n):
                pr, t = divmod(n, 2)
                for f in range(FB):
                    last = nc.tensor.matmul(outs[pr][:, t, :], hid[:, f, n * P:(n + 1) * P], w_down[:, f, :], start=(f == 0), stop=(f == FB - 1))
                if t:
                    last.then_inc(down_full, 1)

            def downs(c, more):
                if more:
                    transposes(c + 1, 0)
                pe.wait_ge(mixed, (c + 1) * FB)
                pe.wait_ge(hid_done, (c + 1) * E)
                down(c, 0)
                if more:
                    transposes(c + 1, 1)
                down(c, 1)
                if more:
                    logits(c + 1)
                down(c, 2)
                down(c, 3)

            pe.wait_ge(ld_r, 64)
            for k in range(KD):
                transposes(0, k)
            logits(0)
            pe.wait_ge(expand_done, 1)
            pe.wait_ge(ld_gu, 16 * 4 * KD)
            pe.wait_ge(ld_dn, 32)
            with nc.tensor.Fori(0, CH - 1) as c:
                hidden(c)
                downs(c, True)
            hidden(CH - 1)
            downs(CH - 1, False)


def build(nc, io):
    with ExitStack() as ctx:
        sb = lambda n, s, d=F32: ctx.enter_context(nc.sbuf_tensor(n, s, d))
        mem = {
            "ident": sb("ident", [P, P]),
            "eps": sb("eps", [P, 1]),
            "x": sb("x", [P, TB, D]),
            "mv1": sb("mv1", [P, TB, 2]), "mv2": sb("mv2", [P, TB, 2]),
        }
        for name, shape in (("sz_dram", [DI, T]), ("C_dram", [NB, NS, L]), ("vo_dram", [NB, HJ, D])):
            mem[name] = nc.dram_tensor(name, shape, F32, kind="Internal").ap()
        with ExitStack() as mixer:
            sb = lambda n, s, d=F32: mixer.enter_context(nc.sbuf_tensor(n, s, d))
            mem["u"] = sb("u", [P, NB, MB, L])
            with ExitStack() as recurrence:
                sb = lambda n, s, d=F32: recurrence.enter_context(nc.sbuf_tensor(n, s, d))
                mem["delta"] = sb("delta", [P, NB, MB, L])
                mem["duT"] = sb("duT", [P, NB, BB, DI])
                mem["B"] = sb("B", [P, BB, QUARTERS * NS])
                mem["rates"] = sb("rates", [P, QM, QUARTERS * NS])
                stage_mixer_in(nc, io, mem)
                stage_scan(nc, io, mem)
            stage_mixer_out(nc, io, mem)
        mem["G"] = ctx.enter_context(nc.sbuf_tensor("G", [P, NB, KD, HJ], F32))
        mem["upper"] = ctx.enter_context(nc.sbuf_tensor("upper", [P, NB * S2], F32))
        stage_context(nc, io, mem)
        stage_attention(nc, io, mem)
        stage_experts(nc, io, mem)


_INS = ["x", "ctx_1024", "mask_BxS2_bk1", "L0_attn_W_in", "L0_attn_W_xproj", "L0_attn_W_dt", "L0_attn_A_log", "L0_attn_W_out", "L0_xattn_Wq",
        "L0_xattn_Wkv", "L0_xattn_Wo", "L0_xattn_bo", "L0_ffn_Wr", "L0_ffn_Wg", "L0_ffn_Wu", "L0_ffn_Wd", "L0_ffn_Sg",
        "L0_ffn_Su", "L0_ffn_Sd", "L0_ffn_expert_bias"]


def _constants():
    import numpy as np
    expand = np.zeros((3, E, E, P), np.float32)
    for e in range(E):
        expand[:, e, e, :] = 1
    expand = expand.reshape(3 * E, E, P)
    rank = np.ascontiguousarray(np.broadcast_to(np.arange(E, 0, -1, dtype=np.float32), (P, E)))
    return {"c_ident": np.eye(P, dtype=np.float32), "c_expand": expand, "c_rank": rank}


def kernel(**inputs):
    import numpy as _np
    import concourse.bacc as _bacc
    from concourse import mybir as _mybir
    from concourse.bass_utils import run_bass_kernel_spmd as _run

    nc = _bacc.Bacc("TRN2", target_bir_lowering=False, num_devices=1)
    arrays, io = {}, {}
    consts = _constants()
    vectors = [_np.asarray(inputs[name]).reshape(-1, P).T for name in ("L0_attn_ln_w", "L0_attn_ln_b")]
    vectors.append(_np.asarray(inputs["L0_attn_conv_w"]).reshape(MB, P, TAPS).transpose(1, 0, 2).reshape(P, MB * TAPS))
    vectors += [_np.asarray(inputs[name]).reshape(-1, P).T for name in ("L0_attn_conv_b", "L0_attn_b_dt")]
    consts["vectors"] = _np.concatenate(vectors, axis=1)
    consts["skip"] = _np.asarray(inputs["L0_attn_D"]).reshape(MB, P).T
    for name in _INS + list(consts):
        a = _np.ascontiguousarray(inputs[name] if name in inputs else consts[name])
        arrays[f"in_{name}"] = a
        io[name] = nc.dram_tensor(f"in_{name}", a.shape, _mybir.dt.from_np(a.dtype), kind="ExternalInput").ap()
    io["out"] = nc.dram_tensor("out_0", (T, D), F32, kind="ExternalOutput").ap()
    build(nc, io)
    r = _run(nc, [arrays], core_ids=[0])
    return r.results[0]["out_0"].reshape(NB, L, D)
```

```python
import concourse.bass as bass
from concourse import mybir
from contextlib import ExitStack

F32 = mybir.dt.float32
BF16 = mybir.dt.bfloat16
U8 = mybir.dt.uint8
ALU = mybir.AluOpType
ACT = mybir.ActivationFunctionType
AXX = mybir.AxisListType.X

P = 128
NB, L, D = 2, 1024, 256
T = NB * L
KD = D // P
DI, NS, R = 512, 64, 16
MB = DI // P
TAPS = 4
S2, H, DH = 77, 16, 64
HJ = H * S2
E, F = 8, 128
FB = E + 2
TB = T // P
BB = L // P
HALF = 512
QM = 2
QD = MB // QM
QUARTERS = NB * QD
EPS = 1e-5
LOG1P_ROOT = 2.48581596
LOG1P_QUADS = ((1.86992378, 1.9141985), (0.412151349, 3.58254016), (-0.94338271, 1.43031292))
LOG1P_SCALE = 0.452101746
HEAD_GROUPS = ((0, 6), (6, 11), (11, 16))
HJ_CHUNKS = -(-HJ // P)
HJ_LAST = HJ - (HJ_CHUNKS - 1) * P


def warm(nc, mem, function, done):
    nc.scalar.activation(mem["unused"][:], mem["eps"][:], function).then_inc(done, 1)


def stage_context(nc, io, mem):
    KV = 2 * H // 2
    BANKS = 8
    with ExitStack() as ctx:
        sb = lambda n, s, d=F32: ctx.enter_context(nc.sbuf_tensor(n, s, d))
        sem = lambda n: ctx.enter_context(nc.semaphore(n))
        cx = mem["cx"]
        wq = sb("wq", [P, KD, H * DH])
        wkv = sb("wkv", [P, KD, 2 * H * DH])
        wo = sb("wo", [P, H // 2, D])
        cxT = sb("cxT", [P, KD, NB * S2])
        wqT = sb("wqT", [P, H // 2, D])
        kvT = sb("kvT", [P, 2 * H, NB * S2])
        vo = sb("vo", [S2, NB, H, D])
        mask = sb("mask", [P, NB * S2], U8)
        sd = sb("sd1", [P, TB])
        bank = [ctx.enter_context(nc.psum_tensor(f"cbank{i}", [P, HALF], F32)) for i in range(BANKS)]
        ld_wq, ld_wo = sem("ld_wq"), sem("ld_wo")
        WKV = 4
        ld_wkv = [sem(f"ld_wkv{i}") for i in range(WKV)]
        ld_mask = sem("ld_mask")
        kv_zeroed = sem("kv_zeroed")
        filled = sem("filled")
        act_emptied = sem("act_emptied")
        dve_emptied = sem("dve_emptied")
        limits_done, stored, ld_vo = sem("limits_done"), sem("stored"), sem("ld_vo")
        sd_done, rs_done = sem("sd1_done"), sem("rs1_done")
        J_CTX, J_KV = 0, 1
        J_VO = J_KV + KV // 2
        J_WQ = J_VO + NB * H // 2
        J_G = J_WQ + H // 4
        J_END = J_G + NB * KD * len(HEAD_GROUPS)

        def emptied(eng, job):
            if job % 2:
                eng.wait_ge(dve_emptied, job // 2 + 1)
            else:
                eng.wait_ge(act_emptied, job // 2 + 1)

        block = ctx.enter_context(nc.Block())

        @block.sync
        def _(sp):
            for i in range(WKV):
                cols = slice(i * (2 * H * DH // WKV), (i + 1) * (2 * H * DH // WKV))
                sp.dma_start(wkv[:, :, cols], io["L0_xattn_Wkv"][:, cols].rearrange("(k p) n -> p k n", p=P)).then_inc(ld_wkv[i], 16)
            sp.dma_start(mask[:], io["mask_BxS2_bk1"].rearrange("b j -> (b j)").unsqueeze(0).broadcast_to([P, NB * S2])).then_inc(ld_mask, 16)
            sp.dma_start(wo[:], io["L0_xattn_Wo"].rearrange("(k p) n -> p k n", p=P)).then_inc(ld_wo, 16)
            sp.dma_start(wq[:], io["L0_xattn_Wq"].rearrange("(k p) n -> p k n", p=P)).then_inc(ld_wq, 16)
            for b in range(NB):
                emptied(sp, J_VO + (b + 1) * H // 2 - 1)
                emptied(sp, J_VO + (b + 1) * H // 2 - 2)
                sp.dma_start(mem["vo_dram"][b, :, :].rearrange("(h j) e -> j h e", j=S2), vo[:, b, :, :]).then_inc(stored, 16)
            sp.wait_ge(stored, 16 * NB)
            for b in range(NB):
                vo_b, vo_to = mem["vo_dram"][b], mem["vo"][:, b]
                sp.dma_start(vo_to[:, 0:HJ_CHUNKS - 1, :], vo_b[0:(HJ_CHUNKS - 1) * P, :].rearrange("(c p) e -> p c e", p=P)).then_inc(ld_vo, 16)
                sp.dma_start(vo_to[0:HJ_LAST, HJ_CHUNKS - 1, :], vo_b[(HJ_CHUNKS - 1) * P:HJ, :]).then_inc(ld_vo, 16)
                sp.dma_start(vo_to[HJ_LAST:HJ_LAST + 1, HJ_CHUNKS - 1, :], io["L0_xattn_bo"].unsqueeze(0)).then_inc(ld_vo, 16)
            sp.wait_ge(ld_vo, 16 * 3 * NB)

        @block.gpsimd
        def _(pool):
            nc.gpsimd.memset(kvT[:], 0.0).then_inc(kv_zeroed, 1)

        @block.tensor
        def _(pe):
            for k in range(KD):
                for b in range(NB):
                    at = (k * NB + b) * S2
                    last = nc.tensor.transpose(bank[J_CTX][:, at:at + S2], cx[:, b, k * P:(k + 1) * P], mem["ident"][0:S2, 0:S2])
            last.then_inc(filled, 1)
            emptied(pe, J_CTX)
            for job in range(J_KV, J_VO):
                pe.wait_ge(ld_wkv[(job - J_KV) * WKV // (J_VO - J_KV)], 16)
                if job >= BANKS:
                    emptied(pe, job - BANKS)
                for s in range(2):
                    rb = 2 * (job - J_KV) + s
                    for k in range(KD):
                        last = nc.tensor.matmul(bank[job % BANKS][:, s * 256:s * 256 + NB * S2], wkv[:, k, rb * P:(rb + 1) * P],
                                                cxT[:, k, :], start=(k == 0), stop=(k == KD - 1))
                last.then_inc(filled, 1)
            pe.wait_ge(ld_wo, 16)
            job = J_VO
            for before in (J_VO - 1, J_VO - 2):
                emptied(pe, before)
            for b in range(NB):
                for hp in range(H // 2):
                    emptied(pe, job - BANKS)
                    for s in range(2):
                        last = nc.tensor.matmul(bank[job % BANKS][0:S2, s * D:(s + 1) * D], kvT[:, H + 2 * hp + s, b * S2:(b + 1) * S2],
                                                wo[:, hp, :], start=True, stop=True)
                    last.then_inc(filled, 1)
                    job += 1
            pe.wait_ge(ld_wq, 16)
            for job in range(J_WQ, J_G):
                emptied(pe, job - BANKS)
                for s in range(2):
                    rb = 2 * (job - J_WQ) + s
                    for k in range(KD):
                        last = nc.tensor.transpose(bank[job % BANKS][:, s * D + k * P:s * D + (k + 1) * P],
                                                   wq[:, k, rb * P:(rb + 1) * P], mem["ident"][:])
                last.then_inc(filled, 1)
            job = J_G
            for before in (J_G - 1, J_G - 2):
                emptied(pe, before)
            for b in range(NB):
                for k in range(KD):
                    for h0, h1 in HEAD_GROUPS:
                        emptied(pe, job - BANKS)
                        for h in range(h0, h1):
                            last = nc.tensor.matmul(bank[job % BANKS][:, (h - h0) * S2:(h - h0 + 1) * S2], wqT[:, h // 2, k * P:(k + 1) * P],
                                                    kvT[:, h, b * S2:(b + 1) * S2], start=True, stop=True)
                        last.then_inc(filled, 1)
                        job += 1

        def copies(job):
            src = bank[job % BANKS]
            if job < J_KV:
                return [(cxT[:].rearrange("p k n -> p (k n)"), src[:, 0:KD * NB * S2], 1.0)]
            if job < J_VO:
                both = src[:].rearrange("p (s n) -> p s n", s=2)[:, :, 0:NB * S2]
                rb = 2 * (job - J_KV)
                to = kvT[:].rearrange("p (r e) n -> p r e n", e=2)
                return [(to[e * DH:(e + 1) * DH, rb:rb + 2, e, :], both[e * DH:(e + 1) * DH], 1.0) for e in range(2)]
            if job < J_WQ:
                b, hp = divmod(job - J_VO, H // 2)
                return [(vo[:, b, 2 * hp:2 * hp + 2, :].rearrange("p s n -> p (s n)"), src[0:S2, :], 1.0)]
            if job < J_G:
                rb = 2 * (job - J_WQ)
                return [(wqT[:, rb:rb + 2, :].rearrange("p r n -> p (r n)"), src[:], 1.0)]
            q, g = divmod(job - J_G, len(HEAD_GROUPS))
            h0, h1 = HEAD_GROUPS[g]
            b, k = divmod(q, KD)
            return [(mem["G"][:, b, k, h0 * S2:h1 * S2], src[:, 0:(h1 - h0) * S2], DH ** -0.5)]

        @block.scalar
        def _(act):
            for job in range(0, J_END, 2):
                if job == 2:
                    act.wait_ge(kv_zeroed, 1)
                act.wait_ge(filled, job + 1)
                for out, src, factor in copies(job):
                    last = nc.scalar.activation(out, src, ACT.Copy, scale=factor)
                last.then_inc(act_emptied, 1)
                if job == J_WQ // 2 * 2:
                    nc.scalar.activation(sd[:], mem["mv1"][:, :, 1], ACT.Sqrt, bias=mem["eps"][:, 0:1]).then_inc(sd_done, 1)

        @block.vector
        def _(dve):
            dve.wait_ge(kv_zeroed, 1)
            for job in range(1, J_END, 2):
                dve.wait_ge(filled, job + 1)
                for out, src, factor in copies(job):
                    last = nc.vector.tensor_scalar(out, src, factor, None, ALU.mult)
                last.then_inc(dve_emptied, 1)
                if job == 1:
                    dve.wait_ge(ld_mask, 16)
                    nc.vector.tensor_scalar(mem["upper"][:], mask[:], 10.0, -5.0, ALU.mult, ALU.add).then_inc(limits_done, 1)
            dve.wait_ge(sd_done, 1)
            nc.vector.reciprocal(mem["rs1"][:], sd[:]).then_inc(rs_done, 1)


def reach(eng, semaphore, value):
    if value > 0:
        eng.wait_ge(semaphore, value)


def reach(eng, semaphore, value):
    if value > 0:
        eng.wait_ge(semaphore, value)


def wait_apart(eng, semaphore, value, passed):
    eng.wait_ge(semaphore, value)
    eng.sem_inc(passed, 1)


def stage_mixer_in(nc, io, mem):
    SLOTS = 3
    HALO = TAPS - 1
    N_CH = BB // 2
    TA = 2 * KD
    SQ, N_SQ = len(LOG1P_QUADS), MB
    LOGS = 1 + SQ
    of = lambda kind, b: [(kind, b, m) for m in range(MB)]
    JOBS = of("xi", 0) + of("z", 0) + of("xi", 1) + [("low", 0, 0), ("B", 0, 0), ("dt", 0, 0), ("C", 0, 0), ("dt", 0, 1), ("dt", 0, 2), ("low", 1, 0)]
    JOBS += [("dt", 0, 3), ("dt", 1, 0), ("C", 1, 0), ("dt", 1, 1), ("B", 1, 0)] + of("dt", 1)[2:] + of("z", 1)
    NORMS = ((0, BB // 2), (BB // 2, BB), (BB, TB))
    BLOCKS = [(b, m) for b in range(NB) for m in range(MB)]
    with ExitStack() as ctx:
        sb = lambda n, s, d=F32: ctx.enter_context(nc.sbuf_tensor(n, s, d))
        sem = lambda n: ctx.enter_context(nc.semaphore(n))
        w_in = sb("w_in", [P, KD, 2 * DI])
        w_x = sb("w_x", [P, MB, R + 2 * NS])
        w_dt = sb("w_dt", [R, DI])
        vectors = sb("vectors", [P, 2 * KD + MB * TAPS + 2 * MB])
        lnw, lnb = vectors[:, 0:KD], vectors[:, KD:2 * KD]
        at = 2 * KD + MB * TAPS
        cw = vectors[:, 2 * KD:at].rearrange("p (m t) -> p m t", t=TAPS)
        cb, bdt = (vectors[:, at + i * MB:at + (i + 1) * MB] for i in range(2))
        alog = sb("alog", [P, MB, NS])
        quad_bias = sb("quad_bias", [P, SQ])
        st, mv, sd, rs = sb("st", [P, TB, 6]), sb("mv", [P, TB, 2]), sb("sd", [P, TB]), sb("rs", [P, TB])
        xn = sb("xn", [P, BB, D])
        xnT = sb("xnT", [P, KD, L])
        xi = sb("xi", [P, MB, HALO + L])
        sz = [sb(f"sz{i}", [P, L]) for i in range(2)]
        low = [sb(f"low{b}", [R, L]) for b in range(NB)]
        C_sb = sb("C_sb", [NS, L])
        e_ = [sb(f"e{i}", [P, L]) for i in range(2)]
        pos = [sb(f"pos{i}", [P, L]) for i in range(2)]
        du = [xn[:, i * BB // 2:(i + 1) * BB // 2, :].rearrange("p n d -> p (n d)") for i in range(2)]
        square = [xi[:, i, 0:L] for i in range(N_SQ)]
        u, delta, duT = mem["u"], mem["delta"], mem["duT"]
        tp = [ctx.enter_context(nc.psum_tensor(f"tp{i}", [P, N_CH, P], F32)) for i in range(2)]
        mm = [ctx.enter_context(nc.psum_tensor(f"mm{i}", [P, L], F32)) for i in range(SLOTS)]

        ld_x = [sem(f"ld_x{i}") for i in range(len(NORMS))]
        ld_ident, ld_v, ld_w, ld_w2 = sem("ld_ident"), sem("ld_v"), sem("ld_w"), sem("ld_w2")
        zeroed, set_done, warmed = sem("zeroed"), sem("set_done"), sem("warmed_sqrt")
        stats_done, mean_done, sd_done, rs_done, xn_done = (sem(n) for n in ("stats_done", "mean_done", "sd_done", "rs_done", "xn_done"))
        xT_full, xT_copied = sem("xnT_full"), sem("xnT_copied")
        duT_full, duT_copied = sem("duT_full"), sem("duT_copied")
        mm_full, mm_act, mm_dve = sem("mm_full"), sem("mm_act"), sem("mm_dve")
        conv_step, u_done = sem("conv_step"), sem("u_done")
        sz_out = mem["sz_out"]
        C_out = sem("C_out")
        pos_done, e_done, sq_done = sem("pos_done"), sem("e_done"), sem("sq_done")
        rates_exp, rates_done = sem("rates_exp"), sem("rates_done")
        log_step, delta_done, du_done = sem("log_step"), sem("delta_done"), sem("du_done")
        N_W2 = 3

        def since(i, kinds):
            first = JOBS.index(("dt", *BLOCKS[i - 1])) if i else 0
            return [job for job in JOBS[first:JOBS.index(("dt", *BLOCKS[i]))] if job[0] in kinds]

        def slot(job):
            return mm[JOBS.index(job) % SLOTS]

        def full(eng, job):
            eng.wait_ge(mm_full, JOBS.index(job) + 1)

        def emptied(eng, job):
            dve = job[0] in ("B", "C")
            count = sum(1 for j in JOBS[:JOBS.index(job) + 1] if (j[0] in ("B", "C")) == dve)
            eng.wait_ge(mm_dve if dve else mm_act, count)

        block = ctx.enter_context(nc.Block())

        @block.sync
        def _(sp):
            x_blocks = io["x"].rearrange("b (n p) d -> p (b n) d", p=P)
            for i in range(2):
                sp.dma_start(mem["x"][:, slice(*NORMS[i]), :], x_blocks[:, slice(*NORMS[i]), :]).then_inc(ld_x[i], 16)
            sp.dma_start(mem["ident"][:], io["c_ident"]).then_inc(ld_ident, 16)
            sp.dma_start(vectors[:], io["vectors"]).then_inc(ld_v, 16)
            sp.dma_start(w_in[:], io["L0_attn_W_in"].rearrange("(k p) n -> p k n", p=P)).then_inc(ld_w, 16)
            sp.dma_start(mem["x"][:, slice(*NORMS[2]), :], x_blocks[:, slice(*NORMS[2]), :]).then_inc(ld_x[2], 16)
            sp.dma_start(w_x[:], io["L0_attn_W_xproj"].rearrange("(m p) n -> p m n", p=P)).then_inc(ld_w2, 16)
            sp.dma_start(w_dt[:], io["L0_attn_W_dt"]).then_inc(ld_w2, 16)
            sp.dma_start(alog[:], io["L0_attn_A_log"].rearrange("(m p) n -> p m n", p=P)).then_inc(ld_w2, 16)
            for b in range(NB):
                for m in range(MB):
                    emptied(sp, ("z", b, m))
                    sp.dma_start(mem["sz_dram"][m * P:(m + 1) * P, b * L:(b + 1) * L], sz[m % 2][:]).then_inc(sz_out[m % 2], 16)
                if b == 0:
                    for c in range(NB):
                        emptied(sp, ("C", c, 0))
                        sp.dma_start(mem["C_dram"][c], C_sb[:]).then_inc(C_out, 16)
            sp.wait_ge(C_out, 16 * NB)

        @block.tensor
        def _(pe):
            def transpose_x(b):
                for t in range(TA):
                    half, k = divmod(t, KD)
                    pe.wait_ge(xn_done, b * BB + (half + 1) * N_CH)
                    reach(pe, xT_copied, b * TA + t - 1)
                    for n in range(N_CH):
                        last = nc.tensor.transpose(tp[t % 2][:, n, :], xn[:, half * N_CH + n, k * P:(k + 1) * P], mem["ident"][:])
                    last.then_inc(xT_full, 1)
                pe.wait_ge(xT_copied, (b + 1) * TA)

            def transpose_du(i):
                pe.wait_ge(du_done, i + 1)
                for half in range(2):
                    reach(pe, duT_copied, 2 * i + half - 1)
                    for n in range(N_CH):
                        last = nc.tensor.transpose(tp[half][:, n, :], du[i % 2][:, (half * N_CH + n) * P:(half * N_CH + n + 1) * P], mem["ident"][:])
                    last.then_inc(duT_full, 1)

            def project(job):
                kind, b, m = job
                o = slot(job)
                if kind == "B":
                    for c in range(BB):
                        for k in range(MB):
                            last = nc.tensor.matmul(o[:, c * NS:(c + 1) * NS], u[:, b, k, c * P:(c + 1) * P], w_x[:, k, R:R + NS], start=(k == 0), stop=(k == MB - 1))
                    return last
                for half in range(2):
                    cols = slice(half * HALF, (half + 1) * HALF)
                    if kind in ("xi", "z"):
                        j = m + (MB if kind == "z" else 0)
                        for k in range(KD):
                            last = nc.tensor.matmul(o[:, cols], w_in[:, k, j * P:(j + 1) * P], xnT[:, k, cols], start=(k == 0), stop=(k == KD - 1))
                    elif kind == "dt":
                        last = nc.tensor.matmul(o[:, cols], w_dt[:, m * P:(m + 1) * P], low[b][:, cols], start=True, stop=True)
                    else:
                        w0, w1 = (0, R) if kind == "low" else (R + NS, R + 2 * NS)
                        for k in range(MB):
                            last = nc.tensor.matmul(o[0:w1 - w0, cols], w_x[:, k, w0:w1], u[:, b, k, cols], start=(k == 0), stop=(k == MB - 1))
                return last

            pe.wait_ge(ld_ident, 16)
            for i, job in enumerate(JOBS):
                kind, b, m = job
                if kind == "xi" and m == 0:
                    transpose_x(b)
                    pe.wait_ge(ld_w, 16)
                if kind in ("low", "B", "C"):
                    pe.wait_ge(ld_w2, 16 * N_W2)
                    pe.wait_ge(u_done, (b + 1) * MB)
                if kind == "dt" and m == 0:
                    emptied(pe, ("low", b, 0))
                if i >= SLOTS:
                    emptied(pe, JOBS[i - SLOTS])
                project(job).then_inc(mm_full, 1)
                if kind == "dt" and 2 <= b * MB + m < NB * MB - 1:
                    transpose_du(b * MB + m - 2)
                if kind == "z" and b == NB - 1 and m < 2:
                    transpose_du(NB * MB - 3 + m)
            transpose_du(NB * MB - 1)

        @block.scalar
        def _(act):
            def copy_x(b):
                for t in range(TA):
                    half, k = divmod(t, KD)
                    act.wait_ge(xT_full, b * TA + t + 1)
                    nc.scalar.activation(xnT[:, k, half * HALF:(half + 1) * HALF], tp[t % 2][:].rearrange("p n c -> p (n c)"), ACT.Identity,
                                         scale=lnw[:, k:k + 1], bias=lnb[:, k:k + 1]).then_inc(xT_copied, 1)

            def copy_xi(b):
                for m in range(MB):
                    full(act, ("xi", b, m))
                    reach(act, conv_step, ((b - 1) * MB + m + 1) * TAPS)
                    nc.scalar.activation(xi[:, m, HALO:HALO + L], slot(("xi", b, m))[:], ACT.Copy).then_inc(mm_act, 1)

            def gates(b):
                for m in range(MB):
                    full(act, ("z", b, m))
                    reach(act, sz_out[m % 2], 16 * (b * MB // 2 + m // 2))
                    nc.scalar.activation(sz[m % 2][:], slot(("z", b, m))[:], ACT.Silu).then_inc(mm_act, 1)

            def convolved(b):
                for m in range(MB):
                    act.wait_ge(conv_step, (b * MB + m + 1) * TAPS)
                    nc.scalar.activation(u[:, b, m, :], u[:, b, m, :], ACT.Silu).then_inc(u_done, 1)

            act.wait_ge(set_done, 1)
            warm(nc, mem, ACT.Sqrt, warmed)
            for n0, n1 in NORMS:
                act.wait_ge(mean_done, n1)
                nc.scalar.activation(sd[:, n0:n1], mv[:, n0:n1, 1], ACT.Sqrt, bias=mem["eps"][:, 0:1]).then_inc(sd_done, 1)
                if n1 == BB:
                    act.wait_ge(ld_v, 16)
                    copy_x(0)
            act.wait_ge(zeroed, 1)
            copy_xi(0)
            gates(0)
            copy_x(1)
            convolved(0)
            copy_xi(1)
            full(act, ("low", 0, 0))
            nc.scalar.activation(low[0][:], slot(("low", 0, 0))[0:R, :], ACT.Copy).then_inc(mm_act, 1)
            convolved(1)
            act.wait_ge(ld_w2, 16 * N_W2)
            nc.scalar.activation(alog[:], alog[:], ACT.Exp).then_inc(rates_exp, 1)
            for i, (b, m) in enumerate(BLOCKS):
                job = ("dt", b, m)
                for other in since(i, ["low"]) if i else []:
                    full(act, other)
                    nc.scalar.activation(low[other[1]][:], slot(other)[0:R, :], ACT.Copy).then_inc(mm_act, 1)
                full(act, job)
                reach(act, delta_done, i - 1)
                nc.scalar.activation(pos[i % 2][:], slot(job)[:], ACT.Relu, bias=bdt[:, m:m + 1]).then_inc(pos_done, 1)
                nc.scalar.activation(e_[i % 2][:], slot(job)[:], ACT.Abs, bias=bdt[:, m:m + 1]).then_inc(mm_act, 1)
                emptied(act, job)
                nc.scalar.activation(e_[i % 2][:], e_[i % 2][:], ACT.Exp, scale=-1.0).then_inc(e_done, 1)
                act.wait_ge(e_done, i + 1)
                for k in range(SQ):
                    before, part = divmod(i * SQ + k - N_SQ, SQ)
                    reach(act, log_step, before * LOGS + part + 2)
                    nc.scalar.activation(square[(i * SQ + k) % N_SQ], e_[i % 2][:], ACT.Square, scale=LOG1P_SCALE, bias=quad_bias[:, k:k + 1]).then_inc(sq_done, 1)
            gates(1)

        @block.gpsimd
        def _(pool):
            for i, (b, m) in enumerate(BLOCKS):
                pool.wait_ge(log_step, (i + 1) * LOGS)
                nc.gpsimd.tensor_tensor(delta[:, b, m, :], pos[i % 2][:], delta[:, b, m, :], ALU.subtract).then_inc(delta_done, 1)
                pool.wait_ge(delta_done, i + 1)
                pool.wait_ge(xT_full, NB * TA)
                reach(pool, duT_full, 2 * (i - 1))
                nc.gpsimd.tensor_tensor(du[i % 2], delta[:, b, m, :], u[:, b, m, :], ALU.mult).then_inc(du_done, 1)

        @block.vector
        def _(dve):
            nc.vector.memset(mem["eps"][:], EPS)
            for k, (centre, _) in enumerate(LOG1P_QUADS):
                last = nc.vector.memset(quad_bias[:, k:k + 1], -LOG1P_SCALE * centre)
            last.then_inc(set_done, 1)
            nc.vector.memset(xi[:, :, 0:HALO], 0.0).then_inc(zeroed, 1)
            for i, (n0, n1) in enumerate(NORMS):
                dve.wait_ge(ld_x[i], 16)
                for n in range(n0, n1):
                    nc.vector.bn_stats(st[:, n, :], mem["x"][:, n, :]).then_inc(stats_done, 1)
                for n in range(n0, n1):
                    dve.wait_ge(stats_done, n + 1)
                    nc.vector.bn_aggr(mv[:, n, :], st[:, n, :]).then_inc(mean_done, 1)
                dve.wait_ge(sd_done, i + 1)
                nc.vector.reciprocal(rs[:, n0:n1], sd[:, n0:n1]).then_inc(rs_done, 1)
                dve.wait_ge(rs_done, i + 1)
                if n0 == BB:
                    dve.wait_ge(xT_full, TA)
                for n in range(n0, n1):
                    nc.vector.tensor_scalar(xn[:, n % BB, :], mem["x"][:, n, :], mv[:, n, 0:1], rs[:, n:n + 1],
                                            ALU.subtract, ALU.mult).then_inc(xn_done, 1)
            dve.wait_ge(ld_v, 16)
            for i, (b, m) in enumerate(BLOCKS):
                emptied(dve, ("xi", b, m))
                nc.vector.tensor_scalar(u[:, b, m, :], xi[:, m, 0:L], cw[:, m, 0:1], cb[:, m:m + 1], ALU.mult, ALU.add).then_inc(conv_step, 1)
                for tap in range(1, TAPS):
                    dve.wait_ge(conv_step, i * TAPS + tap)
                    nc.vector.scalar_tensor_tensor(out=u[:, b, m, :], in0=xi[:, m, tap:tap + L], scalar=cw[:, m, tap:tap + 1], in1=u[:, b, m, :],
                                                   op0=ALU.mult, op1=ALU.add).then_inc(conv_step, 1)

            def take_B(b):
                full(dve, ("B", b, 0))
                for s in range(QD):
                    last = nc.vector.tensor_copy(mem["B"][:, :, (b * QD + s) * NS:(b * QD + s + 1) * NS],
                                                 slot(("B", b, 0))[:, 0:BB * NS].rearrange("p (c n) -> p c n", n=NS))
                last.then_inc(mm_dve, 1)

            def take_C(b):
                full(dve, ("C", b, 0))
                reach(dve, C_out, 16 * b)
                nc.vector.tensor_copy(C_sb[:], slot(("C", b, 0))[0:NS, :]).then_inc(mm_dve, 1)

            def copy_du(i):
                b, m = BLOCKS[i]
                for half in range(2):
                    dve.wait_ge(duT_full, 2 * i + half + 1)
                    nc.vector.tensor_copy(duT[:, b, half * N_CH:(half + 1) * N_CH, m * P:(m + 1) * P], tp[half][:]).then_inc(duT_copied, 1)

            for i, (b, m) in enumerate(BLOCKS):
                for kind, batch, _ in since(i, ["B", "C"]):
                    (take_B if kind == "B" else take_C)(batch)
                e, q = e_[i % 2], delta[:, b, m, :]
                dve.wait_ge(e_done, i + 1)
                nc.vector.scalar_tensor_tensor(out=q, in0=e[:], scalar=LOG1P_ROOT, in1=e[:], op0=ALU.subtract, op1=ALU.mult).then_inc(log_step, 1)
                for k, (_, height) in enumerate(LOG1P_QUADS):
                    dve.wait_ge(sq_done, i * SQ + k + 1)
                    dve.wait_ge(log_step, i * LOGS + k + 1)
                    nc.vector.scalar_tensor_tensor(out=q, in0=square[(i * SQ + k) % N_SQ], scalar=LOG1P_SCALE ** 2 * height, in1=q,
                                                   op0=ALU.add, op1=ALU.mult).then_inc(log_step, 1)
                if i == 3:
                    dve.wait_ge(rates_exp, 1)
                    for s in range(QUARTERS):
                        for k in range(QM):
                            last = nc.vector.tensor_scalar(mem["rates"][:, k, s * NS:(s + 1) * NS], alog[:, (s % QD) * QM + k, :], -1.0, None, ALU.mult)
                    last.then_inc(rates_done, 1)
                if i >= 2:
                    copy_du(i - 2)
            for i in (NB * MB - 2, NB * MB - 1):
                copy_du(i)


def stage_scan(nc, io, mem):
    BODY = 16
    SUB = 8
    TURNS = NS // BODY
    TILES = BODY * QM
    STEP_AHEAD = 2
    AHEAD = 3
    N_T, N_IN, N_DECAY, N_STATE, N_PROD, N_C = 2, 2, 4, 4, 4, 4
    OCT, ADDED, WITH = 8, 5, 7
    SUMS = OCT - 1
    ACT_CH = (6, 7, 7, 7)
    IN_FREE, SCAN_FREE, PROD_FREE, SUM_FREE, PAIR_FREE = 3, 4, 8, SUMS, 1
    with ExitStack() as ctx:
        sb = lambda n, s, d=F32: ctx.enter_context(nc.sbuf_tensor(n, s, d))
        sem = lambda n: ctx.enter_context(nc.semaphore(n))
        skip = sb("skip", [P, MB])
        zeros = sb("zeros", [1, P], BF16)
        w_out = sb("w_out", [P, MB, D])
        st = sb("st1", [P, 2, 6])
        B_now = [sb(f"B_now{i}", [P, BB, SUB]) for i in range(2)]
        rates_now = [sb(f"rates_now{i}", [P, QM, SUB]) for i in range(2)]
        inT = [sb(f"inT{i}", [P, BB, QM * P]) for i in range(N_T)]
        decay = [sb(f"decay{i}", [P, L]) for i in range(N_DECAY)]
        state = [mem["x"][:, i * L // D:(i + 1) * L // D, :].rearrange("p n d -> p (n d)") for i in range(N_STATE)]
        prod = [sb(f"prod{i}", [P, L]) for i in range(N_PROD)]
        C_all = [sb(f"C_all{i}", [P, L]) for i in range(N_C)]
        sz = sb("sz_q", [P, QM, L])
        inp = [ctx.enter_context(nc.psum_tensor(f"inp{i}", [P, L], F32)) for i in range(N_IN)]
        y_ps = ctx.enter_context(nc.psum_tensor("y_ps", [P, QM, L], F32))
        outs = [bank[:, h * HALF:(h + 1) * HALF].rearrange("p (s d) -> p s d", s=2)
                for bank in [inp[0], inp[1]] + [y_ps[:, k, :] for k in range(QM)] for h in range(2)]
        x_again = [decay[i][:].rearrange("p (n d) -> p n d", d=D) for i in range(N_DECAY)]
        ld_skip, sz_in, ld_w, ld_x = sem("ld_skip"), sem("sz_in"), sem("ld_wout"), sem("ld_x_again")
        ld_cx = sem("ld_cx")
        C_in = [sem(f"C_in{i}") for i in range(N_C)]
        zeros_set, warmed = sem("zeros_set"), sem("warmed_exp")
        cols_done = sem("cols_done")
        inT_act, inT_dve = sem("inT_act"), sem("inT_dve")
        in_full = sem("in_full")
        decay_done = sem("decay_done")
        scan_done = sem("scan_done")
        prod_done = sem("prod_done")
        paired = sem("paired")
        summed = sem("summed")
        y_full = sem("y_full")
        projected, added = sem("projected"), sem("added")
        stats_done, mean_done = sem("stats1_done"), sem("mean1_done")
        y_skip, y_gated = sem("y_skip"), sem("y_gated")

        class Turn:
            def __init__(self, quarter, turn):
                self.quarter, self.turn = quarter, turn
                self.b, self.half = divmod(quarter, QD)
                self.tiles = quarter * (NS * QM) + turn * TILES
                self.steps = quarter * NS + turn * BODY
                self.subs = quarter * (NS // SUB) + turn * (BODY // SUB)
                self.octs = quarter * (NS * QM // OCT) + turn * (TILES // OCT)
                self.C_loads = quarter * (NS // N_C * 16) + turn * (BODY // N_C * 16)

        def chunks(b, half):
            return mem["duT"][:, b, :, half * QM * P:(half + 1) * QM * P]

        block = ctx.enter_context(nc.Block())

        @block.sync
        def _(sp):
            sp.dma_start(skip[:], io["skip"]).then_inc(ld_skip, 16)
            sp.dma_start(mem["cx"][:], io["ctx_1024"].rearrange("b j d -> j b d")).then_inc(ld_cx, 16)
            sp.dma_start(w_out[:], io["L0_attn_W_out"].rearrange("(m p) n -> p m n", p=P)).then_inc(ld_w, 16)
            for quarter in range(QUARTERS):
                b, half = divmod(quarter, QD)
                with nc.sync.Fori(0, TURNS) as turn:
                    at = Turn(quarter, turn)
                    for n in range(BODY):
                        sp.wait_ge(prod_done, at.tiles + QM * (n - N_C) + QM + PROD_FREE)
                        row = mem["C_dram"][b, bass.ds(turn * BODY + n, 1), :]
                        sp.dma_start(C_all[n % N_C][:], row.broadcast_to([P, L])).then_inc(C_in[n % N_C], 16)
                for out in mem["sz_out"]:
                    sp.wait_ge(out, 16 * NB * MB // 2)
                reach(sp, y_gated, quarter * QM)
                sp.dma_start(sz[:], mem["sz_dram"][half * QM * P:(half + 1) * QM * P, b * L:(b + 1) * L].rearrange("(m p) t -> p m t", p=P)).then_inc(sz_in, 16)
            sp.wait_ge(scan_done, QUARTERS * NS * QM + SCAN_FREE)
            x_blocks = io["x"].rearrange("b (n p) d -> p (b n) d", p=P)
            for i in range(N_DECAY):
                sp.dma_start(x_again[i], x_blocks[:, i * L // D:(i + 1) * L // D, :]).then_inc(ld_x, 16)
            sp.wait_ge(ld_cx, 16)

        @block.scalar
        def _(act):
            warm(nc, mem, ACT.Exp, warmed)
            for quarter in range(QUARTERS):
                with nc.scalar.Fori(0, TURNS) as turn:
                    at = Turn(quarter, turn)
                    for n in range(BODY):
                        s, col = divmod(n, SUB)
                        if col == 0:
                            act.wait_ge(cols_done, at.subs + s + 1)
                        act.wait_ge(in_full, at.tiles + QM * (n - N_T) + QM + IN_FREE)
                        for c in range(ACT_CH[n % len(ACT_CH)]):
                            last = nc.scalar.activation(inT[n % N_T][:, c, :], chunks(at.b, at.half)[:, c, :], ACT.Identity,
                                                        scale=B_now[s][:, c, col:col + 1])
                        last.then_inc(inT_act, 1)
                        for k in range(QM):
                            i = QM * n + k
                            act.wait_ge(scan_done, at.tiles + i - N_DECAY + 1 + SCAN_FREE)
                            nc.scalar.activation(decay[i % N_DECAY][:], mem["delta"][:, at.b, at.half * QM + k, :], ACT.Exp,
                                                 scale=rates_now[s][:, k, col:col + 1]).then_inc(decay_done, 1)

        @block.tensor
        def _(pe):
            pe.sem_inc(in_full, IN_FREE)
            pe.sem_inc(summed, SUM_FREE)
            pe.wait_ge(zeros_set, 1)

            def transposes(at, i):
                n, k = divmod(i, QM)
                if k == 0:
                    pe.wait_ge(inT_act, at.steps + n + 1)
                    pe.wait_ge(inT_dve, at.steps + n + 1)
                pe.wait_ge(scan_done, at.tiles + i - N_IN + 1 + SCAN_FREE)
                for c in range(BB):
                    last = nc.tensor.transpose(inp[i % N_IN][:, c * P:(c + 1) * P], inT[n % N_T][:, c, k * P:(k + 1) * P], mem["ident"][:])
                last.then_inc(in_full, 1)

            def add_up(at, i):
                if i % OCT == WITH:
                    pe.wait_ge(paired, at.octs + i // OCT + 1 + PAIR_FREE)
                else:
                    pe.wait_ge(prod_done, at.tiles + i + 1 + PROD_FREE)
                for h in range(2):
                    cols = slice(h * HALF, (h + 1) * HALF)
                    last = nc.tensor.matmul(y_ps[:, i % QM, cols], mem["ident"][:], prod[i % N_PROD][:, cols], start=False, stop=False)
                last.then_inc(summed, 1)

            def bound(k, start):
                for h in range(2):
                    last = nc.tensor.matmul(y_ps[:, k, h * HALF:(h + 1) * HALF], zeros[:], zeros[:, 0:1].broadcast_to([1, HALF]), start=start, stop=not start)
                return last

            def turn_of(at, first=False, last=False):
                for i in range(TILES):
                    if at.quarter < QUARTERS - 1 or not last or i + AHEAD < TILES:
                        transposes(at, i + AHEAD)
                    if first and i < QM:
                        reach(pe, y_skip, (at.quarter - 1) * QM + i + 1)
                        bound(i, True)
                    if i % OCT != ADDED:
                        add_up(at, i)
                    if last and i >= TILES - QM:
                        bound(i % QM, False).then_inc(y_full, 1)

            for i in range(AHEAD):
                transposes(Turn(0, 0), i)
            for quarter in range(QUARTERS):
                turn_of(Turn(quarter, 0), first=True)
                with nc.tensor.Fori(1, TURNS - 1) as turn:
                    turn_of(Turn(quarter, turn))
                turn_of(Turn(quarter, TURNS - 1), last=True)
            pe.wait_ge(ld_w, 16)
            pe.wait_ge(scan_done, QUARTERS * NS * QM + SCAN_FREE)
            for pair in range(TB // 2):
                for s in range(2):
                    b, n = divmod(pair * 2 + s, BB)
                    if n == 0:
                        pe.wait_ge(y_gated, (b + 1) * QD * QM)
                    for m in range(MB):
                        last = nc.tensor.matmul(outs[pair][:, s, :], mem["u"][:, b, m, n * P:(n + 1) * P], w_out[:, m, :], start=(m == 0), stop=(m == MB - 1))
                last.then_inc(projected, 1)

        @block.vector
        def _(dve):
            dve.sem_inc(scan_done, SCAN_FREE)
            dve.sem_inc(paired, PAIR_FREE)
            nc.vector.memset(zeros[:], 0.0).then_inc(zeros_set, 1)

            def columns(at, s):
                reach_first = at.tiles + (s - 1) * SUB * QM
                if not isinstance(reach_first, int) or reach_first > 0:
                    dve.wait_ge(decay_done, reach_first)
                first = at.steps + s * SUB
                nc.vector.tensor_scalar(B_now[s % 2][:], mem["B"][:, :, bass.ds(first, SUB)], 1.0, None, ALU.mult)
                nc.vector.tensor_scalar(rates_now[s % 2][:], mem["rates"][:, :, bass.ds(first, SUB)], 1.0, None, ALU.mult).then_inc(cols_done, 1)

            def form(at, n, last=False):
                b, half = divmod(at.quarter + 1, QD) if last and n >= BODY else (at.b, at.half)
                s, col = divmod(n, SUB)
                if col == 0:
                    dve.wait_ge(cols_done, at.subs + s + 1)
                for c in range(ACT_CH[n % len(ACT_CH)], BB):
                    last = nc.vector.tensor_scalar(inT[n % N_T][:, c, :], chunks(b, half)[:, c, :], B_now[s % 2][:, c, col:col + 1], None, ALU.mult)
                last.then_inc(inT_dve, 1)

            def scan(at, i):
                dve.wait_ge(in_full, at.tiles + i + 1 + IN_FREE)
                dve.wait_ge(decay_done, at.tiles + i + 1)
                dve.wait_ge(prod_done, at.tiles + i - N_STATE + 1 + PROD_FREE)
                nc.vector.tensor_tensor_scan(state[i % N_STATE][:], decay[i % N_DECAY][:], inp[i % N_IN][:], 0.0, ALU.mult, ALU.add).then_inc(scan_done, 1)

            def add_pair(tiles):
                dve.wait_ge(prod_done, tiles + PROD_FREE)
                to = prod[WITH % N_PROD]
                nc.vector.tensor_tensor(to[:], to[:], prod[ADDED % N_PROD][:], ALU.add).then_inc(paired, 1)

            def finish(quarter, part, k):
                b, half = divmod(quarter, QD)
                m = half * QM + k
                rows = mem["u"][:, b, m, :]
                if part == 0:
                    dve.wait_ge(y_full, quarter * QM + k + 1)
                    nc.vector.scalar_tensor_tensor(out=rows, in0=rows, scalar=skip[:, m:m + 1], in1=y_ps[:, k, :], op0=ALU.mult, op1=ALU.add).then_inc(y_skip, 1)
                else:
                    dve.wait_ge(sz_in, 16 * (quarter + 1))
                    dve.wait_ge(y_skip, quarter * QM + k + 1)
                    nc.vector.tensor_tensor(rows, rows, sz[:, k, :], ALU.mult).then_inc(y_gated, 1)

            def steps(at, first=False, last=False):
                end = last and at.quarter == QUARTERS - 1
                for n in range(BODY):
                    if n % SUB == SUB // 2 and not (end and n > SUB):
                        columns(at, n // SUB + 1)
                    scan(at, QM * n)
                    if QM * n % OCT == 0 and not (first and at.quarter == 0 and n == 0):
                        add_pair(at.tiles + QM * n)
                    if first and at.quarter and n == 0:
                        finish(at.quarter - 1, 0, 0)
                    if not end or n + STEP_AHEAD < BODY:
                        dve.wait_ge(in_full, at.tiles + QM * n + QM + IN_FREE)
                        form(at, n + STEP_AHEAD, last)
                    scan(at, QM * n + 1)
                    if first and at.quarter and n < 1 + QM:
                        finish(at.quarter - 1, *((0, 1) if n == 0 else (1, n - 1)))

            columns(Turn(0, 0), 0)
            for n in range(STEP_AHEAD):
                form(Turn(0, 0), n)
            dve.wait_ge(ld_skip, 16)
            for quarter in range(QUARTERS):
                steps(Turn(quarter, 0), first=True)
                with nc.vector.Fori(1, TURNS - 1) as turn:
                    steps(Turn(quarter, turn))
                steps(Turn(quarter, TURNS - 1), last=True)
            add_pair(QUARTERS * NS * QM)
            for part in range(2):
                for k in range(QM):
                    finish(QUARTERS - 1, part, k)
            dve.wait_ge(prod_done, QUARTERS * NS * QM + PROD_FREE)
            for pair in range(TB // 2):
                dve.wait_ge(projected, pair + 1)
                rows = mem["x"][:, 2 * pair:2 * pair + 2, :]
                x_rows = x_again[2 * pair // (L // D)][:, 2 * pair % (L // D):2 * pair % (L // D) + 2, :]
                dve.wait_ge(ld_x, 16 * N_DECAY)
                nc.vector.scalar_tensor_tensor(out=rows, in0=x_rows, scalar=2.0, in1=outs[pair], op0=ALU.mult, op1=ALU.add).then_inc(added, 1)
                for n in (2 * pair, 2 * pair + 1):
                    dve.wait_ge(added, pair + 1)
                    nc.vector.bn_stats(st[:, n % 2, :], mem["x"][:, n, :]).then_inc(stats_done, 1)
                for n in (2 * pair, 2 * pair + 1):
                    dve.wait_ge(stats_done, n + 1)
                    nc.vector.bn_aggr(mem["mv1"][:, n, :], st[:, n % 2, :]).then_inc(mean_done, 1)
            dve.wait_ge(mean_done, TB)

        @block.gpsimd
        def _(pool):
            pool.sem_inc(prod_done, PROD_FREE)
            for quarter in range(QUARTERS):
                with nc.gpsimd.Fori(0, TURNS) as turn:
                    at = Turn(quarter, turn)
                    for i in range(TILES):
                        n, k = divmod(i, QM)
                        if k == 0:
                            pool.wait_ge(C_in[n % N_C], at.C_loads + n // N_C * 16 + 16)
                        pool.wait_ge(scan_done, at.tiles + i + 1 + SCAN_FREE)
                        octet, before = divmod(i - N_PROD, OCT)
                        if before == ADDED:
                            pool.wait_ge(paired, at.octs + octet + 1 + PAIR_FREE)
                        else:
                            pool.wait_ge(summed, at.octs * SUMS + octet * SUMS + before + (before < ADDED) + SUM_FREE)
                        nc.gpsimd.tensor_tensor(prod[i % N_PROD][:], state[i % N_STATE][:], C_all[n % N_C][:], ALU.mult).then_inc(prod_done, 1)


def stage_attention(nc, io, mem):
    TURN = 2 * NB
    TURNS = TB // TURN
    AHEAD = 2
    SG = len(HEAD_GROUPS)
    TP = -(-HJ_CHUNKS // 4)
    with ExitStack() as ctx:
        sb = lambda n, s, d=F32: ctx.enter_context(nc.sbuf_tensor(n, s, d))
        sem = lambda n: ctx.enter_context(nc.semaphore(n))
        vo, rs = mem["vo"], mem["rs1"]
        x1 = [sb(f"x1_{i}", [P, D]) for i in range(TURN)]
        xT = [sb(f"xT1_{i}", [P, KD, P]) for i in range(2)]
        p = [sb(f"p{i}", [P, H, S2]) for i in range(TURN)]
        den = [sb(f"den{i}", [P, H]) for i in range(TURN)]
        pT = sb("pT", [P, HJ_CHUNKS, P])
        st, mv = sb("st2", [P, TURN, 6]), sb("mv2_turn", [P, TURN, 2])
        xT_ps = ctx.enter_context(nc.psum_tensor("xT_ps", [P, KD, P], F32))
        s_ps = [ctx.enter_context(nc.psum_tensor(f"s_ps{i}", [P, HALF], F32)) for i in range(SG)]
        pT_ps = [ctx.enter_context(nc.psum_tensor(f"pT_ps{i}", [P, 4, P], F32)) for i in range(2)]
        o_ps = [ctx.enter_context(nc.psum_tensor(f"o_ps{i}", [P, D], F32)) for i in range(2)]
        ld_experts, ones_set, warmed = sem("ld_experts"), sem("ones_set"), sem("warmed_sqrt2")
        x1_done = sem("x1_done")
        xT_full, xT_copied, scored = sem("xT_full"), sem("xT_copied"), sem("scored")
        clipped = sem("clipped")
        exp_done, den_done, inv_done, p_done = sem("exp_done"), sem("den_done"), sem("inv_done"), sem("p_done")
        pT_full, pT_copied, out_done = sem("pT_full"), sem("pT_copied"), sem("out_done")
        added = sem("added2")
        O_FREE = len(o_ps)
        stats_done, mean_done, mean_kept, passed = sem("stats2_done"), sem("mean2_done"), sem("mean2_kept"), sem("passed2")
        block = ctx.enter_context(nc.Block())

        def row(turn, s):
            return turn * (TURN // NB) + (s // (TURN // NB) * BB + s % (TURN // NB))

        def batch(s):
            return s % TURN // (TURN // NB)

        def later(turn, s, ahead):
            return turn + (s + ahead) // TURN, (s + ahead) % TURN

        @block.sync
        def _(sp):
            sp.dma_start(mem["w_r"][:], io["L0_ffn_Wr"].rearrange("(k p) e -> p k e", p=P)).then_inc(ld_experts, 16)
            sp.dma_start(mem["bias"][:], io["L0_ffn_expert_bias"].unsqueeze(0).broadcast_to([P, E])).then_inc(ld_experts, 16)
            sp.dma_start(mem["rank"][:], io["c_rank"]).then_inc(ld_experts, 16)
            sp.dma_start(mem["expand_wide"][:], io["c_expand"]).then_inc(ld_experts, 16)
            for w, routed_w, shared in ((mem["w_gate"], "L0_ffn_Wg", "L0_ffn_Sg"), (mem["w_up"], "L0_ffn_Wu", "L0_ffn_Su")):
                for k in range(KD):
                    sp.dma_start(w[:, k, 0:E, :], io[routed_w][:, k * P:(k + 1) * P, :].rearrange("e p f -> p e f")).then_inc(ld_experts, 16)
                    sp.dma_start(w[:, k, E:FB, :].rearrange("p a f -> p (a f)"), io[shared][k * P:(k + 1) * P, :]).then_inc(ld_experts, 16)
            sp.dma_start(mem["w_down"][:, 0:E, :], io["L0_ffn_Wd"].rearrange("e p d -> p e d")).then_inc(ld_experts, 16)
            sp.dma_start(mem["w_down"][:, E:FB, :], io["L0_ffn_Sd"].rearrange("(a p) d -> p a d", p=P)).then_inc(ld_experts, 16)
            sp.wait_ge(ld_experts, 16 * (4 + 4 * KD + 2))

        @block.scalar
        def _(act):
            def copy_x(turn, s):
                act.wait_ge(xT_full, turn * TURN + s + 1)
                nc.scalar.activation(xT[s % 2][:], xT_ps[:], ACT.Copy).then_inc(xT_copied, 1)

            def exps(turn, s):
                act.wait_ge(clipped, (turn * TURN + s + 2) * SG)
                nc.scalar.activation(p[s][:], p[s][:], ACT.Exp).then_inc(exp_done, 1)

            def copy_p(turn, s):
                for t in range(TP):
                    act.wait_ge(pT_full, (turn * TURN + s) * TP + t + 1)
                    chunks = range(4 * t, min(4 * t + 4, HJ_CHUNKS))
                    whole = sum(1 for c in chunks if c < HJ_CHUNKS - 1)
                    if whole:
                        last = nc.scalar.activation(pT[:, 4 * t:4 * t + whole, :], pT_ps[t % 2][:, 0:whole, :], ACT.Copy)
                    if HJ_CHUNKS - 1 in chunks:
                        last = nc.scalar.activation(pT[0:HJ_LAST, HJ_CHUNKS - 1, :], pT_ps[t % 2][0:HJ_LAST, whole, :], ACT.Copy)
                    last.then_inc(pT_copied, 1)

            for s in range(AHEAD):
                copy_x(0, s)
            for s in range(AHEAD):
                exps(0, s)
            act.wait_ge(ones_set, 1)
            with nc.scalar.Fori(0, TURNS - 1) as turn:
                for s in range(TURN):
                    copy_x(*later(turn, s, AHEAD))
                    copy_p(turn, s)
                    exps(*later(turn, s, AHEAD))
            for s in range(TURN):
                if s + AHEAD < TURN:
                    copy_x(TURNS - 1, s + AHEAD)
                copy_p(TURNS - 1, s)
                if s + AHEAD < TURN:
                    exps(TURNS - 1, s + AHEAD)
                if s + AHEAD == TURN:
                    warm(nc, mem, ACT.Sqrt, warmed)

        @block.vector
        def _(dve):
            dve.sem_inc(clipped, SG)
            dve.sem_inc(added, O_FREE)
            nc.vector.memset(pT[64:P, HJ_CHUNKS - 1, :], 1.0).then_inc(ones_set, 1)

            def normed(turn, s):
                n = row(turn, s)
                nc.vector.tensor_scalar(x1[s][:], mem["x"][:, bass.ds(n, 1), :].rearrange("p a d -> p (a d)"),
                                        mem["mv1"][:, bass.ds(n, 1), 0:1].rearrange("p a d -> p (a d)"), rs[:, bass.ds(n, 1)],
                                        ALU.subtract, ALU.mult).then_inc(x1_done, 1)

            def weights(turn, s):
                n = turn * TURN + s
                upper = mem["upper"][:, batch(s) * S2:(batch(s) + 1) * S2]
                for g, (h0, h1) in enumerate(HEAD_GROUPS):
                    dve.wait_ge(scored, n * SG + g + 1)
                    nc.vector.scalar_tensor_tensor(out=p[s][:, h0:h1, :], in0=s_ps[g][:, 0:(h1 - h0) * S2].rearrange("p (h j) -> p h j", j=S2),
                                                   scalar=-5.0, in1=upper.unsqueeze(1).broadcast_to([P, h1 - h0, S2]),
                                                   op0=ALU.max, op1=ALU.min).then_inc(clipped, 1)
                dve.wait_ge(exp_done, n + 1)
                nc.vector.tensor_reduce(den[s][:], p[s][:], AXX, ALU.add).then_inc(den_done, 1)
                dve.wait_ge(den_done, n + 1)
                nc.vector.reciprocal(den[s][:], den[s][:]).then_inc(inv_done, 1)

            def residual(turn, s):
                n, block_n = turn * TURN + s, row(turn, s)
                rows = mem["x"][:, bass.ds(block_n, 1), :].rearrange("p a d -> p (a d)")
                dve.wait_ge(out_done, n + 1)
                nc.vector.tensor_tensor(rows, x1[s][:], o_ps[s % 2][:], ALU.add).then_inc(added, 1)
                wait_apart(dve, added, n + 1 + O_FREE, passed)
                nc.vector.bn_stats(st[:, s, :], rows).then_inc(stats_done, 1)
                wait_apart(dve, stats_done, n + 1, passed)
                nc.vector.bn_aggr(mv[:, s, :], st[:, s, :]).then_inc(mean_done, 1)
                dve.wait_ge(mean_done, n + 1)
                nc.vector.tensor_scalar(mem["mv2"][:, bass.ds(block_n, 1), :].rearrange("p a d -> p (a d)"), mv[:, s, :], 1.0, None, ALU.mult).then_inc(mean_kept, 1)

            for s in range(AHEAD + 1):
                normed(0, s)
            for s in range(AHEAD):
                weights(0, s)
            with nc.vector.Fori(0, TURNS - 1) as turn:
                for s in range(TURN):
                    normed(*later(turn, s, AHEAD + 1))
                    weights(*later(turn, s, AHEAD))
                    residual(turn, s)
            for s in range(TURN):
                if s + AHEAD + 1 < TURN:
                    normed(TURNS - 1, s + AHEAD + 1)
                if s + AHEAD < TURN:
                    weights(TURNS - 1, s + AHEAD)
                residual(TURNS - 1, s)

        @block.gpsimd
        def _(pool):
            with nc.gpsimd.Fori(0, TURNS) as turn:
                for s in range(TURN):
                    pool.wait_ge(inv_done, turn * TURN + s + 1)
                    nc.gpsimd.tensor_tensor(p[s][:], p[s][:], den[s][:].unsqueeze(2).broadcast_to([P, H, S2]), ALU.mult).then_inc(p_done, 1)

        @block.tensor
        def _(pe):
            def transpose_x(turn, s):
                pe.wait_ge(x1_done, turn * TURN + s + 1)
                for k in range(KD):
                    last = nc.tensor.transpose(xT_ps[:, k, :], x1[s][:, k * P:(k + 1) * P], mem["ident"][:])
                last.then_inc(xT_full, 1)

            def scores(turn, s):
                n = turn * TURN + s
                pe.wait_ge(xT_copied, n + 1)
                for g, (h0, h1) in enumerate(HEAD_GROUPS):
                    pe.wait_ge(clipped, n * SG + g + 1)
                    for k in range(KD):
                        last = nc.tensor.matmul(s_ps[g][:, 0:(h1 - h0) * S2], xT[s % 2][:, k, :], mem["G"][:, batch(s), k, h0 * S2:h1 * S2], start=(k == 0), stop=(k == KD - 1))
                    last.then_inc(scored, 1)

            def transpose_p(turn, s, t):
                n = turn * TURN + s
                if t == 0:
                    pe.wait_ge(p_done, n + 1)
                if t >= 2:
                    pe.wait_ge(pT_copied, n * TP + t - 1)
                flat = p[s][:].rearrange("p h j -> p (h j)")
                for c in range(4 * t, min(4 * t + 4, HJ_CHUNKS)):
                    w = P if c < HJ_CHUNKS - 1 else HJ_LAST
                    last = nc.tensor.transpose(pT_ps[t % 2][0:w, c - 4 * t, :], flat[:, c * P:c * P + w], mem["ident"][:])
                last.then_inc(pT_full, 1)

            def outputs(turn, s):
                n = turn * TURN + s
                pe.wait_ge(added, n + 1)
                for c in range(HJ_CHUNKS):
                    w = P if c < HJ_CHUNKS - 1 else HJ_LAST + 1
                    if c % 4 == 0:
                        pe.wait_ge(pT_copied, n * TP + c // 4 + 1)
                    last = nc.tensor.matmul(o_ps[s % 2][:], pT[0:w, c, :], vo[0:w, batch(s), c, :], start=(c == 0), stop=(c == HJ_CHUNKS - 1))
                last.then_inc(out_done, 1)

            def step(turn, s, more):
                if more:
                    transpose_x(*later(turn, s, AHEAD))
                transpose_p(turn, s, 0)
                transpose_p(turn, s, 1)
                if more:
                    scores(*later(turn, s, AHEAD))
                for t in range(2, TP):
                    transpose_p(turn, s, t)
                outputs(turn, s)

            for s in range(AHEAD):
                transpose_x(0, s)
                scores(0, s)
            with nc.tensor.Fori(0, TURNS - 1) as turn:
                for s in range(TURN):
                    step(turn, s, True)
            for s in range(TURN):
                step(TURNS - 1, s, s + AHEAD < TURN)


def stage_experts(nc, io, mem):
    CB = HALF // P
    CH = T // HALF
    G_OPS = 19
    PARTS = 3
    with ExitStack() as ctx:
        sb = lambda n, s, d=F32: ctx.enter_context(nc.sbuf_tensor(n, s, d))
        sem = lambda n: ctx.enter_context(nc.semaphore(n))
        w_gate, w_up, w_down, w_r, bias, rank, expand_wide = (mem[n] for n in ("w_gate", "w_up", "w_down", "w_r", "bias", "rank", "expand_wide"))
        expand = sb("expand", [PARTS * E, E, P], BF16)
        sd, rs = sb("sd2", [P, TB]), sb("rs2", [P, TB])
        x2 = sb("x2", [P, CB, D])
        xT = sb("xT2", [P, KD, HALF])
        lg, eq, hot1, l2, hot2, rw, rest = (sb(n, [P, CB, E]) for n in ("lg", "eq", "hot1", "l2", "hot2", "rw", "rest"))
        hi, mid = (sb(n, [P, CB, E], BF16) for n in ("rw_hi", "rw_mid"))
        rw3 = sb("rw3", [P, CB, PARTS, E])
        m1, m2, first1, first2, gap, th, p1, p2 = (sb(n, [P, CB]) for n in ("m1", "m2", "first1", "first2", "gap", "th", "w_first", "w_second"))
        rwT = sb("rwT", [PARTS * E, HALF], BF16)
        act_g = [sb(f"act_g{i}", [P, HALF]) for i in range(2)]
        hid = sb("hid", [P, FB, HALF])
        st, mv_pair = sb("st3", [P, 2, 6]), sb("mv3_pair", [P, 2, 2])
        mv, sd3, rs3 = sb("mv3", [P, TB, 2]), sb("sd3", [P, TB]), sb("rs3", [P, TB])
        tp = ctx.enter_context(nc.psum_tensor("tp2", [P, HALF], F32))
        lg_ps = ctx.enter_context(nc.psum_tensor("lg_ps", [P, CB, E], F32))
        g_ps = [ctx.enter_context(nc.psum_tensor(f"g_ps{i}", [P, HALF], F32)) for i in range(2)]
        u_ps = [ctx.enter_context(nc.psum_tensor(f"u_ps{i}", [P, HALF], F32)) for i in range(2)]
        rw_ps = ctx.enter_context(nc.psum_tensor("rw_ps", [P, HALF], F32))
        d_ps = ctx.enter_context(nc.psum_tensor("d_ps", [P, 2, D], F32))
        outs = [d_ps[:], rw_ps[:].rearrange("p (t d) -> p t d", t=2)]
        expand_done = sem("expand_done")
        sd_done, rs_done, x2_done, x_done = sem("sd2_done"), sem("rs2_done"), sem("x2_done"), sem("x_normed")
        tp_full, xT_copied, rwT_copied = sem("tp2_full"), sem("xT2_copied"), sem("rwT_copied")
        logits_done, routing, routed, th_done = sem("logits_done"), sem("routing"), sem("routed"), sem("th_done")
        up_full, rw_full, silu_done, mixed, hid_done = sem("up_full"), sem("rw_full"), sem("silu_done"), sem("mixed"), sem("hid_done")
        down_full, stats_done, mean_done = sem("down_full"), sem("stats3_done"), sem("mean3_done")
        added = sem("added3")
        mean_kept, passed = sem("mean3_kept"), sem("passed3")
        sd3_done, rs3_done, normed, stored = sem("sd3_done"), sem("rs3_done"), sem("normed"), sem("stored3")
        ENDS = ((0, TB - CB), (TB - CB, TB))
        block = ctx.enter_context(nc.Block())

        @block.sync
        def _(sp):
            for c in range(CH):
                sp.wait_ge(normed, (c + 1) * CB)
                sp.dma_start(io["out"][c * HALF:(c + 1) * HALF, :].rearrange("(n p) d -> p n d", p=P), mem["x"][:, c * CB:(c + 1) * CB, :]).then_inc(stored, 16)
            sp.wait_ge(stored, 16 * CH)

        @block.scalar
        def _(act):
            nc.scalar.activation(sd[:], mem["mv2"][:, :, 1], ACT.Sqrt, bias=mem["eps"][:, 0:1]).then_inc(sd_done, 1)
            def head(c):
                for k in range(KD):
                    act.wait_ge(tp_full, c * (KD + 1) + k + 1)
                    nc.scalar.activation(xT[:, k, :], tp[:], ACT.Copy).then_inc(xT_copied, 1)
                if isinstance(c, int):
                    nc.scalar.activation(expand[:], expand_wide[:], ACT.Copy).then_inc(expand_done, 1)
                act.wait_ge(routing, c * G_OPS + 9)
                nc.scalar.activation(th[:], gap[:], ACT.Tanh, scale=0.5).then_inc(th_done, 1)

            def hidden(c):
                for f in range(FB):
                    j = c * FB + f
                    act.wait_ge(up_full, j + 1)
                    if f >= 2:
                        act.wait_ge(mixed, j - 1)
                    nc.scalar.activation(act_g[f % 2][:], g_ps[f % 2][:], ACT.Silu).then_inc(silu_done, 1)
                    if f == 1:
                        act.wait_ge(tp_full, (c + 1) * (KD + 1))
                        nc.scalar.activation(rwT[:], tp[0:PARTS * E, :], ACT.Copy).then_inc(rwT_copied, 1)

            head(0)
            with nc.scalar.Fori(0, CH - 1) as c:
                hidden(c)
                head(c + 1)
            hidden(CH - 1)
            for n0, n1 in ENDS:
                act.wait_ge(mean_kept, n1 // 2)
                nc.scalar.activation(sd3[:, n0:n1], mv[:, n0:n1, 1], ACT.Sqrt, bias=mem["eps"][:, 0:1]).then_inc(sd3_done, 1)

        @block.vector
        def _(dve):
            dve.sem_inc(added, 2)
            dve.wait_ge(sd_done, 1)
            nc.vector.reciprocal(rs[:], sd[:]).then_inc(rs_done, 1)
            dve.wait_ge(rs_done, 1)

            def wide(a):
                return a.unsqueeze(2).broadcast_to([P, CB, E])

            def each(a):
                return a.unsqueeze(1).broadcast_to([P, CB, E])

            def norm(c):
                for out, done in ((x2, x2_done), (None, x_done)):
                    for n in range(CB):
                        rows = mem["x"][:, bass.ds(c * CB + n, 1), :].rearrange("p a d -> p (a d)")
                        nc.vector.tensor_scalar(rows if out is None else out[:, n, :], rows,
                                                mem["mv2"][:, bass.ds(c * CB + n, 1), 0:1].rearrange("p a d -> p (a d)"), rs[:, bass.ds(c * CB + n, 1)],
                                                ALU.subtract, ALU.mult).then_inc(done, 1)

            def route(c):
                def then(n, ins):
                    ins.then_inc(routing, 1)
                    dve.wait_ge(routing, c * G_OPS + n)

                dve.wait_ge(logits_done, c + 1)
                then(1, nc.vector.tensor_tensor(lg[:], lg_ps[:], each(bias[:]), ALU.add))
                then(2, nc.vector.tensor_reduce(m1[:], lg[:], AXX, ALU.max))
                then(3, nc.vector.tensor_tensor(eq[:], lg[:], wide(m1[:]), ALU.is_equal))
                then(4, nc.vector.tensor_tensor(eq[:], eq[:], each(rank[:]), ALU.mult))
                then(5, nc.vector.tensor_reduce(first1[:], eq[:], AXX, ALU.max))
                then(6, nc.vector.tensor_tensor(hot1[:], each(rank[:]), wide(first1[:]), ALU.is_equal))
                then(7, nc.vector.scalar_tensor_tensor(out=l2[:], in0=hot1[:], scalar=-3e38, in1=lg[:], op0=ALU.mult, op1=ALU.add))
                then(8, nc.vector.tensor_reduce(m2[:], l2[:], AXX, ALU.max))
                then(9, nc.vector.tensor_tensor(gap[:], m2[:], m1[:], ALU.subtract))
                then(10, nc.vector.tensor_tensor(eq[:], l2[:], wide(m2[:]), ALU.is_equal))
                then(11, nc.vector.tensor_tensor(eq[:], eq[:], each(rank[:]), ALU.mult))
                then(12, nc.vector.tensor_reduce(first2[:], eq[:], AXX, ALU.max))
                then(13, nc.vector.tensor_tensor(hot2[:], each(rank[:]), wide(first2[:]), ALU.is_equal))
                dve.wait_ge(th_done, c + 1)
                nc.vector.tensor_scalar(p2[:], th[:], 0.5, 0.5, ALU.mult, ALU.add)
                then(14, nc.vector.tensor_scalar(p1[:], th[:], -0.5, 0.5, ALU.mult, ALU.add))
                nc.vector.tensor_tensor(hot1[:], hot1[:], wide(p1[:]), ALU.mult)
                then(15, nc.vector.tensor_tensor(hot2[:], hot2[:], wide(p2[:]), ALU.mult))
                then(16, nc.vector.tensor_tensor(rw[:], hot1[:], hot2[:], ALU.add))
                then(17, nc.vector.tensor_copy(hi[:], rw[:]))
                nc.vector.tensor_copy(rw3[:, :, 0, :], hi[:])
                then(18, nc.vector.tensor_tensor(rest[:], rw[:], hi[:], ALU.subtract))
                then(19, nc.vector.tensor_copy(mid[:], rest[:]))
                nc.vector.tensor_copy(rw3[:, :, 1, :], mid[:])
                nc.vector.tensor_tensor(rw3[:, :, 2, :], rest[:], mid[:], ALU.subtract).then_inc(routed, 1)

            def hidden(c, more):
                for f in range(FB):
                    j = c * FB + f
                    dve.wait_ge(silu_done, j + 1)
                    nc.vector.tensor_tensor(hid[:, f, :], act_g[f % 2][:], u_ps[f % 2][:], ALU.mult).then_inc(mixed, 1)
                    if f < E:
                        dve.wait_ge(mixed, j + 1)
                        dve.wait_ge(rw_full, c * E + f + 1)
                        nc.vector.tensor_tensor(hid[:, f, :], hid[:, f, :], rw_ps[:], ALU.mult).then_inc(hid_done, 1)
                    if f == E and more:
                        norm(c + 1)

            def add(c):
                for pr in range(2):
                    pair = c * 2 + pr
                    rows = mem["x"][:, bass.ds(pair * 2, 2), :]
                    dve.wait_ge(x_done, (c + 1) * CB)
                    dve.wait_ge(down_full, pair + 1)
                    nc.vector.tensor_tensor(rows, rows, outs[pr], ALU.add).then_inc(added, 1)
                    wait_apart(dve, added, pair + 3, passed)
                    for t in range(2):
                        nc.vector.bn_stats(st[:, t, :], mem["x"][:, bass.ds(pair * 2 + t, 1), :].rearrange("p a d -> p (a d)")).then_inc(stats_done, 1)
                    wait_apart(dve, stats_done, (pair + 1) * 2, passed)
                    for t in range(2):
                        nc.vector.bn_aggr(mv_pair[:, t, :], st[:, t, :]).then_inc(mean_done, 1)
                    dve.wait_ge(mean_done, (pair + 1) * 2)
                    nc.vector.tensor_scalar(mv[:, bass.ds(pair * 2, 2), :], mv_pair[:], 1.0, None, ALU.mult).then_inc(mean_kept, 1)

            def end(i):
                n0, n1 = ENDS[i]
                dve.wait_ge(sd3_done, i + 1)
                nc.vector.reciprocal(rs3[:, n0:n1], sd3[:, n0:n1]).then_inc(rs3_done, 1)
                dve.wait_ge(rs3_done, i + 1)
                for n in range(n0, n1):
                    nc.vector.tensor_scalar(mem["x"][:, n, :], mem["x"][:, n, :], mv[:, n, 0:1], rs3[:, n:n + 1], ALU.subtract, ALU.mult).then_inc(normed, 1)

            norm(0)
            route(0)
            with nc.vector.Fori(0, CH - 1) as c:
                hidden(c, True)
                route(c + 1)
                add(c)
            hidden(CH - 1, False)
            end(0)
            add(CH - 1)
            end(1)

        @block.tensor
        def _(pe):
            def transposes(c, k):
                pe.wait_ge(x2_done, (c + 1) * CB)
                if k:
                    pe.wait_ge(xT_copied, c * KD + k)
                for n in range(CB):
                    last = nc.tensor.transpose(tp[:, n * P:(n + 1) * P], x2[:, n, k * P:(k + 1) * P], mem["ident"][:])
                last.then_inc(tp_full, 1)

            def logits(c):
                pe.wait_ge(xT_copied, (c + 1) * KD)
                for n in range(CB):
                    for k in range(KD):
                        last = nc.tensor.matmul(lg_ps[:, n, :], xT[:, k, n * P:(n + 1) * P], w_r[:, k, :], start=(k == 0), stop=(k == KD - 1))
                last.then_inc(logits_done, 1)

            def up(c, f):
                if f >= 2:
                    pe.wait_ge(mixed, c * FB + f - 1)
                for w, o in ((w_gate, g_ps), (w_up, u_ps)):
                    for k in range(KD):
                        last = nc.tensor.matmul(o[f % 2][:], w[:, k, f, :], xT[:, k, :], start=(k == 0), stop=(k == KD - 1))
                last.then_inc(up_full, 1)

            def hidden(c):
                up(c, 0)
                up(c, 1)
                pe.wait_ge(routed, c + 1)
                for n in range(CB):
                    last = nc.tensor.transpose(tp[0:PARTS * E, n * P:(n + 1) * P], rw3[:, n, :, :].rearrange("p a e -> p (a e)"), mem["ident"][:])
                last.then_inc(tp_full, 1)
                pe.wait_ge(rwT_copied, c + 1)
                pe.wait_ge(added, c * 2 + 2)
                for f in range(FB):
                    if f < E:
                        if f >= 1:
                            pe.wait_ge(hid_done, c * E + f)
                        nc.tensor.matmul(rw_ps[:], expand[:, f, :], rwT[:], start=True, stop=True).then_inc(rw_full, 1)
                    if f + 2 < FB:
                        up(c, f + 2)

            def down(c, n):
                pr, t = divmod(n, 2)
                for f in range(FB):
                    if n == 0 and f == FB - 1:
                        pe.wait_ge(mixed, (c + 1) * FB)
                    last = nc.tensor.matmul(outs[pr][:, t, :], hid[:, f, n * P:(n + 1) * P], w_down[:, f, :], start=(f == 0), stop=(f == FB - 1))
                if t:
                    last.then_inc(down_full, 1)

            def downs(c, more):
                if more:
                    transposes(c + 1, 0)
                pe.wait_ge(mixed, (c + 1) * FB - 1)
                pe.wait_ge(hid_done, (c + 1) * E)
                down(c, 0)
                if more:
                    transposes(c + 1, 1)
                down(c, 1)
                if more:
                    logits(c + 1)
                down(c, 2)
                down(c, 3)

            for k in range(KD):
                transposes(0, k)
            logits(0)
            pe.wait_ge(expand_done, 1)
            with nc.tensor.Fori(0, CH - 1) as c:
                hidden(c)
                downs(c, True)
            hidden(CH - 1)
            downs(CH - 1, False)


def build(nc, io):
    with ExitStack() as ctx:
        sb = lambda n, s, d=F32: ctx.enter_context(nc.sbuf_tensor(n, s, d))
        mem = {
            "ident": sb("ident", [P, P]),
            "eps": sb("eps", [P, 1]),
            "x": sb("x", [P, TB, D]),
            "unused": sb("unused", [P, 1]),
            "mv1": sb("mv1", [P, TB, 2]), "mv2": sb("mv2", [P, TB, 2]),
        }
        for name, shape in (("sz_dram", [DI, T]), ("C_dram", [NB, NS, L]), ("vo_dram", [NB, HJ, D])):
            mem[name] = nc.dram_tensor(name, shape, F32, kind="Internal").ap()
        mem["cx"] = sb("cx", [S2, NB, D])
        with ExitStack() as mixer:
            mem["sz_out"] = [mixer.enter_context(nc.semaphore(f"sz_out{i}")) for i in range(2)]
            sb = lambda n, s, d=F32: mixer.enter_context(nc.sbuf_tensor(n, s, d))
            mem["u"] = sb("u", [P, NB, MB, L])
            mem["delta"] = sb("delta", [P, NB, MB, L])
            mem["duT"] = sb("duT", [P, NB, BB, DI])
            mem["B"] = sb("B", [P, BB, QUARTERS * NS])
            mem["rates"] = sb("rates", [P, QM, QUARTERS * NS])
            stage_mixer_in(nc, io, mem)
            stage_scan(nc, io, mem)
        sb = lambda n, s, d=F32: ctx.enter_context(nc.sbuf_tensor(n, s, d))
        mem["G"] = sb("G", [P, NB, KD, HJ])
        mem["vo"] = sb("vo_in", [P, NB, HJ_CHUNKS, D])
        mem["upper"] = sb("upper", [P, NB * S2])
        mem["rs1"] = sb("rs1", [P, TB])
        for name, shape in (("w_gate", [P, KD, FB, F]), ("w_up", [P, KD, FB, F]), ("w_down", [P, FB, D]), ("w_r", [P, KD, E]), ("bias", [P, E]),
                            ("rank", [P, E]),
                            ("expand_wide", [3 * E, E, P])):
            mem[name] = sb(name, shape)
        stage_context(nc, io, mem)
        stage_attention(nc, io, mem)
        stage_experts(nc, io, mem)


_INS = ["x", "ctx_1024", "mask_BxS2_bk1", "L0_attn_W_in", "L0_attn_W_xproj", "L0_attn_W_dt", "L0_attn_A_log", "L0_attn_W_out", "L0_xattn_Wq",
        "L0_xattn_Wkv", "L0_xattn_Wo", "L0_xattn_bo", "L0_ffn_Wr", "L0_ffn_Wg", "L0_ffn_Wu", "L0_ffn_Wd", "L0_ffn_Sg",
        "L0_ffn_Su", "L0_ffn_Sd", "L0_ffn_expert_bias"]


def _constants():
    import numpy as np
    expand = np.zeros((3, E, E, P), np.float32)
    for e in range(E):
        expand[:, e, e, :] = 1
    expand = expand.reshape(3 * E, E, P)
    rank = np.ascontiguousarray(np.broadcast_to(np.arange(E, 0, -1, dtype=np.float32), (P, E)))
    return {"c_ident": np.eye(P, dtype=np.float32), "c_expand": expand, "c_rank": rank}


def kernel(**inputs):
    import numpy as _np
    import concourse.bacc as _bacc
    from concourse import mybir as _mybir
    from concourse.bass_utils import run_bass_kernel_spmd as _run

    nc = _bacc.Bacc("TRN2", target_bir_lowering=False, num_devices=1)
    arrays, io = {}, {}
    consts = _constants()
    vectors = [_np.asarray(inputs[name]).reshape(-1, P).T for name in ("L0_attn_ln_w", "L0_attn_ln_b")]
    vectors.append(_np.asarray(inputs["L0_attn_conv_w"]).reshape(MB, P, TAPS).transpose(1, 0, 2).reshape(P, MB * TAPS))
    vectors += [_np.asarray(inputs[name]).reshape(-1, P).T for name in ("L0_attn_conv_b", "L0_attn_b_dt")]
    consts["vectors"] = _np.concatenate(vectors, axis=1)
    consts["skip"] = _np.asarray(inputs["L0_attn_D"]).reshape(MB, P).T
    for name in _INS + list(consts):
        a = _np.ascontiguousarray(inputs[name] if name in inputs else consts[name])
        arrays[f"in_{name}"] = a
        io[name] = nc.dram_tensor(f"in_{name}", a.shape, _mybir.dt.from_np(a.dtype), kind="ExternalInput").ap()
    io["out"] = nc.dram_tensor("out_0", (T, D), F32, kind="ExternalOutput").ap()
    build(nc, io)
    r = _run(nc, [arrays], core_ids=[0])
    return r.results[0]["out_0"].reshape(NB, L, D)
```
